# Optimizing a Trainium2 kernel written in Bass

```python
import numpy as np
import jax
import jax.numpy as jnp

def _softmax(x, axis=-1):
    return jax.nn.softmax(x, axis=axis)

def _gelu(x):
    return jax.nn.gelu(x, approximate=True)

def _silu(x):
    return jax.nn.silu(x)

def _sigmoid(x):
    return jax.nn.sigmoid(x)

def _layernorm(x, axis=-1, eps=1e-05):
    m = jnp.mean(x, axis=axis, keepdims=True)
    v = jnp.var(x, axis=axis, keepdims=True)
    return (x - m) / jnp.sqrt(v + eps)

def _scatter_add(tgt, idx, src, axis=0):
    return tgt.at[idx].add(src)

def _segment_sum(src, seg, n):
    return jax.ops.segment_sum(src, seg, n)
kernel_name = 'mk_prb_d2_jaxref_r8_62ca04'

def setup_inputs(seed: int=0):
    np.random.seed(seed)
    _w = jnp.asarray

    def _L0_attn_setup():
        import jax, jax.numpy as jnp
        import numpy as np
        N_HEADS = 16
        D_HEAD = 128
        D_MODEL = 256
        MAXLEN = 256
        key = jax.random.key(seed)
        ks = jax.random.split(key, 9)
        b, t = (2, 256)
        hd = N_HEADS * D_HEAD
        init = 0.02
        return {'x': jax.random.normal(ks[0], (b, t, D_MODEL), dtype=jnp.float32), 'Wq': jax.random.normal(ks[1], (D_MODEL, hd), dtype=jnp.float32) * init, 'bq': jnp.zeros((hd,), dtype=jnp.float32), 'Wk': jax.random.normal(ks[2], (D_MODEL, hd), dtype=jnp.float32) * init, 'bk': jnp.zeros((hd,), dtype=jnp.float32), 'Wv': jax.random.normal(ks[3], (D_MODEL, hd), dtype=jnp.float32) * init, 'bv': jnp.zeros((hd,), dtype=jnp.float32), 'Wo': jax.random.normal(ks[4], (hd, D_MODEL), dtype=jnp.float32) * init, 'bo': jnp.zeros((D_MODEL,), dtype=jnp.float32)}
    _L0_attn_in = _L0_attn_setup()

    def _L0_ffn_setup():
        import jax, jax.numpy as jnp
        import numpy as np
        D_IN = 256
        D_OUT = 256
        RANK = 16
        N_EXPERTS = 16
        MAX_EXPERTS = 32
        ROUTER_HID = 64
        TOPK = 2
        ALPHA = 1.0

        def _forward(x, W, bias, rw1, rb1, rw2, rb2, A, B, gates):
            lead = x.shape[:-1]
            x_flat = x.reshape(-1, D_IN)
            n = x_flat.shape[0]
            feat = jax.lax.stop_gradient(x_flat)
            h = jax.nn.silu(feat @ rw1.T + rb1)
            logits = (h @ rw2.T + rb2)[:, :N_EXPERTS] + gates[None, :]
            topv, topi = jax.lax.top_k(logits, TOPK)
            sm = jax.nn.softmax(topv, axis=-1)
            rows = jnp.arange(n)[:, None]
            coeff = jnp.zeros_like(logits).at[rows, topi].set(sm)
            base = x_flat @ W.T + bias
            xa = jnp.einsum('ni,eri->ner', x_flat, A)
            wxa = xa * coeff[:, :, None]
            delta = jnp.einsum('ner,eor->no', wxa, B)
            out = base + ALPHA * delta
            return out.reshape(*lead, D_OUT)
        key = jax.random.key(seed)
        ks = jax.random.split(key, 10)
        s = 0.02
        x = jax.random.normal(ks[0], (4, 512, D_IN), dtype=jnp.float32)
        W = jax.random.normal(ks[1], (D_OUT, D_IN), dtype=jnp.float32) * s
        bias = jax.random.normal(ks[2], (D_OUT,), dtype=jnp.float32) * s
        rw1 = jax.random.normal(ks[3], (ROUTER_HID, D_IN), dtype=jnp.float32) * s
        rb1 = jnp.zeros((ROUTER_HID,), dtype=jnp.float32)
        rw2 = jax.random.normal(ks[4], (MAX_EXPERTS, ROUTER_HID), dtype=jnp.float32) * s
        rb2 = jnp.zeros((MAX_EXPERTS,), dtype=jnp.float32)
        A = jax.random.normal(ks[5], (N_EXPERTS, RANK, D_IN), dtype=jnp.float32) * s
        B = jax.random.normal(ks[6], (N_EXPERTS, D_OUT, RANK), dtype=jnp.float32) * s
        gates = jnp.ones((N_EXPERTS,), dtype=jnp.float32)
        return {'x': x, 'W': W, 'bias': bias, 'rw1': rw1, 'rb1': rb1, 'rw2': rw2, 'rb2': rb2, 'A': A, 'B': B, 'gates': gates}
    _L0_ffn_in = _L0_ffn_setup()

    def _L1_attn_setup():
        import jax, jax.numpy as jnp
        import numpy as np
        HIDDEN = 256
        NUM_HEADS = 16
        NUM_KV_HEADS = 4
        HEAD_DIM = HIDDEN // NUM_HEADS
        Q_PER_KV = NUM_HEADS // NUM_KV_HEADS
        GROUP_SIZE = (Q_PER_KV + 2) * HEAD_DIM
        TOTAL_PROJ = NUM_KV_HEADS * GROUP_SIZE
        SEQ, BATCH = (256, 2)
        key = jax.random.key(seed)
        k1, k2, k3 = jax.random.split(key, 3)
        x = jax.random.normal(k1, (SEQ, BATCH, HIDDEN), dtype=jnp.float32)
        weight_qkv = jax.random.normal(k2, (TOTAL_PROJ, HIDDEN), dtype=jnp.float32) * 0.02
        weight_proj = jax.random.normal(k3, (HIDDEN, NUM_HEADS * HEAD_DIM), dtype=jnp.float32) * 0.02
        return {'x': x, 'weight_qkv': weight_qkv, 'weight_proj': weight_proj}
    _L1_attn_in = _L1_attn_setup()

    def _L1_ffn_setup():
        import jax, jax.numpy as jnp
        import numpy as np
        B, S, H = (1, 128, 256)
        E, K = (32, 4)
        F, FS = (176, 704)
        CAP = 32

        def silu(x):
            return x * jax.nn.sigmoid(x)
        key = jax.random.key(seed)
        ks = jax.random.split(key, 9)
        sc = 0.02
        return {'hidden_states': jax.random.normal(ks[0], (B, S, H), jnp.float32), 'Wr': jax.random.normal(ks[1], (H, E), jnp.float32) * sc, 'Wg': jax.random.normal(ks[2], (E, H, F), jnp.float32) * sc, 'Wu': jax.random.normal(ks[3], (E, H, F), jnp.float32) * sc, 'Wd': jax.random.normal(ks[4], (E, F, H), jnp.float32) * sc, 'Wsg': jax.random.normal(ks[5], (H, FS), jnp.float32) * sc, 'Wsu': jax.random.normal(ks[6], (H, FS), jnp.float32) * sc, 'Wsd': jax.random.normal(ks[7], (FS, H), jnp.float32) * sc, 'Wse': jax.random.normal(ks[8], (H, 1), jnp.float32) * sc}
    _L1_ffn_in = _L1_ffn_setup()
    _d = {'L0_attn_x': _L0_attn_in['x'], 'L0_attn_Wq': _L0_attn_in['Wq'], 'L0_attn_bq': _L0_attn_in['bq'], 'L0_attn_Wk': _L0_attn_in['Wk'], 'L0_attn_bk': _L0_attn_in['bk'], 'L0_attn_Wv': _L0_attn_in['Wv'], 'L0_attn_bv': _L0_attn_in['bv'], 'L0_attn_Wo': _L0_attn_in['Wo'], 'L0_attn_bo': _L0_attn_in['bo'], 'L0_ffn_W': _L0_ffn_in['W'], 'L0_ffn_bias': _L0_ffn_in['bias'], 'L0_ffn_rw1': _L0_ffn_in['rw1'], 'L0_ffn_rb1': _L0_ffn_in['rb1'], 'L0_ffn_rw2': _L0_ffn_in['rw2'], 'L0_ffn_rb2': _L0_ffn_in['rb2'], 'L0_ffn_A': _L0_ffn_in['A'], 'L0_ffn_B': _L0_ffn_in['B'], 'L0_ffn_gates': _L0_ffn_in['gates'], 'L1_attn_weight_qkv': _L1_attn_in['weight_qkv'], 'L1_attn_weight_proj': _L1_attn_in['weight_proj'], 'L1_ffn_Wr': _L1_ffn_in['Wr'], 'L1_ffn_Wg': _L1_ffn_in['Wg'], 'L1_ffn_Wu': _L1_ffn_in['Wu'], 'L1_ffn_Wd': _L1_ffn_in['Wd'], 'L1_ffn_Wsg': _L1_ffn_in['Wsg'], 'L1_ffn_Wsu': _L1_ffn_in['Wsu'], 'L1_ffn_Wsd': _L1_ffn_in['Wsd'], 'L1_ffn_Wse': _L1_ffn_in['Wse']}
    _x0 = _d['L0_attn_x']
    _d['L0_attn_x'] = jax.random.normal(jax.random.fold_in(jax.random.key(seed), 1), (4, 256, 256), dtype=_x0.dtype)
    del _x0
    return _d

def reference(L0_attn_x, L0_attn_Wq, L0_attn_bq, L0_attn_Wk, L0_attn_bk, L0_attn_Wv, L0_attn_bv, L0_attn_Wo, L0_attn_bo, L0_ffn_W, L0_ffn_bias, L0_ffn_rw1, L0_ffn_rb1, L0_ffn_rw2, L0_ffn_rb2, L0_ffn_A, L0_ffn_B, L0_ffn_gates, L1_attn_weight_qkv, L1_attn_weight_proj, L1_ffn_Wr, L1_ffn_Wg, L1_ffn_Wu, L1_ffn_Wd, L1_ffn_Wsg, L1_ffn_Wsu, L1_ffn_Wsd, L1_ffn_Wse):

    def _L0_attn_ref(x, Wq, bq, Wk, bk, Wv, bv, Wo, bo):
        import jax, jax.numpy as jnp
        import numpy as np
        N_HEADS = 16
        D_HEAD = 128
        D_MODEL = 256
        MAXLEN = 256
        b, t, _ = x.shape
        h, dh = (N_HEADS, D_HEAD)
        scale = 1.0 / np.sqrt(dh).astype(np.float32)
        q = (x @ Wq + bq).reshape(b, h, t, dh)
        k = (x @ Wk + bk).reshape(b, t, h, dh).transpose(0, 2, 3, 1)
        v = (x @ Wv + bv).reshape(b, t, h, dh).transpose(0, 2, 1, 3)
        logits = jnp.einsum('bhtd,bhds->bhts', q, k) * scale
        mask = jnp.triu(jnp.full((t, t), -jnp.inf, dtype=x.dtype), k=1)
        weights = jax.nn.softmax(logits + mask, axis=-1)
        out = jnp.einsum('bhts,bhsd->bhtd', weights, v)
        out = out.transpose(0, 2, 1, 3).reshape(b, t, h * dh)
        return out @ Wo + bo

    def _L0_ffn_ref(x, W, bias, rw1, rb1, rw2, rb2, A, B, gates):
        import jax, jax.numpy as jnp
        import numpy as np
        D_IN = 256
        D_OUT = 256
        RANK = 16
        N_EXPERTS = 16
        MAX_EXPERTS = 32
        ROUTER_HID = 64
        TOPK = 2
        ALPHA = 1.0

        def _forward(x, W, bias, rw1, rb1, rw2, rb2, A, B, gates):
            lead = x.shape[:-1]
            x_flat = x.reshape(-1, D_IN)
            n = x_flat.shape[0]
            feat = jax.lax.stop_gradient(x_flat)
            h = jax.nn.silu(feat @ rw1.T + rb1)
            logits = (h @ rw2.T + rb2)[:, :N_EXPERTS] + gates[None, :]
            topv, topi = jax.lax.top_k(logits, TOPK)
            sm = jax.nn.softmax(topv, axis=-1)
            rows = jnp.arange(n)[:, None]
            coeff = jnp.zeros_like(logits).at[rows, topi].set(sm)
            base = x_flat @ W.T + bias
            xa = jnp.einsum('ni,eri->ner', x_flat, A)
            wxa = xa * coeff[:, :, None]
            delta = jnp.einsum('ner,eor->no', wxa, B)
            out = base + ALPHA * delta
            return out.reshape(*lead, D_OUT)
        return _forward(x, W, bias, rw1, rb1, rw2, rb2, A, B, gates)

    def _L1_attn_ref(x, weight_qkv, weight_proj):
        import jax, jax.numpy as jnp
        import numpy as np
        HIDDEN = 256
        NUM_HEADS = 16
        NUM_KV_HEADS = 4
        HEAD_DIM = HIDDEN // NUM_HEADS
        Q_PER_KV = NUM_HEADS // NUM_KV_HEADS
        GROUP_SIZE = (Q_PER_KV + 2) * HEAD_DIM
        TOTAL_PROJ = NUM_KV_HEADS * GROUP_SIZE
        SEQ, BATCH = (256, 2)
        seq, batch, hidden = x.shape
        q_size = Q_PER_KV * HEAD_DIM
        qkv = x.reshape(-1, hidden) @ weight_qkv.T
        qkv = qkv.reshape(-1, NUM_KV_HEADS, GROUP_SIZE)
        q = qkv[:, :, :q_size].reshape(seq, batch, NUM_HEADS, HEAD_DIM)
        k = qkv[:, :, q_size:q_size + HEAD_DIM].reshape(seq, batch, NUM_KV_HEADS, HEAD_DIM)
        v = qkv[:, :, q_size + HEAD_DIM:].reshape(seq, batch, NUM_KV_HEADS, HEAD_DIM)
        k = jnp.repeat(k, Q_PER_KV, axis=2)
        v = jnp.repeat(v, Q_PER_KV, axis=2)
        q = q.transpose(1, 2, 0, 3)
        k = k.transpose(1, 2, 0, 3)
        v = v.transpose(1, 2, 0, 3)
        scale = 1.0 / np.sqrt(HEAD_DIM)
        scores = jnp.einsum('bhqd,bhkd->bhqk', q, k) * scale
        causal = jnp.tril(jnp.ones((seq, seq), dtype=bool))
        scores = jnp.where(causal, scores, jnp.float32(-jnp.inf))
        probs = jax.nn.softmax(scores, axis=-1)
        attn = jnp.einsum('bhqk,bhkd->bhqd', probs, v)
        attn = attn.transpose(2, 0, 1, 3).reshape(seq * batch, NUM_HEADS * HEAD_DIM)
        out = attn @ weight_proj.T
        return out.reshape(seq, batch, hidden)

    def _L1_ffn_ref(hidden_states, Wr, Wg, Wu, Wd, Wsg, Wsu, Wsd, Wse):
        import jax, jax.numpy as jnp
        import numpy as np
        B, S, H = (1, 128, 256)
        E, K = (32, 4)
        F, FS = (176, 704)
        CAP = 32

        def silu(x):
            return x * jax.nn.sigmoid(x)
        b, s_len, h = hidden_states.shape
        x = hidden_states.reshape(-1, h)
        T = x.shape[0]
        probs = jax.nn.softmax(x @ Wr, axis=-1)
        topw, topi = jax.lax.top_k(probs, K)
        topw = topw / jnp.sum(topw, axis=-1, keepdims=True)
        shared = silu(x @ Wsg) * (x @ Wsu) @ Wsd
        shared = shared * jax.nn.sigmoid(x @ Wse)
        sel = topi.reshape(-1)
        w = topw.reshape(-1)
        tok = jnp.repeat(jnp.arange(T), K)
        oh = jax.nn.one_hot(sel, E, dtype=jnp.int32)
        pos = (jnp.cumsum(oh, axis=0) * oh).sum(-1) - 1
        valid = (pos < CAP).astype(x.dtype)
        posc = jnp.clip(pos, 0, CAP - 1)
        xe = jnp.zeros((E, CAP, h), x.dtype).at[sel, posc].add(x[tok] * valid[:, None])
        g = silu(jnp.einsum('ech,ehf->ecf', xe, Wg))
        u = jnp.einsum('ech,ehf->ecf', xe, Wu)
        ye = jnp.einsum('ecf,efh->ech', g * u, Wd)
        y_pair = ye[sel, posc] * (w * valid)[:, None]
        out = shared.at[tok].add(y_pair)
        return out.reshape(b, s_len, h)
    x = L0_attn_x
    xn = _layernorm(x, axis=-1)
    x = x + _L0_attn_ref(xn, L0_attn_Wq, L0_attn_bq, L0_attn_Wk, L0_attn_bk, L0_attn_Wv, L0_attn_bv, L0_attn_Wo, L0_attn_bo) + _L0_ffn_ref(xn, L0_ffn_W, L0_ffn_bias, L0_ffn_rw1, L0_ffn_rb1, L0_ffn_rw2, L0_ffn_rb2, L0_ffn_A, L0_ffn_B, L0_ffn_gates)
    xn = _layernorm(x, axis=-1)
    x = x + _L1_attn_ref(xn, L1_attn_weight_qkv, L1_attn_weight_proj) + _L1_ffn_ref(xn, L1_ffn_Wr, L1_ffn_Wg, L1_ffn_Wu, L1_ffn_Wd, L1_ffn_Wsg, L1_ffn_Wsu, L1_ffn_Wsd, L1_ffn_Wse)
    return x

_drawn_inputs = setup_inputs


def setup_inputs(seed=0):
    import zlib

    import numpy as np

    out = dict(_drawn_inputs(seed))
    spreads = {'L0_attn_bq': (0.0, 0.8),
     'L0_attn_bk': (0.0, 0.8),
     'L0_attn_bv': (0.0, 0.1),
     'L0_attn_bo': (0.0, 0.1),
     'L0_ffn_rb1': (0.0, 0.8),
     'L0_ffn_rb2': (0.0, 0.8),
     'L0_ffn_gates': (1.0, 0.6)}
    factors = {'L0_attn_Wq': 8.0,
     'L0_attn_Wk': 8.0,
     'L0_ffn_bias': 2.952,
     'L0_ffn_rw1': 8.0,
     'L0_ffn_rw2': 8.0,
     'L0_ffn_A': 3.364,
     'L0_ffn_B': 3.361,
     'L1_ffn_Wr': 8.0,
     'L1_ffn_Wg': 8.0,
     'L1_ffn_Wu': 8.0,
     'L1_ffn_Wd': 8.0,
     'L1_ffn_Wsg': 4.337,
     'L1_ffn_Wsu': 4.314,
     'L1_ffn_Wsd': 4.303,
     'L1_ffn_Wse': 8.0}
    for name, (base, spread) in spreads.items():
        noise = np.random.default_rng([zlib.crc32(name.encode()), seed]).standard_normal(out[name].shape)
        drawn = base * np.exp(spread * noise) if base else spread * noise
        out[name] = jnp.asarray(drawn.astype(out[name].dtype))
    for name, factor in factors.items():
        out[name] = (out[name] * factor).astype(out[name].dtype)
    return out
```

```python
from contextlib import ExitStack

import concourse.bass as bass
from concourse import mybir

F32 = mybir.dt.float32
FR = mybir.dt.float32r
BF16 = mybir.dt.bfloat16
U32 = mybir.dt.uint32
ALU = mybir.AluOpType
ACT = mybir.ActivationFunctionType
AX = mybir.AxisListType.X

P = 128
B, T, D = 4, 256, 256
N = B * T
NT = N // P
C = D // P
H, DH = 16, 128
SCALE = float(DH) ** -0.5
PAIRS = H // 2
UNITS = H * B
AHEAD = 10
E0, RANK, HID = 16, 16, 64
H1, D1, G1 = 16, 16, 4
SCALE1 = float(D1) ** -0.5
GW = (H1 // G1 + 2) * D1
QKV = G1 * GW
E1, K1, CAP = 32, 4, 32
F1, FS = 176, 704
FC = 6
FP = FC * P
SLOTS = E1 * CAP
GR = SLOTS // P
EPG = E1 // GR
EPS = 1e-5
MASKED = -1.0e30


def program(nc, a, out, stop_after_l0=False):
    ctx = ExitStack()
    with ctx:
        def sb(name, shape, dt=F32):
            return ctx.enter_context(nc.sbuf_tensor(name, shape, dt))

        def sem(name):
            return ctx.enter_context(nc.semaphore(name))

        pb = [ctx.enter_context(nc.psum_tensor(f"bank{i}", [P, 512], F32)) for i in range(8)]

        ident = sb("ident", [P, P])
        identb = sb("identb", [P, P], BF16)
        maskb = sb("maskb", [P, P], BF16)
        trib = sb("trib", [P, P], BF16)
        onesb = sb("onesb", [P, P], BF16)
        iota = sb("iota", [P, 32])

        X = sb("X", [P, NT, D])
        XT = sb("XT", [P, C, N])
        XTh = sb("XTh", [P, C, N], FR)
        XTl = sb("XTl", [P, C, N], FR)
        stats = sb("stats", [P, NT, 6])
        mv = sb("mv", [P, NT, 2])
        rstd = sb("rstd", [P, NT])

        WA = sb("WA", [P, 2, 2, 1024], FR)

        arena = sb("arena", [P, 35840])

        def region(at, words):
            return arena[:, at:at + words]

        QO = region(0, 16384).rearrange("p (h b t) -> p h b t", h=H, b=B)
        QOb = region(0, 16384).rearrange("p (h b t k) -> p h b t k", h=H, b=B, k=16)
        WQ = region(16384, 4096)
        WQv = WQ.rearrange("p (g c n) -> p g c n", g=4, c=C)
        WOv = WQ.rearrange("p (h n) -> p h n", h=H)
        KVR = region(31744, 1024).rearrange("p (a c n) -> p a c n", a=2, c=C)
        KTf = region(20480, 4096)
        KT = KTf.rearrange("p (a h n) -> p a h n", a=2, h=2)
        XN = KTf[:, 0:2048].rearrange("p (j d) -> p j d", j=NT)
        WXA = KTf[:, 2048:4096].rearrange("p (j d) -> p j d", j=NT)
        Vf = region(24576, 4096)
        V = Vf.rearrange("p (a j n) -> p a j n", a=2, j=NT)
        stW = Vf[:, 0:512].rearrange("p (o i) -> p o i", o=2)
        stA = Vf[:, 512:1024].rearrange("p (o i) -> p o i", o=2)
        stB = Vf[:, 1024:1536].rearrange("p (o e r) -> p o e r", o=2, e=E0)
        stBf = Vf[:, 1024:1536].rearrange("p (o i) -> p o i", o=2)
        stQKV = Vf[:, 1536:2304].rearrange("p (o i) -> p o i", o=3)
        stP = Vf[:, 2304:2816].rearrange("p (o i) -> p o i", o=2)
        stR1 = Vf[0:HID, 2816:3072]
        stR2 = Vf[0:E0, 3072:3136]
        VB = Vf[0:48, 3136:3264]
        bo2 = Vf[:, 3264:3776].rearrange("p (o i) -> p o i", o=2)
        Pb = region(28672, 768).rearrange("p (i n) -> p i n", i=2)
        PTb = region(29440, 768).rearrange("p (i n) -> p i n", i=2)
        nmax = sb("nmax", [P, 2, 2])
        psumr = sb("psumr", [P, 2, 2])
        rinv = sb("rinv", [P, 2, 2])
        WT, AT, B2 = (region(30208 + 512 * i, 512).rearrange("p (c n) -> p c n", c=C) for i in range(3))
        QW = sb("QW", [P, C, QKV + E1 + 1])
        projT = sb("projT", [P, C, D])
        R1T = sb("R1T", [P, C, P])
        R2T = sb("R2T", [P, E0])
        rb1c = sb("rb1c", [P, 1])
        VC = sb("VC", [P, 48])
        bqs = sb("bqs", [P, H])
        rg = sb("rg", [P, 2, E0])
        HT = region(32768, N)
        lg = sb("lg", [P, NT, E0])
        top = sb("top", [P, NT, 8])
        topi = sb("topi", [P, NT, 8], U32)
        topf = sb("topf", [P, NT, 8])
        tmpk = sb("tmpk", [P, NT, E0])
        coef = sb("coef", [P, NT, E0])
        p01 = sb("p01", [P, 3, NT])
        WXT = region(33792, 2048).rearrange("p (c n) -> p c n", c=C)

        EW = [region(4864 * i, 4864) for i in range(2)]
        WGU = [w[:, 0:2816].rearrange("p (e c n) -> p e c n", e=EPG, c=C) for w in EW]
        WD = [w[:, 2816:4864].rearrange("p (e c n) -> p e c n", e=EPG, c=2) for w in EW]
        ACTT = region(9728, FC * N).rearrange("p (m n) -> p m n", m=FC)
        CM = region(9728, 2048).rearrange("p (i n) -> p i n", i=2)
        CT = region(11776, 2048).rearrange("p (i g n) -> p i g n", i=2, g=GR)
        HTE = region(15872, 512).rearrange("p (i k n) -> p i k n", i=2, k=2)
        QS = region(16384, 3360).rearrange("p (j n) -> p j n", j=NT)
        HE = region(19744, 352).rearrange("p (i n) -> p i n", i=2)
        SGR = region(20480, 3072).rearrange("p (a c n) -> p a c n", a=2, c=C)
        PR = region(23552, 1024).rearrange("p (i n) -> p i n", i=4)
        SD = region(24576, 1536).rearrange("p (m n) -> p m n", m=FC)
        AOT = region(26112, 2048).rearrange("p (c n) -> p c n", c=C)
        XE = region(28672, 2048).rearrange("p (c n) -> p c n", c=C)
        SC = region(30720, 512).rearrange("p (f i h j) -> p f i h j", f=2, i=4, h=H1)
        SCf = region(30720, 512).rearrange("p (x j) -> p x j", j=4)
        XN2 = region(31744, 2048).rearrange("p (j n) -> p j n", j=NT)
        AO = XN2
        YE = region(33792, 2048).rearrange("p (g n) -> p g n", g=GR)
        XRh, XRl = (WA[:, i].rearrange("p a n -> p (a n)").rearrange("p (j n) -> p j n", j=NT) for i in range(2))
        SG = sb("SG", [P, 2, 2, 2, C, P], FR)
        DM = sb("DM", [P, 2, SLOTS], FR)
        selb = sb("selb", [P, NT, E1], BF16)
        sel = sb("sel", [P, NT, E1])
        wsel = sb("wsel", [P, NT, E1])
        tmp1 = sb("tmp1", [P, NT, E1])
        posm = sb("posm", [P, NT, E1])
        top1 = sb("top1", [P, NT, 8])
        topi1 = sb("topi1", [P, NT, 8], U32)
        topf1 = sb("topf1", [P, NT, 8])
        w4 = sb("w4", [P, NT, K1])
        ws = sb("ws", [P, NT])
        sig = sb("sig", [P, NT])
        mx1 = sb("mx1", [P, 128])
        pvt = sb("pvt", [P, 256])

        s_x = [sem(f"x_loaded{b}") for b in range(B)]
        s_vb = sem("bias_vectors_loaded")
        s_r = sem("router_weights_loaded")
        s_wq = [sem(f"wq_loaded{g}") for g in range(4)]
        s_sw = sem("small_weights_loaded")
        s_bo = sem("output_biases_loaded")
        s_kv = sem("kv_weights_loaded")
        s_wo = sem("wo_loaded")
        s_pool = sem("pool_step_done")
        s_const = sem("constants_ready")
        s_pad = sem("padding_ready")
        s_st = sem("ln_stats_done")
        s_var = sem("var_ready")
        s_std = sem("std_ready")
        s_rs = sem("rstd_ready")
        s_xn = sem("xn_ready")
        s_xb = sem("x_biased")
        s_xt = sem("xn_transposed")
        s_xtc = sem("xt_copied")
        s_xth = sem("xt_high_ready")
        s_xtl = sem("xt_low_ready")
        s_t = sem("weights_transposed")
        s_tc = sem("transposed_weights_copied")
        s_vc = sem("bias_columns_ready")
        s_wh = sem("weight_high_ready")
        s_wl = sem("weight_low_ready")
        s_qf = sem("q_filled")
        s_qa = sem("q_copied_by_act")
        s_qd = sem("q_copied_by_dve")
        s_ht = sem("router_hidden_done")
        s_hs = sem("router_silu_done")
        s_lg = sem("router_logits_done")
        s_lc = sem("router_logits_copied")
        s_dv = sem("dve_step_done")
        s_ex = sem("router_exp_done")
        s_df = sem("router_difference_ready")
        s_xa = sem("xa_done")
        s_wxa = sem("xa_weighted")
        s_wxt = sem("xa_transposed")
        s_wxc = sem("xa_transposed_copied")
        s_kf = sem("kv_filled")
        s_kc = sem("kv_copied")
        s_S = sem("scores_ready")
        s_m = sem("max_ready")
        s_e = sem("exp_ready")
        s_ri = sem("rinv_ready")
        s_p = sem("probs_ready")
        s_T = sem("probs_transposed")
        s_Tc = sem("probs_transposed_copied")
        s_O = sem("heads_ready")
        s_Oc = sem("heads_copied")
        s_y = sem("l0_out_done")
        s_x1 = sem("x1_ready")
        s_pd = sem("l1_padding_ready")
        s_pe = sem("expert_padding_ready")
        s_sg = sem("shared_up_weights_loaded")
        s_sd = sem("shared_down_weights_loaded")
        s_ew = [sem(f"expert_weights_loaded{i}") for i in range(2)]
        s_va2 = sem("var2_ready")
        s_sd2 = sem("std2_ready")
        s_xn2 = sem("xn2_ready")
        s_xr = sem("xn2_high_ready")
        s_xrl = sem("xn2_low_ready")
        s_t2 = sem("xn2_transposed")
        s_c2 = sem("xn2_transpose_copied")
        s_h2 = sem("xn2_transpose_high_ready")
        s_l2 = sem("xn2_transpose_low_ready")
        s_qk = sem("qkv_done")
        s_qc = sem("qkv_copied")
        s_gh = sem("shared_weight_high_ready")
        s_gl = sem("shared_weight_low_ready")
        s_sf = sem("shared_filled")
        s_ss = sem("shared_silu_done")
        s_sm = sem("shared_product_done")
        s_d1 = sem("gate_logit_differences_ready")
        s_e1 = sem("gate_exp_done")
        s_sel = sem("selection_ready")
        s_po = sem("positions_done")
        s_dm = sem("dispatch_mask_ready")
        s_di = sem("dispatched_tile")
        s_xe = sem("slots_copied")
        s_up = sem("expert_up_done")
        s_es = sem("expert_silu_done")
        s_eh = sem("expert_hidden_ready")
        s_et = sem("expert_hidden_transposed")
        s_ec = sem("expert_hidden_copied")
        s_dn = sem("expert_down_done")
        s_ye = sem("expert_output_copied")
        s_sh = sem("shared_down_done")
        s_x2 = sem("shared_added")
        s_am = sem("attn1_scores_less_max")
        s_ae = sem("attn1_exp_done")
        s_ap = sem("attn1_probs_ready")
        s_pv = sem("attn1_step_done")
        s_ao = sem("attn1_tile_ready")
        s_at = sem("attn1_transposed")
        s_ac = sem("attn1_transposed_copied")
        s_cm = sem("combine_weights_ready")
        s_ct = sem("combine_weights_transposed")
        s_cc = sem("combine_weights_copied")
        s_fo = sem("l1_out_done")
        s_o = sem("out_ready")
        s_out = sem("out_stored")

        block = ctx.enter_context(nc.Block())

        x_t = a["L0_attn_x"].rearrange("b (q p) d -> p b q d", p=P)
        out_t = out.rearrange("b (q p) d -> p (b q) d", p=P)
        wq_t = a["L0_attn_Wq"].rearrange("(c p) n -> p c n", p=P)
        wk_t = a["L0_attn_Wk"].rearrange("(c p) n -> p c n", p=P)
        wv_t = a["L0_attn_Wv"].rearrange("(c p) n -> p c n", p=P)
        two = lambda w: w.rearrange("(o p) i -> p o i", p=P)
        row = lambda v, k: v.rearrange("(h d) -> h d", h=k)

        def unit(u):
            p, hh, b = u // 8, u // 4 % 2, u % 4
            return p, hh, b, 2 * p + hh

        @block.sync
        def _(sp):
            for b in range(B):
                sp.dma_start(X[:, 2 * b:2 * b + 2, :], x_t[:, b]).then_inc(s_x[b], 16)
            sp.dma_start(WQv[:, 0], wq_t[:, :, 0:512]).then_inc(s_wq[0], 16)
            for i, n in enumerate(("bq", "bk", "bv")):
                sp.dma_start(VB[16 * i:16 * i + 16, :], row(a["L0_attn_" + n], H)).then_inc(s_vb, 16)
            sp.dma_start(stR1, a["L0_ffn_rw1"]).then_inc(s_r, 16)
            sp.dma_start(stR2, a["L0_ffn_rw2"][0:E0, :]).then_inc(s_r, 16)
            sp.wait_ge(s_pad, 3)
            sp.dma_start(rb1c[0:HID, :], a["L0_ffn_rb1"].rearrange("(p a) -> p a", a=1)).then_inc(s_r, 16)
            sp.dma_start(rg[:, 0], a["L0_ffn_rb2"][0:E0].partition_broadcast(P)).then_inc(s_r, 16)
            sp.dma_start(rg[:, 1], a["L0_ffn_gates"].partition_broadcast(P)).then_inc(s_r, 16)
            sp.dma_start(WQv[:, 1], wq_t[:, :, 512:1024]).then_inc(s_wq[1], 16)
            sp.dma_start(stW, two(a["L0_ffn_W"])).then_inc(s_sw, 16)
            sp.dma_start(stA, a["L0_ffn_A"].rearrange("(o e) r i -> (e r) o i", o=2)).then_inc(s_sw, 16)
            for o in range(2):
                sp.dma_start(stB[:, o], a["L0_ffn_B"][:, P * o:P * o + P, :].rearrange("e p r -> p e r")).then_inc(s_sw, 16)
            sp.dma_start(stQKV, two(a["L1_attn_weight_qkv"])).then_inc(s_sw, 16)
            sp.dma_start(stP, two(a["L1_attn_weight_proj"])).then_inc(s_sw, 16)
            sp.dma_start(bo2[:, 0], a["L0_attn_bo"].partition_broadcast(P)).then_inc(s_bo, 16)
            sp.dma_start(bo2[:, 1], a["L0_ffn_bias"].partition_broadcast(P)).then_inc(s_bo, 16)
            for g in (2, 3):
                sp.dma_start(WQv[:, g], wq_t[:, :, 512 * g:512 * g + 512]).then_inc(s_wq[g], 16)

            for c in range(C):
                sp.dma_start(QW[:, c, QKV:QKV + E1], a["L1_ffn_Wr"][P * c:P * c + P, :]).then_inc(s_bo, 16)
                sp.dma_start(QW[:, c, QKV + E1:QKV + E1 + 1], a["L1_ffn_Wse"][P * c:P * c + P, :]).then_inc(s_bo, 16)

            def load_kv(p):
                sp.dma_start(KVR[:, 0], wk_t[:, :, 256 * p:256 * p + 256]).then_inc(s_kv, 16)
                sp.dma_start(KVR[:, 1], wv_t[:, :, 256 * p:256 * p + 256]).then_inc(s_kv, 16)

            load_kv(0)
            sp.wait_ge(s_wl, 4)
            sp.dma_start(WOv, a["L0_attn_Wo"].rearrange("(h d) n -> d h n", d=P)).then_inc(s_wo, 16)
            for p in range(1, PAIRS):
                sp.wait_ge(s_wl, 4 + p)
                load_kv(p)
            if stop_after_l0:
                sp.wait_ge(s_x1, NT)
                sp.dma_start(out_t, X[:]).then_inc(s_out, 16)
                sp.wait_ge(s_out, 16)
                return
            sp.wait_ge(s_pd, 2)
            for i, n in enumerate(("Wsg", "Wsu")):
                sp.dma_start(SGR[:, i, :, 0:FS], a["L1_ffn_" + n].rearrange("(c p) n -> p c n", p=P)).then_inc(s_sg, 16)
            sp.dma_start(SD[:, 0:FC - 1], a["L1_ffn_Wsd"][0:P * (FC - 1), :].rearrange("(m p) n -> p m n", p=P)).then_inc(s_sd, 16)
            sp.dma_start(SD[0:FS - P * (FC - 1), FC - 1], a["L1_ffn_Wsd"][P * (FC - 1):FS, :]).then_inc(s_sd, 16)
            sp.wait_ge(s_pe, 3)
            for g in range(GR):
                e, i = slice(EPG * g, EPG * g + EPG), g % 2
                if g >= 2:
                    sp.wait_ge(s_dn, g - 1)
                for k, n in enumerate(("Wg", "Wu")):
                    sp.dma_start(WGU[i][:, :, :, F1 * k:F1 * k + F1],
                                 a["L1_ffn_" + n][e].rearrange("e (c p) n -> p e c n", p=P)).then_inc(s_ew[i], 16)
                sp.dma_start(WD[i][:, :, 0], a["L1_ffn_Wd"][e, 0:P].rearrange("e p n -> p e n")).then_inc(s_ew[i], 16)
                sp.dma_start(WD[i][0:F1 - P, :, 1], a["L1_ffn_Wd"][e, P:F1].rearrange("e p n -> p e n")).then_inc(s_ew[i], 16)
            for j in range(NT):
                sp.wait_ge(s_o, j + 1)
                sp.dma_start(out_t[:, j], X[:, j]).then_inc(s_out, 16)
            sp.wait_ge(s_out, 16 * NT)

        @block.gpsimd
        def _(pool):
            steps = [0]

            def step(ins):
                ins.then_inc(s_pool, 1)
                steps[0] += 1
                pool.wait_ge(s_pool, steps[0])

            step(pool.memset(ident[:], 0.0))
            pool.affine_select(out=ident[:], in_=ident[:], compare_op=ALU.not_equal, fill=1.0, base=0,
                               pattern=[[-1, P]], channel_multiplier=1).then_inc(s_const, 1)
            pool.memset(R1T[:], 0.0).then_inc(s_pad, 1)
            pool.memset(R2T[:], 0.0).then_inc(s_pad, 1)
            pool.memset(rb1c[:], 0.0).then_inc(s_pad, 1)
            pool.wait_ge(s_const, 1)
            pool.tensor_copy(identb[:], ident[:]).then_inc(s_const, 1)
            step(pool.memset(maskb[:], 0.0))
            pool.affine_select(out=maskb[:], in_=maskb[:], compare_op=ALU.is_ge, fill=MASKED, base=0,
                               pattern=[[-1, P]], channel_multiplier=1).then_inc(s_const, 1)
            pool.iota(iota[:], [[1, 32]], base=0, channel_multiplier=0,
                      allow_small_or_imprecise_dtypes=True).then_inc(s_const, 1)
            pool.memset(onesb[:], 1.0).then_inc(s_const, 1)
            pool.wait_ge(s_const, 5)
            pool.affine_select(out=trib[:], in_=onesb[:], compare_op=ALU.is_ge, fill=0.0, base=0,
                               pattern=[[1, P]], channel_multiplier=-1).then_inc(s_const, 1)
            pool.wait_ge(s_bo, 96)
            step(pool.tensor_tensor(bo2[:, 0], bo2[:, 0], bo2[:, 1], ALU.add))
            for j in range(NT):
                pool.wait_ge(s_xn, j + 1)
                pool.tensor_tensor(X[:, j], X[:, j], bo2[:, 0], ALU.add).then_inc(s_xb, 1)
            if stop_after_l0:
                return
            pool.wait_ge(s_Oc, UNITS)
            pool.wait_ge(s_kc, 8 * PAIRS)
            pool.memset(SGR[:, :, :, FS:FP], 0.0).then_inc(s_pd, 1)
            pool.memset(SD[:, FC - 1], 0.0).then_inc(s_pd, 1)
            pool.wait_ge(s_y, NT)
            for i in range(2):
                pool.memset(WD[i][:, :, 1], 0.0).then_inc(s_pe, 1)
            pool.memset(HTE, 0.0).then_inc(s_pe, 1)
            chain = 0
            for f in range(2):
                pool.wait_ge(s_ap, f + 1)
                for i in range(4):
                    j = 2 * i + f
                    for k in range(i + 1):
                        v = QS[:, 2 * k + f, 0:QKV].rearrange("p (g n) -> p g n", g=G1)[:, :, None, GW - D1:GW].to_broadcast([P, G1, 4, D1])
                        p = SC[:, f, i, :, k].rearrange("p (g r) -> p g r", g=G1)[:, :, :, None].to_broadcast([P, G1, 4, D1])
                        dst = AO[:, j] if k == 0 else pvt[:]
                        pool.tensor_tensor(dst.rearrange("p (g r d) -> p g r d", g=G1, r=4), p, v, ALU.mult).then_inc(s_pv, 1)
                        chain += 1
                        pool.wait_ge(s_pv, chain)
                        if k:
                            pool.tensor_tensor(AO[:, j], AO[:, j], pvt[:], ALU.add).then_inc(s_pv, 1)
                            chain += 1
                            pool.wait_ge(s_pv, chain)

        @block.scalar
        def _(act):
            for b in range(B):
                act.wait_ge(s_var, b + 1)
                nc.scalar.activation(rstd[:, 2 * b:2 * b + 2], mv[:, 2 * b:2 * b + 2, 1], ACT.Sqrt).then_inc(s_std, 1)

            def w_high(n, raw):
                if n >= 2:
                    act.wait_ge(s_qf, 8 * (n - 1)) if n < 6 else act.wait_ge(s_kf, 8 * (n - 5))
                nc.scalar.activation(WA[:, n % 2, 0], raw, ACT.Copy).then_inc(s_wh, 1)

            for f in range(4):
                half, c = f // 2, f % 2
                act.wait_ge(s_xt, f + 1)
                nc.scalar.activation(XT[:, c, 512 * half:512 * half + 512], pb[f][:], ACT.Copy).then_inc(s_xtc, 1)
                nc.scalar.activation(XTh[:, c, 512 * half:512 * half + 512], pb[f][:], ACT.Copy).then_inc(s_xth, 1)
            act.wait_ge(s_wq[0], 16)
            w_high(0, WQv[:, 0])
            act.wait_ge(s_t, 2)
            act.wait_ge(s_pad, 3)
            nc.scalar.activation(R1T[:, :, 0:HID], pb[5][:, 0:2 * HID].rearrange("p (c n) -> p c n", c=C), ACT.Copy).then_inc(s_tc, 1)
            nc.scalar.activation(R2T[0:HID, :], pb[5][0:HID, 256:256 + E0], ACT.Copy).then_inc(s_tc, 1)
            act.wait_ge(s_r, 80)
            for half in range(2):
                act.wait_ge(s_ht, half + 1)
                nc.scalar.activation(HT[:, 512 * half:512 * half + 512], pb[6 + half][:], ACT.Silu, bias=rb1c[:]).then_inc(s_hs, 1)
            act.wait_ge(s_wq[1], 16)
            w_high(1, WQv[:, 1])
            act.wait_ge(s_vc, 2)

            def q_copy(n):
                blk, half = n // 2, n % 2
                act.wait_ge(s_qf, n + 1)
                nc.scalar.activation(QOb[:, :, 2 * half:2 * half + 2, :, blk].rearrange("p h b t -> p b h t"),
                                     pb[n % 4][:].rearrange("p (b h t) -> p b h t", b=2, h=H),
                                     ACT.Identity, bias=bqs[:, blk:blk + 1], scale=SCALE).then_inc(s_qa, 1)

            def weight_copy(n, dst, src):
                act.wait_ge(s_t, n)
                nc.scalar.activation(dst, src, ACT.Copy).then_inc(s_tc, 1)

            for g in range(4):
                if g >= 1 and g + 1 < 4:
                    act.wait_ge(s_wq[g + 1], 16)
                    w_high(g + 1, WQv[:, g + 1])
                for n in range(8 * g, 8 * g + 8, 2):
                    q_copy(n)
                if g == 0:
                    act.wait_ge(s_df, 1)
                    nc.scalar.activation(p01[:, 1], p01[:, 0], ACT.Exp).then_inc(s_ex, 1)
                    for i, dst in enumerate((WT, AT, B2)):
                        weight_copy(3 + i, dst.rearrange("p c n -> p (c n)"), pb[5 + i][:])
                if g == 1:
                    weight_copy(6, QW[:, 0, 0:QKV], pb[5][:, 0:QKV])
                    weight_copy(7, QW[:, 1, 0:QKV], pb[6][:, 0:QKV])
                    weight_copy(8, projT[:].rearrange("p c n -> p (c n)"), pb[7][:])
            for f in range(4):
                act.wait_ge(s_wxt, f + 1)
                nc.scalar.activation(WXT[:, f // 2, 512 * (f % 2):512 * (f % 2) + 512], pb[f][:], ACT.Copy).then_inc(s_wxc, 1)
            for p in (0, 1, 2):
                act.wait_ge(s_kv, 32 * (p + 1))
                w_high(4 + p, KVR.rearrange("p a c n -> p (a c n)"))

            def exps(u):
                i = u % 2
                act.wait_ge(s_m, u + 1)
                if u >= 2:
                    act.wait_ge(s_T, u - 1)
                nc.scalar.activation(Pb[:, i, 0:128], pb[i][:, 0:128], ACT.Exp, bias=nmax[:, i, 0:1],
                                     accum_out=psumr[:, i, 0:1])
                nc.scalar.activation(Pb[:, i, 128:384], pb[i][:, 128:384], ACT.Exp, bias=nmax[:, i, 1:2],
                                     accum_out=psumr[:, i, 1:2]).then_inc(s_e, 1)

            def t_copy(u):
                act.wait_ge(s_T, u + 1)
                if u >= 2:
                    act.wait_ge(s_O, u - 1)
                nc.scalar.activation(PTb[:, u % 2], pb[2 + u % 2][:, 0:384], ACT.Copy).then_inc(s_Tc, 1)

            def o_copy(u):
                _, _, b, h = unit(u)
                act.wait_ge(s_O, u + 1)
                nc.scalar.activation(QO[:, h, b], pb[4 + u % 2][:, 0:256], ACT.Identity,
                                     bias=VC[:, 32 + h:33 + h]).then_inc(s_Oc, 1)

            exps(0)
            exps(1)
            t_copy(0)
            for u in range(UNITS):
                if u >= 1:
                    o_copy(u - 1)
                if u + 2 < UNITS:
                    exps(u + 2)
                if u + 1 < UNITS:
                    t_copy(u + 1)
                if u % 8 == 6 and u // 8 + 3 < PAIRS:
                    act.wait_ge(s_kv, 32 * (u // 8 + 4))
                    w_high(4 + u // 8 + 3, KVR.rearrange("p a c n -> p (a c n)"))
            o_copy(UNITS - 1)
            if stop_after_l0:
                return
            act.wait_ge(s_kf, 8 * PAIRS)

            def t2_copy(f):
                half, c = f // 2, f % 2
                xs = slice(512 * half, 512 * half + 512)
                act.wait_ge(s_t2, f + 1)
                nc.scalar.activation(XT[:, c, xs], pb[f][:], ACT.Copy).then_inc(s_c2, 1)
                nc.scalar.activation(XTh[:, c, xs], pb[f][:], ACT.Copy).then_inc(s_h2, 1)

            for j in range(NT):
                act.wait_ge(s_va2, j + 1)
                nc.scalar.activation(rstd[:, j:j + 1], mv[:, j, 1:2], ACT.Sqrt).then_inc(s_sd2, 1)
                act.wait_ge(s_xn2, j + 1)
                nc.scalar.activation(XRh[:, j], XN2[:, j], ACT.Copy).then_inc(s_xr, 1)
                if j == 5:
                    t2_copy(0)
                    t2_copy(1)
            t2_copy(2)
            t2_copy(3)

            def g_high(m):
                if m >= 2:
                    act.wait_ge(s_sf, 2 * (m - 1))
                nc.scalar.activation(SG[:, m % 2, 0], SGR[:, :, :, P * m:P * m + P], ACT.Copy).then_inc(s_gh, 1)

            act.wait_ge(s_sg, 32)
            g_high(0)
            g_high(1)
            for j in range(NT):
                act.wait_ge(s_qk, j + 1)
                nc.scalar.activation(QS[:, j, 0:QKV + E1 + 1], pb[4 + j % 4][:, 0:QKV + E1 + 1], ACT.Copy).then_inc(s_qc, 1)

            def silu(q):
                m, half = q // 2, q % 2
                act.wait_ge(s_sf, q + 1)
                nc.scalar.activation(ACTT[:, m, 512 * half:512 * half + 512], pb[2 * half][:], ACT.Silu).then_inc(s_ss, 1)

            act.wait_ge(s_d1, 1)
            nc.scalar.activation(w4[:], w4[:], ACT.Exp).then_inc(s_e1, 1)
            nc.scalar.activation(sig[:], QS[:, :, QKV + E1], ACT.Exp, scale=-1.0).then_inc(s_e1, 1)
            for q in range(6):
                silu(q)
                if q % 2 and q < 5:
                    g_high(q // 2 + 2)
            for k in range(4):
                c, half = k // 2, k % 2
                act.wait_ge(s_di, NT)
                nc.scalar.activation(XE[:, c, 512 * half:512 * half + 512], pb[k][:], ACT.Copy).then_inc(s_xe, 1)
            g_high(4)

            def e_copy(g):
                act.wait_ge(s_et, g + 1)
                if g >= 2:
                    act.wait_ge(s_dn, g - 1)
                nc.scalar.activation(HTE[:, g % 2, 0], pb[6][:, 0:P], ACT.Copy)
                nc.scalar.activation(HTE[0:F1 - P, g % 2, 1], pb[6][0:F1 - P, P:2 * P], ACT.Copy).then_inc(s_ec, 1)

            act.wait_ge(s_pe, 3)
            for g in range(GR):
                act.wait_ge(s_up, g + 1)
                if g >= 2:
                    act.wait_ge(s_et, g - 1)
                nc.scalar.activation(HE[:, g % 2], pb[4 + g % 2][:, 0:F1], ACT.Silu).then_inc(s_es, 1)
                if g >= 1:
                    e_copy(g - 1)
                if g < 6:
                    silu(6 + g)
                if g == 1:
                    g_high(5)
            e_copy(GR - 1)
            for f in range(2):
                act.wait_ge(s_am, f + 1)
                nc.scalar.activation(SCf[:, 64 * f:64 * f + 64], SCf[:, 64 * f:64 * f + 64], ACT.Exp, scale=SCALE1).then_inc(s_ae, 1)
            for f in range(4):
                act.wait_ge(s_at, f + 1)
                nc.scalar.activation(AOT[:, f // 2, 512 * (f % 2):512 * (f % 2) + 512], pb[4 + f][:], ACT.Copy).then_inc(s_ac, 1)
            for j in range(NT):
                act.wait_ge(s_ct, j + 1)
                if j >= 2:
                    act.wait_ge(s_fo, j - 1)
                for k in range(2):
                    ins = nc.scalar.activation(CT[:, j % 2, 4 * k:4 * k + 4], pb[2 * (j % 2) + k][:].rearrange("p (g n) -> p g n", g=4), ACT.Copy)
                ins.then_inc(s_cc, 1)

        @block.tensor
        def _(pe):
            def mm3(dst, wh, wl, xh, xl, start, stop):
                pe.matmul(dst, wh, xl, start=start, stop=False)
                pe.matmul(dst, wl, xh, start=False, stop=False)
                return pe.matmul(dst, wh, xh, start=False, stop=stop)

            pe.wait_ge(s_const, 1)
            for f in range(4):
                half, c = f // 2, f % 2
                for i in range(4):
                    j = 4 * half + i
                    if c == 0:
                        pe.wait_ge(s_xn, j + 1)
                    ins = pe.transpose(pb[f][:, P * i:P * i + P], XN[:, j, P * c:P * c + P], ident[:])
                ins.then_inc(s_xt, 1)
            pe.wait_ge(s_vb, 48)
            pe.transpose(pb[4][:, 0:48], VB, ident[0:48, 0:48]).then_inc(s_t, 1)
            pe.wait_ge(s_r, 80)
            for c in range(C):
                pe.transpose(pb[5][:, HID * c:HID * c + HID], stR1[:, P * c:P * c + P], ident[0:HID, 0:HID])
            pe.transpose(pb[5][0:HID, 256:256 + E0], stR2, ident[0:E0, 0:E0]).then_inc(s_t, 1)
            pe.wait_ge(s_tc, 2)
            pe.wait_ge(s_xtc, 4)
            for half in range(2):
                for c in range(C):
                    ins = pe.matmul(pb[6 + half][:], R1T[:, c], XT[:, c, 512 * half:512 * half + 512],
                                    start=(c == 0), stop=(c == C - 1))
                ins.then_inc(s_ht, 1)
            pe.wait_ge(s_hs, 2)
            pe.wait_ge(s_vc, 2)
            for j in range(NT):
                ins = pe.matmul(pb[4][:, E0 * j:E0 * j + E0], HT[:, P * j:P * j + P], R2T[:], start=True, stop=True)
            ins.then_inc(s_lg, 1)
            pe.wait_ge(s_xtl, 4)

            def square(bank, st):
                for c in range(C):
                    for o in range(2):
                        ins = pe.transpose(pb[bank][:, 256 * c + P * o:256 * c + P * o + P], st[:, o, P * c:P * c + P], ident[:])
                ins.then_inc(s_t, 1)

            for g in range(4):
                pe.wait_ge(s_wh, g + 1)
                pe.wait_ge(s_wl, g + 1)
                wh = WA[:, g % 2, 0].rearrange("p (c n) -> p c n", c=C)
                wl = WA[:, g % 2, 1].rearrange("p (c n) -> p c n", c=C)
                for n in range(8 * g, 8 * g + 8):
                    blk, half = n // 2 % 4, n % 2
                    if n >= 4:
                        pe.wait_ge(s_qa if n % 2 == 0 else s_qd, n // 2 - 1)
                    for c in range(C):
                        xs = slice(512 * half, 512 * half + 512)
                        ins = mm3(pb[n % 4][:], wh[:, c, P * blk:P * blk + P], wl[:, c, P * blk:P * blk + P],
                                  XTh[:, c, xs], XTl[:, c, xs], c == 0, c == C - 1)
                    ins.then_inc(s_qf, 1)
                if g == 0:
                    pe.wait_ge(s_sw, 96)
                    square(5, stW)
                    square(6, stA)
                    square(7, stBf)
                if g == 1:
                    pe.wait_ge(s_tc, 5)
                    for c in range(C):
                        for o in range(3):
                            ins = pe.transpose(pb[5 + c][:, P * o:P * o + P], stQKV[:, o, P * c:P * c + P], ident[:])
                        ins.then_inc(s_t, 1)
                    square(7, stP)
                if g == 2:
                    pe.wait_ge(s_tc, 8)
                    pe.wait_ge(s_lc, 1)
                    for j in range(NT):
                        for c in range(C):
                            ins = pe.matmul(pb[4 + j // 2][:, 256 * (j % 2):256 * (j % 2) + 256], XT[:, c, P * j:P * j + P],
                                            AT[:, c], start=(c == 0), stop=(c == C - 1))
                        ins.then_inc(s_xa, 1)
            pe.wait_ge(s_qa, 16)
            pe.wait_ge(s_qd, 16)
            for f in range(4):
                c, half = f // 2, f % 2
                for i in range(4):
                    j = 4 * half + i
                    if c == 0:
                        pe.wait_ge(s_wxa, j + 1)
                    ins = pe.transpose(pb[f][:, P * i:P * i + P], WXA[:, j, P * c:P * c + P], ident[:])
                ins.then_inc(s_wxt, 1)

            def fill(n):
                p, f = n // 8, n % 8
                if f == 0:
                    pe.wait_ge(s_wh, 5 + p)
                    pe.wait_ge(s_wl, 5 + p)
                if n >= 2:
                    pe.wait_ge(s_kc, n - 1)
                bank = pb[6 + n % 2]
                wh = WA[:, p % 2, 0].rearrange("p (a c n) -> p a c n", a=2, c=C)
                wl = WA[:, p % 2, 1].rearrange("p (a c n) -> p a c n", a=2, c=C)
                if f < 4:
                    hh, xs = f // 2, slice(512 * (f % 2), 512 * (f % 2) + 512)
                    for c in range(C):
                        ins = mm3(bank[:], wh[:, 0, c, P * hh:P * hh + P], wl[:, 0, c, P * hh:P * hh + P],
                                  XTh[:, c, xs], XTl[:, c, xs], c == 0, c == C - 1)
                else:
                    for i in range(2):
                        j = 2 * (f - 4) + i
                        for c in range(C):
                            ins = mm3(bank[:, 256 * i:256 * i + 256], XTh[:, c, P * j:P * j + P], XTl[:, c, P * j:P * j + P],
                                      wh[:, 1, c], wl[:, 1, c], c == 0, c == C - 1)
                ins.then_inc(s_kf, 1)

            def scores(u):
                p, hh, b, h = unit(u)
                if u % 8 == 0:
                    pe.wait_ge(s_kc, 8 * p + 8)
                if u >= 2:
                    pe.wait_ge(s_e, u - 1)
                s, k = pb[u % 2], KT[:, p % 2, hh]
                pe.matmul(s[:, 0:128], QO[:, h, b, 0:128], k[:, T * b:T * b + 128], start=True, stop=False)
                pe.matmul(s[:, 0:128], identb[:], maskb[:], start=False, stop=True)
                pe.matmul(s[:, 128:384], QO[:, h, b, 128:256], k[:, T * b:T * b + 256], start=True, stop=False)
                pe.matmul(s[:, 256:384], identb[:], maskb[:], start=False, stop=True).then_inc(s_S, 1)

            def turn(u):
                pe.wait_ge(s_p, u + 1)
                if u >= 2:
                    pe.wait_ge(s_Tc, u - 1)
                for i in range(3):
                    ins = pe.transpose(pb[2 + u % 2][:, P * i:P * i + P], Pb[:, u % 2, P * i:P * i + P], ident[:])
                ins.then_inc(s_T, 1)

            def heads(u):
                p, hh, b, h = unit(u)
                pe.wait_ge(s_Tc, u + 1)
                if u >= 2:
                    pe.wait_ge(s_Oc, u - 1)
                o = pb[4 + u % 2][:, 0:256]
                pe.matmul(o, V[:, p % 2, 2 * b, P * hh:P * hh + P], PTb[:, u % 2, 0:256], start=True, stop=False)
                pe.matmul(o[:, 128:256], V[:, p % 2, 2 * b + 1, P * hh:P * hh + P], PTb[:, u % 2, 256:384],
                          start=False, stop=True).then_inc(s_O, 1)

            for n in range(AHEAD):
                if n == 0:
                    pe.wait_ge(s_wxa, NT)
                fill(n)
            pe.wait_ge(s_wxc, 4)
            pe.wait_ge(s_const, 3)
            scores(0)
            scores(1)
            turn(0)
            for u in range(UNITS):
                if u + 2 < UNITS:
                    scores(u + 2)
                if u + 1 < UNITS:
                    turn(u + 1)
                heads(u)
                if u + AHEAD < UNITS:
                    fill(u + AHEAD)

            def turn2(f):
                half, c = f // 2, f % 2
                pe.wait_ge(s_xn2, 4 * half + 4)
                for i in range(4):
                    ins = pe.transpose(pb[f][:, P * i:P * i + P], XN2[:, 4 * half + i, P * c:P * c + P], ident[:])
                ins.then_inc(s_t2, 1)

            pe.wait_ge(s_wo, 16)
            for j in range(NT):
                if j == 6 and not stop_after_l0:
                    turn2(0)
                    turn2(1)
                b, q = j // 2, slice(P * (j % 2), P * (j % 2) + P)
                dst, t = pb[j][:, 0:256], slice(P * j, P * j + P)
                if j == 0:
                    pe.wait_ge(s_Oc, UNITS)
                    pe.wait_ge(s_kc, 8 * PAIRS)
                pe.matmul(dst, XT[:, 0, t], WT[:, 0], start=True, stop=False)
                pe.matmul(dst, XT[:, 1, t], WT[:, 1], start=False, stop=False)
                pe.matmul(dst, WXT[:, 0, t], B2[:, 0], start=False, stop=False)
                pe.matmul(dst, WXT[:, 1, t], B2[:, 1], start=False, stop=False)
                for h in range(H):
                    ins = pe.matmul(dst, QO[:, h, b, q], WOv[:, h], start=False, stop=(h == H - 1))
                ins.then_inc(s_y, 1)
            if stop_after_l0:
                return
            turn2(2)
            turn2(3)
            pe.wait_ge(s_c2, 4)
            for j in range(NT):
                if j < 4:
                    pe.wait_ge(s_x1, 5 + j)
                else:
                    pe.wait_ge(s_qc, j - 3)
                for c in range(C):
                    ins = pe.matmul(pb[4 + j % 4][:, 0:QKV + E1 + 1], XT[:, c, P * j:P * j + P], QW[:, c],
                                    start=(c == 0), stop=(c == C - 1))
                ins.then_inc(s_qk, 1)
            pe.wait_ge(s_l2, 4)

            def shared_up(q):
                m, half = q // 2, q % 2
                pe.wait_ge(s_gh, m + 1)
                pe.wait_ge(s_gl, m + 1)
                if q >= 2:
                    pe.wait_ge(s_sm, q - 1)
                xs = slice(512 * half, 512 * half + 512)
                for k in range(2):
                    for c in range(C):
                        ins = mm3(pb[2 * half + k][:], SG[:, m % 2, 0, k, c], SG[:, m % 2, 1, k, c],
                                  XTh[:, c, xs], XTl[:, c, xs], c == 0, c == C - 1)
                ins.then_inc(s_sf, 1)

            pe.wait_ge(s_h2, 4)
            for q in range(4):
                shared_up(q)
            pe.wait_ge(s_sel, 1)
            pe.wait_ge(s_qc, NT)
            for j in range(NT):
                for i in range(j + 1):
                    ins = pe.matmul(pb[4][:, E1 * j:E1 * j + E1], (trib if i == j else onesb)[:], selb[:, i],
                                    start=(i == 0), stop=(i == j))
            ins.then_inc(s_po, 1)
            shared_up(4)
            shared_up(5)
            pe.wait_ge(s_sm, 6)
            for j in range(NT):
                pe.wait_ge(s_dm, j + 1)
                pe.wait_ge(s_xr, j + 1)
                pe.wait_ge(s_xrl, j + 1)
                for k in range(4):
                    c, half = k // 2, k % 2
                    for n, xr in enumerate((XRh, XRl)):
                        ins = pe.matmul(pb[k][:], xr[:, j, P * c:P * c + P], DM[:, j % 2, 512 * half:512 * half + 512],
                                        start=(j == 0 and n == 0), stop=(j == NT - 1 and n == 1))
                ins.then_inc(s_di, 1)

            def expert_up(g):
                pe.wait_ge(s_ew[g % 2], 64 * (g // 2 + 1))
                if g >= 2:
                    pe.wait_ge(s_eh, g - 1)
                for c in range(C):
                    for e in range(EPG):
                        s = slice(CAP * (EPG * g + e), CAP * (EPG * g + e) + CAP)
                        ins = pe.matmul(pb[4 + g % 2][CAP * e:CAP * e + CAP, 0:2 * F1], XE[:, c, s], WGU[g % 2][:, e, c],
                                        start=(c == 0), stop=(c == C - 1), skip_group_check=True)
                ins.then_inc(s_up, 1)

            def expert_turn(g):
                pe.wait_ge(s_eh, g + 1)
                if g >= 1:
                    pe.wait_ge(s_ec, g)
                pe.transpose(pb[6][:, 0:P], HE[:, g % 2, 0:P], ident[:])
                pe.transpose(pb[6][0:F1 - P, P:2 * P], HE[:, g % 2, P:F1], ident[:]).then_inc(s_et, 1)

            def expert_down(g):
                pe.wait_ge(s_ec, g + 1)
                if g >= 1:
                    pe.wait_ge(s_ye, g)
                for k in range(2):
                    for e in range(EPG):
                        ins = pe.matmul(pb[7][CAP * e:CAP * e + CAP, 0:D], HTE[:, g % 2, k, CAP * e:CAP * e + CAP],
                                        WD[g % 2][:, e, k], start=(k == 0), stop=(k == 1), skip_group_check=True)
                ins.then_inc(s_dn, 1)

            pe.wait_ge(s_xe, 4)
            for g in range(GR):
                expert_up(g)
                if g >= 1:
                    expert_turn(g - 1)
                if g < 6:
                    shared_up(6 + g)
                if g >= 1:
                    expert_down(g - 1)
            expert_turn(GR - 1)
            pe.wait_ge(s_sd, 32)
            pe.wait_ge(s_sm, 12)
            for j in range(NT):
                if j >= 4:
                    pe.wait_ge(s_x2, j - 3)
                for m in range(FC):
                    ins = pe.matmul(pb[j % 4][:, 0:D], ACTT[:, m, P * j:P * j + P], SD[:, m], start=(m == 0), stop=(m == FC - 1))
                ins.then_inc(s_sh, 1)
                if j == 0:
                    expert_down(GR - 1)
            pe.wait_ge(s_ye, GR)
            pe.wait_ge(s_pv, 32)
            for f in range(4):
                c, half = f // 2, f % 2
                for i in range(4):
                    ins = pe.transpose(pb[4 + f][:, P * i:P * i + P], AO[:, 4 * half + i, P * c:P * c + P], ident[:])
                ins.then_inc(s_at, 1)
            pe.wait_ge(s_x2, NT)
            pe.wait_ge(s_ac, 4)

            def combine_turn(j):
                pe.wait_ge(s_cm, 2 * j + 2)
                if j >= 2:
                    pe.wait_ge(s_cc, j - 1)
                for g in range(GR):
                    ins = pe.transpose(pb[2 * (j % 2) + g // 4][:, P * (g % 4):P * (g % 4) + P], CM[:, j % 2, P * g:P * g + P], ident[:])
                ins.then_inc(s_ct, 1)

            combine_turn(0)
            for j in range(NT):
                if j + 1 < NT:
                    combine_turn(j + 1)
                dst = pb[4 + j % 4][:, 0:D]
                if j >= 4:
                    pe.wait_ge(s_o, j - 3)
                for c in range(C):
                    pe.matmul(dst, AOT[:, c, P * j:P * j + P], projT[:, c], start=(c == 0), stop=False)
                pe.wait_ge(s_cc, j + 1)
                for g in range(GR):
                    ins = pe.matmul(dst, CT[:, j % 2, g], YE[:, g], start=False, stop=(g == GR - 1))
                ins.then_inc(s_fo, 1)

        @block.vector
        def _(dve):
            steps = [0]

            def step(ins):
                ins.then_inc(s_dv, 1)
                steps[0] += 1
                dve.wait_ge(s_dv, steps[0])

            for b in range(B):
                dve.wait_ge(s_x[b], 16)
                for j in (2 * b, 2 * b + 1):
                    nc.vector.bn_stats(stats[:, j], X[:, j]).then_inc(s_st, 1)
                dve.wait_ge(s_st, 2 * b + 2)
                nc.vector.bn_aggr(mv[:, 2 * b], stats[:, 2 * b])
                step(nc.vector.bn_aggr(mv[:, 2 * b + 1], stats[:, 2 * b + 1]))
                nc.vector.tensor_scalar(mv[:, 2 * b:2 * b + 2, 1], mv[:, 2 * b:2 * b + 2, 1], EPS, None,
                                        ALU.add).then_inc(s_var, 1)
                dve.wait_ge(s_std, b + 1)
                step(nc.vector.reciprocal(rstd[:, 2 * b:2 * b + 2], rstd[:, 2 * b:2 * b + 2]))
                for j in (2 * b, 2 * b + 1):
                    nc.vector.tensor_scalar(XN[:, j], X[:, j], mv[:, j, 0:1], rstd[:, j:j + 1],
                                            ALU.subtract, ALU.mult).then_inc(s_xn, 1)

            def w_low(n, raw):
                if n >= 2:
                    dve.wait_ge(s_qf, 8 * (n - 1)) if n < 6 else dve.wait_ge(s_kf, 8 * (n - 5))
                dve.wait_ge(s_wh, n + 1)
                nc.vector.tensor_tensor(WA[:, n % 2, 1], raw, WA[:, n % 2, 0].bitcast(F32), ALU.subtract).then_inc(s_wl, 1)

            kvraw = KVR.rearrange("p a c n -> p (a c n)")
            wqraw = lambda g: WQ[:, 1024 * g:1024 * g + 1024]
            for f in range(4):
                half, c = f // 2, f % 2
                xs = slice(512 * half, 512 * half + 512)
                dve.wait_ge(s_xtc, f + 1)
                dve.wait_ge(s_xth, f + 1)
                nc.vector.tensor_tensor(XTl[:, c, xs], XT[:, c, xs], XTh[:, c, xs].bitcast(F32), ALU.subtract).then_inc(s_xtl, 1)
            w_low(0, wqraw(0))
            dve.wait_ge(s_t, 1)
            nc.vector.tensor_copy(VC[:], pb[4][:, 0:48]).then_inc(s_vc, 1)
            dve.wait_ge(s_vc, 1)
            nc.vector.tensor_scalar(bqs[:], VC[:, 0:H], SCALE, None, ALU.mult).then_inc(s_vc, 1)
            w_low(1, wqraw(1))
            dve.wait_ge(s_r, 80)
            step(nc.vector.tensor_tensor(rg[:, 0], rg[:, 0], rg[:, 1], ALU.add))
            dve.wait_ge(s_lg, 1)
            nc.vector.tensor_tensor(lg[:], pb[4][:, 0:NT * E0].rearrange("p (j e) -> p j e", j=NT),
                                    rg[:, 0:1].to_broadcast([P, NT, E0]), ALU.add).then_inc(s_lc, 1)
            dve.wait_ge(s_lc, 1)
            for j in range(NT):
                ins = nc.vector.max(top[:, j], lg[:, j])
            step(ins)
            for j in range(NT):
                ins = nc.vector.max_index(topi[:, j], top[:, j], lg[:, j])
            step(ins)
            step(nc.vector.tensor_copy(topf[:], topi[:]))
            nc.vector.tensor_tensor(p01[:, 0], top[:, :, 1], top[:, :, 0], ALU.subtract).then_inc(s_df, 1)

            def q_copy(n):
                blk, half = n // 2, n % 2
                dve.wait_ge(s_qf, n + 1)
                nc.vector.tensor_scalar(QOb[:, :, 2 * half:2 * half + 2, :, blk].rearrange("p h b t -> p b h t"),
                                        pb[n % 4][:].rearrange("p (b h t) -> p b h t", b=2, h=H),
                                        SCALE, bqs[:, blk:blk + 1], ALU.mult, ALU.add).then_inc(s_qd, 1)

            def chosen(k):
                return (iota[:, None, 0:E0].to_broadcast([P, NT, E0]), topf[:, :, k:k + 1].to_broadcast([P, NT, E0]))

            for g in range(4):
                if g >= 1 and g + 1 < 4:
                    w_low(g + 1, wqraw(g + 1))
                for n in range(8 * g + 1, 8 * g + 8, 2):
                    q_copy(n)
                if g == 0:
                    dve.wait_ge(s_ex, 1)
                    step(nc.vector.tensor_scalar(p01[:, 0], p01[:, 1], 1.0, None, ALU.add))
                    step(nc.vector.reciprocal(p01[:, 0], p01[:, 0]))
                    step(nc.vector.tensor_tensor(p01[:, 1], p01[:, 1], p01[:, 0], ALU.mult))
                    dve.wait_ge(s_const, 4)
                    for k in range(2):
                        i, t = chosen(k)
                        dst = coef if k == 0 else tmpk
                        step(nc.vector.tensor_tensor(dst[:], i, t, ALU.is_equal))
                        step(nc.vector.tensor_tensor(dst[:], dst[:], p01[:, k, :, None].to_broadcast([P, NT, E0]), ALU.mult))
                    step(nc.vector.tensor_tensor(coef[:], coef[:], tmpk[:], ALU.add))
                if g == 2:
                    for j in range(NT):
                        dve.wait_ge(s_xa, 2 * (j // 2) + 2)
                        nc.vector.tensor_tensor(
                            WXA[:, j].rearrange("p (e r) -> p e r", e=E0),
                            pb[4 + j // 2][:, 256 * (j % 2):256 * (j % 2) + 256].rearrange("p (e r) -> p e r", e=E0),
                            coef[:, j, :, None].to_broadcast([P, E0, RANK]), ALU.mult).then_inc(s_wxa, 1)

            def fill_copy(n):
                p, f = n // 8, n % 8
                dve.wait_ge(s_kf, n + 1)
                if f == 0 and p >= 2:
                    dve.wait_ge(s_S, 8 * (p - 1))
                if f == 4 and p >= 2:
                    dve.wait_ge(s_O, 8 * (p - 1))
                if f == 0 and p == 0:
                    dve.wait_ge(s_xb, NT)
                if f < 4:
                    hh, ts = f // 2, slice(512 * (f % 2), 512 * (f % 2) + 512)
                    nc.vector.tensor_scalar(KT[:, p % 2, hh, ts], pb[6 + n % 2][:], VC[:, 16 + 2 * p + hh:17 + 2 * p + hh],
                                            None, ALU.add).then_inc(s_kc, 1)
                else:
                    nc.vector.tensor_copy(V[:, p % 2, 2 * (f - 4):2 * (f - 4) + 2].rearrange("p j n -> p (j n)"),
                                          pb[6 + n % 2][:]).then_inc(s_kc, 1)

            def max_of(u):
                i = u % 2
                dve.wait_ge(s_S, u + 1)
                nc.vector.tensor_reduce(nmax[:, i, 0:1], pb[i][:, 0:128], AX, ALU.max, negate=True)
                nc.vector.tensor_reduce(nmax[:, i, 1:2], pb[i][:, 128:384], AX, ALU.max, negate=True).then_inc(s_m, 1)

            def normalise(u):
                i = u % 2
                dve.wait_ge(s_e, u + 1)
                nc.vector.reciprocal(rinv[:, i], psumr[:, i]).then_inc(s_ri, 1)
                dve.wait_ge(s_ri, u + 1)
                nc.vector.tensor_scalar(Pb[:, i, 0:128], Pb[:, i, 0:128], rinv[:, i, 0:1], None, ALU.mult)
                nc.vector.tensor_scalar(Pb[:, i, 128:384], Pb[:, i, 128:384], rinv[:, i, 1:2], None, ALU.mult).then_inc(s_p, 1)

            w_low(4, kvraw)
            dve.wait_ge(s_kv, 64)
            w_low(5, kvraw)
            for n in range(AHEAD):
                fill_copy(n)
                if n == 7:
                    w_low(6, kvraw)
            max_of(0)
            max_of(1)
            normalise(0)
            normalise(1)
            for u in range(UNITS):
                if u + 2 < UNITS:
                    max_of(u + 2)
                if u + AHEAD < UNITS:
                    fill_copy(u + AHEAD)
                if u + 2 < UNITS:
                    normalise(u + 2)
                if u % 8 == 6 and u // 8 + 3 < PAIRS:
                    w_low(4 + u // 8 + 3, kvraw)
            for j in range(NT):
                dve.wait_ge(s_y, j + 1)
                dve.wait_ge(s_xb, j + 1)
                nc.vector.tensor_tensor(X[:, j], pb[j][:, 0:256], X[:, j], ALU.add).then_inc(s_x1, 1)
                if stop_after_l0:
                    continue
                dve.wait_ge(s_x1, j + 1)
                step(nc.vector.bn_stats(stats[:, j], X[:, j]))
                step(nc.vector.bn_aggr(mv[:, j], stats[:, j]))
                nc.vector.tensor_scalar(mv[:, j, 1:2], mv[:, j, 1:2], EPS, None, ALU.add).then_inc(s_va2, 1)
                dve.wait_ge(s_sd2, j + 1)
                step(nc.vector.reciprocal(rstd[:, j:j + 1], rstd[:, j:j + 1]))
                nc.vector.tensor_scalar(XN2[:, j], X[:, j], mv[:, j, 0:1], rstd[:, j:j + 1], ALU.subtract, ALU.mult).then_inc(s_xn2, 1)
                dve.wait_ge(s_xr, j + 1)
                nc.vector.tensor_tensor(XRl[:, j], XN2[:, j], XRh[:, j].bitcast(F32), ALU.subtract).then_inc(s_xrl, 1)
            if stop_after_l0:
                return
            def g_low(m):
                dve.wait_ge(s_gh, m + 1)
                nc.vector.tensor_tensor(SG[:, m % 2, 1].rearrange("p a c n -> p (a c) n"),
                                        SGR[:, :, :, P * m:P * m + P].rearrange("p a c n -> p (a c) n"),
                                        SG[:, m % 2, 0].bitcast(F32).rearrange("p a c n -> p (a c) n"), ALU.subtract).then_inc(s_gl, 1)

            for f in range(4):
                xs = slice(512 * (f // 2), 512 * (f // 2) + 512)
                dve.wait_ge(s_h2, f + 1)
                nc.vector.tensor_tensor(XTl[:, f % 2, xs], XT[:, f % 2, xs], XTh[:, f % 2, xs].bitcast(F32), ALU.subtract).then_inc(s_l2, 1)
            g_low(0)
            g_low(1)
            dve.wait_ge(s_qc, NT)
            for j in range(NT):
                ins = nc.vector.max(top1[:, j], QS[:, j, QKV:QKV + E1])
            step(ins)
            for j in range(NT):
                ins = nc.vector.max_index(topi1[:, j], top1[:, j], QS[:, j, QKV:QKV + E1])
            step(ins)
            nc.vector.tensor_copy(topf1[:], topi1[:])
            nc.vector.tensor_tensor(w4[:], top1[:, :, 0:K1], top1[:, :, 0:1].to_broadcast([P, NT, K1]), ALU.subtract).then_inc(s_d1, 1)

            def shared_product(q):
                m, half = q // 2, q % 2
                dst = ACTT[:, m, 512 * half:512 * half + 512]
                dve.wait_ge(s_ss, q + 1)
                nc.vector.tensor_tensor(dst, dst, pb[2 * half + 1][:], ALU.mult).then_inc(s_sm, 1)

            dve.wait_ge(s_e1, 2)
            step(nc.vector.tensor_reduce(ws[:], w4[:], AX, ALU.add))
            step(nc.vector.reciprocal(ws[:], ws[:]))
            step(nc.vector.tensor_tensor(w4[:], w4[:], ws[:, :, None].to_broadcast([P, NT, K1]), ALU.mult))
            step(nc.vector.tensor_scalar(sig[:], sig[:], 1.0, None, ALU.add))
            step(nc.vector.reciprocal(sig[:], sig[:]))
            full = [P, NT, E1]
            for k in range(K1):
                one = sel if k == 0 else tmp1
                step(nc.vector.tensor_tensor(one[:], iota[:, None, :].to_broadcast(full),
                                             topf1[:, :, k:k + 1].to_broadcast(full), ALU.is_equal))
                if k == 0:
                    step(nc.vector.tensor_tensor(wsel[:], one[:], w4[:, :, k:k + 1].to_broadcast(full), ALU.mult))
                else:
                    step(nc.vector.tensor_tensor(sel[:], sel[:], one[:], ALU.add))
                    step(nc.vector.tensor_tensor(one[:], one[:], w4[:, :, k:k + 1].to_broadcast(full), ALU.mult))
                    step(nc.vector.tensor_tensor(wsel[:], wsel[:], one[:], ALU.add))
            nc.vector.tensor_copy(selb[:], sel[:]).then_inc(s_sel, 1)
            for q in range(4):
                shared_product(q)
                if q % 2:
                    g_low(q // 2 + 2)
            dve.wait_ge(s_po, 1)
            step(nc.vector.tensor_tensor(posm[:], pb[4][:, 0:NT * E1].rearrange("p (j e) -> p j e", j=NT), sel[:], ALU.mult))
            step(nc.vector.tensor_scalar(posm[:], posm[:], -1.0, None, ALU.add))

            def slots_of(j, dst):
                return nc.vector.tensor_tensor(dst.rearrange("p (e c) -> p e c", e=E1),
                                               posm[:, j, :, None].to_broadcast([P, E1, CAP]),
                                               iota[:, None, :].to_broadcast([P, E1, CAP]), ALU.is_equal)

            slots_of(0, DM[:, 0]).then_inc(s_dm, 1)
            slots_of(1, DM[:, 1]).then_inc(s_dm, 1)
            shared_product(4)
            shared_product(5)
            for j in range(2, NT):
                dve.wait_ge(s_di, j - 1)
                slots_of(j, DM[:, j % 2]).then_inc(s_dm, 1)
            g_low(4)
            step(nc.vector.memset(region(30720, 512), MASKED))

            def attn_scores(f, k):
                kk = QS[:, 2 * k + f, 0:QKV].rearrange("p (g n) -> p g n", g=G1)[:, :, None, GW - 2 * D1:GW - D1].to_broadcast([P, G1, 4, D1])
                for i in range(k, 4):
                    q = QS[:, 2 * i + f, 0:QKV].rearrange("p (g n) -> p g n", g=G1)[:, :, 0:4 * D1].rearrange("p g (r d) -> p g r d", r=4)
                    ins = nc.vector.tensor_tensor(PR[:, i].rearrange("p (g r d) -> p g r d", g=G1, r=4), q, kk, ALU.mult)
                step(ins)
                step(nc.vector.tensor_reduce(SC[:, f, k:4, :, k], PR[:, k:4].rearrange("p i (h d) -> p i h d", h=H1), AX, ALU.add))

            for g in range(GR):
                dve.wait_ge(s_es, g + 1)
                nc.vector.tensor_tensor(HE[:, g % 2], HE[:, g % 2], pb[4 + g % 2][:, F1:2 * F1], ALU.mult).then_inc(s_eh, 1)
                if g < 6:
                    shared_product(6 + g)
                if g == 1:
                    g_low(5)
                attn_scores(g // 4, g % 4)
                if g >= 1:
                    dve.wait_ge(s_dn, g)
                    nc.vector.tensor_copy(YE[:, g - 1], pb[7][:, 0:D]).then_inc(s_ye, 1)
            for f in range(2):
                fs = slice(64 * f, 64 * f + 64)
                step(nc.vector.tensor_reduce(mx1[:, fs], SCf[:, fs], AX, ALU.max))
                nc.vector.tensor_tensor(SCf[:, fs], SCf[:, fs], mx1[:, fs, None].to_broadcast([P, 64, 4]), ALU.subtract).then_inc(s_am, 1)
            dve.wait_ge(s_dn, GR)
            nc.vector.tensor_copy(YE[:, GR - 1], pb[7][:, 0:D]).then_inc(s_ye, 1)
            for f in range(2):
                fs = slice(64 * f, 64 * f + 64)
                dve.wait_ge(s_ae, f + 1)
                step(nc.vector.tensor_reduce(mx1[:, fs], SCf[:, fs], AX, ALU.add))
                step(nc.vector.reciprocal(mx1[:, fs], mx1[:, fs]))
                nc.vector.tensor_tensor(SCf[:, fs], SCf[:, fs], mx1[:, fs, None].to_broadcast([P, 64, 4]), ALU.mult).then_inc(s_ap, 1)
            for j in range(NT):
                dve.wait_ge(s_sh, j + 1)
                nc.vector.scalar_tensor_tensor(out=X[:, j], in0=pb[j % 4][:, 0:D], scalar=sig[:, j:j + 1], in1=X[:, j],
                                               op0=ALU.mult, op1=ALU.add).then_inc(s_x2, 1)

            def combine_weights(j):
                if j >= 2:
                    dve.wait_ge(s_ct, j - 1)
                dst = CM[:, j % 2]
                slots_of(j, dst).then_inc(s_cm, 1)
                dve.wait_ge(s_cm, 2 * j + 1)
                v = dst.rearrange("p (e c) -> p e c", e=E1)
                nc.vector.tensor_tensor(v, v, wsel[:, j, :, None].to_broadcast([P, E1, CAP]), ALU.mult).then_inc(s_cm, 1)

            dve.wait_ge(s_sh, NT)
            dve.wait_ge(s_x2, NT)
            combine_weights(0)
            for j in range(NT):
                if j + 1 < NT:
                    combine_weights(j + 1)
                dve.wait_ge(s_fo, j + 1)
                nc.vector.tensor_tensor(X[:, j], pb[4 + j % 4][:, 0:D], X[:, j], ALU.add).then_inc(s_o, 1)


_INS = ['L0_attn_x', 'L0_attn_Wq', 'L0_attn_bq', 'L0_attn_Wk', 'L0_attn_bk', 'L0_attn_Wv', 'L0_attn_bv', 'L0_attn_Wo',
        'L0_attn_bo', 'L0_ffn_W', 'L0_ffn_bias', 'L0_ffn_rw1', 'L0_ffn_rb1', 'L0_ffn_rw2', 'L0_ffn_rb2', 'L0_ffn_A',
        'L0_ffn_B', 'L0_ffn_gates', 'L1_attn_weight_qkv', 'L1_attn_weight_proj', 'L1_ffn_Wr', 'L1_ffn_Wg', 'L1_ffn_Wu',
        'L1_ffn_Wd', 'L1_ffn_Wsg', 'L1_ffn_Wsu', 'L1_ffn_Wsd', 'L1_ffn_Wse']


def kernel(**inputs):
    import numpy as np
    from concourse import bacc
    from concourse.bass_utils import run_bass_kernel_spmd

    nc = bacc.Bacc("TRN2", target_bir_lowering=False, num_devices=1, dynamic_dma_scratch_size=64)
    arrays, aps = {}, {}
    for name in _INS:
        v = np.ascontiguousarray(inputs[name])
        arrays[f"in_{name}"] = v
        aps[name] = nc.dram_tensor(f"in_{name}", v.shape, mybir.dt.from_np(v.dtype), kind="ExternalInput").ap()
    out = nc.dram_tensor("out", (B, T, D), F32, kind="ExternalOutput").ap()
    program(nc, aps, out)
    r = run_bass_kernel_spmd(nc, [arrays], core_ids=[0])
    return r.results[0]["out"]
```

```python
from contextlib import ExitStack

import concourse.bass as bass
from concourse import mybir

F32 = mybir.dt.float32
FR = mybir.dt.float32r
BF16 = mybir.dt.bfloat16
U32 = mybir.dt.uint32
ALU = mybir.AluOpType
ACT = mybir.ActivationFunctionType
AX = mybir.AxisListType.X

P = 128
B, T, D = 4, 256, 256
N = B * T
NT = N // P
C = D // P
H, DH = 16, 128
SCALE = float(DH) ** -0.5
PAIRS = H // 2
UNITS = H * B
WO_AT = [16, 19, 22, 26, 55, 57, 59, 61]
AHEAD = 11
E0, RANK, HID = 16, 16, 64
H1, D1, G1 = 16, 16, 4
SCALE1 = float(D1) ** -0.5
GW = (H1 // G1 + 2) * D1
QKV = G1 * GW
E1, K1, CAP = 32, 4, 32
F1, FS = 176, 704
FC = 6
FP = FC * P
SLOTS = E1 * CAP
GR = SLOTS // P
EPG = E1 // GR
EPS = 1e-5
MASKED = -1.0e30


def program(nc, a, out, stop_after_l0=False):
    ctx = ExitStack()
    with ctx:
        def sb(name, shape, dt=F32):
            return ctx.enter_context(nc.sbuf_tensor(name, shape, dt))

        def sem(name):
            return ctx.enter_context(nc.semaphore(name))

        pb = [ctx.enter_context(nc.psum_tensor(f"bank{i}", [P, 512], F32)) for i in range(8)]

        ident = sb("ident", [P, P])
        identb = sb("identb", [P, P], BF16)
        maskb = sb("maskb", [P, P], BF16)
        trib = sb("trib", [P, P], BF16)
        onesb = sb("onesb", [P, P], BF16)
        iota = sb("iota", [P, 32])

        X = sb("X", [P, NT, D])
        XT = sb("XT", [P, C, N])
        XTh = sb("XTh", [P, C, N], FR)
        XTl = sb("XTl", [P, C, N], FR)
        stats = sb("stats", [P, NT, 6])
        mv = sb("mv", [P, NT, 2])
        rstd = sb("rstd", [P, NT])

        WA = sb("WA", [P, 2, 2, 1024], FR)

        at0 = nc.sbuf_base
        arena = sb("arena", [P, 35840])

        def region(at, words):
            return arena[:, at:at + words]

        QO = region(0, 16384).rearrange("p (h b t) -> p h b t", h=H, b=B)
        QOb = region(0, 16384).rearrange("p (h b t k) -> p h b t k", h=H, b=B, k=16)
        WQ = region(16384, 4096)
        WQv = WQ.rearrange("p (g c n) -> p g c n", g=4, c=C)
        WOv = WQ.rearrange("p (h n) -> p h n", h=H)
        KVR = region(31744, 1024).rearrange("p (a c n) -> p a c n", a=2, c=C)
        KTf = region(20480, 4096)
        KT = KTf.rearrange("p (a h n) -> p a h n", a=2, h=2)
        XN = KTf[:, 0:2048].rearrange("p (j d) -> p j d", j=NT)
        WXA = KTf[:, 2048:4096].rearrange("p (j d) -> p j d", j=NT)
        Vf = region(24576, 4096)
        V = Vf.rearrange("p (a j n) -> p a j n", a=2, j=NT)
        stW = Vf[:, 0:512].rearrange("p (o i) -> p o i", o=2)
        stA = Vf[:, 512:1024].rearrange("p (o i) -> p o i", o=2)
        stB = Vf[:, 1024:1536].rearrange("p (o e r) -> p o e r", o=2, e=E0)
        stBf = Vf[:, 1024:1536].rearrange("p (o i) -> p o i", o=2)
        stQKV = Vf[:, 1536:2304].rearrange("p (o i) -> p o i", o=3)
        stP = Vf[:, 2304:2816].rearrange("p (o i) -> p o i", o=2)
        stR1 = Vf[0:HID, 2816:3072]
        stR2 = Vf[0:E0, 3072:3136]
        VB = Vf[0:48, 3136:3264]
        bo2 = Vf[:, 3264:3776].rearrange("p (o i) -> p o i", o=2)
        Pb = region(28672, 768).rearrange("p (i n) -> p i n", i=2)
        PTb = region(29440, 768).rearrange("p (i n) -> p i n", i=2)
        nmax = sb("nmax", [P, 2, 2])
        psumr = sb("psumr", [P, 2, 2])
        rinv = sb("rinv", [P, 2, 2])
        WT, AT, B2 = (region(30208 + 512 * i, 512).rearrange("p (c n) -> p c n", c=C) for i in range(3))
        QW = sb("QW", [P, C, QKV + E1 + 1])
        projT = sb("projT", [P, C, D])
        R1T = sb("R1T", [P, C, P])
        R2T = sb("R2T", [P, E0])
        rb1c = sb("rb1c", [P, 1])
        VC = sb("VC", [P, 48])
        bqs = sb("bqs", [P, H])
        rg = sb("rg", [P, 2, E0])
        HT = region(32768, N)
        lg = sb("lg", [P, NT, E0])
        top = sb("top", [P, NT, 8])
        topi = sb("topi", [P, NT, 8], U32)
        topf = sb("topf", [P, NT, 8])
        tmpk = sb("tmpk", [P, NT, E0])
        coef = sb("coef", [P, NT, E0])
        p01 = sb("p01", [P, 3, NT])
        WXT = region(33792, 2048).rearrange("p (c n) -> p c n", c=C)

        FRX = sb("FRX", [P, 4096], FR)
        WOP = [w.rearrange("p (s h n) -> p s h n", s=2, h=H // 2)
               for w in (FRX[:], WA[:].rearrange("p a s n -> p (a s n)"))]
        OS = nc.alloc_sbuf_tensor_at("OS", [P, 4, 2, H // 2, P], FR, offset=at0 + 4 * 20480)

        EW = [region(4864 * i, 4864) for i in range(2)]
        WGU = [w[:, 0:2816].rearrange("p (e c n) -> p e c n", e=EPG, c=C) for w in EW]
        WD = [w[:, 2816:4864].rearrange("p (e c n) -> p e c n", e=EPG, c=2) for w in EW]
        ACTT = region(9728, FC * N).rearrange("p (m n) -> p m n", m=FC)
        G = region(0, 8192).rearrange("p (j k n) -> p j k n", j=NT, k=K1)
        HTE = region(15872, 512).rearrange("p (i k n) -> p i k n", i=2, k=2)
        QS = region(16384, 3360).rearrange("p (j n) -> p j n", j=NT)
        HE = region(19744, 352).rearrange("p (i n) -> p i n", i=2)
        SGR = region(20480, 3072).rearrange("p (a c n) -> p a c n", a=2, c=C)
        PR = region(23552, 1024).rearrange("p (i n) -> p i n", i=4)
        SD = region(24576, 1536).rearrange("p (m n) -> p m n", m=FC)
        AOT = region(26112, 2048).rearrange("p (c n) -> p c n", c=C)
        XE = region(28672, 2048).rearrange("p (c n) -> p c n", c=C)
        SC = region(30720, 512).rearrange("p (f i h j) -> p f i h j", f=2, i=4, h=H1)
        SCf = region(30720, 512).rearrange("p (x j) -> p x j", j=4)
        XN2 = region(31744, 2048).rearrange("p (j n) -> p j n", j=NT)
        AO = XN2
        YE = region(33792, 2048).rearrange("p (g n) -> p g n", g=GR)
        XRh, XRl = (WA[:, i].rearrange("p a n -> p (a n)").rearrange("p (j n) -> p j n", j=NT) for i in range(2))
        SG = FRX[:, 0:2048].rearrange("p (i s a c n) -> p i s a c n", i=2, s=2, a=2, c=C)
        DM = FRX[:, 2048:4096].rearrange("p (i n) -> p i n", i=2)
        selb = sb("selb", [P, NT, E1], BF16)
        sel = sb("sel", [P, NT, E1])
        tmp1 = sb("tmp1", [P, NT, E1])
        posm = sb("posm", [P, NT, E1])
        top1 = sb("top1", [P, NT, 8])
        topi1 = sb("topi1", [P, NT, 8], U32)
        topf1 = sb("topf1", [P, NT, 8])
        w4 = sb("w4", [P, NT, K1])
        pk = sb("pk", [P, NT, K1])
        ok = sb("ok", [P, NT, K1])
        idx = sb("idx", [P, NT, K1], U32)
        rows = nc.dram_tensor("expert_rows", (SLOTS, D), F32, kind="Internal").ap()
        ws = sb("ws", [P, NT])
        sig = sb("sig", [P, NT])
        mx1 = sb("mx1", [P, 128])
        pvt = sb("pvt", [P, 256])

        s_x = [sem(f"x_loaded{b}") for b in range(B)]
        s_vb = sem("bias_vectors_loaded")
        s_r = sem("router_weights_loaded")
        s_wq = [sem(f"wq_loaded{g}") for g in range(4)]
        s_sw = sem("small_weights_loaded")
        s_bo = sem("output_biases_loaded")
        s_kv = sem("kv_weights_loaded")
        s_wo = sem("wo_loaded")
        s_pool = sem("pool_step_done")
        s_const = sem("constants_ready")
        s_pad = sem("padding_ready")
        s_st = sem("ln_stats_done")
        s_var = sem("var_ready")
        s_std = sem("std_ready")
        s_rs = sem("rstd_ready")
        s_xn = sem("xn_ready")
        s_xb = sem("x_biased")
        s_xt = sem("xn_transposed")
        s_xtc = sem("xt_copied")
        s_xth = sem("xt_high_ready")
        s_xtl = sem("xt_low_ready")
        s_t = sem("weights_transposed")
        s_tc = sem("transposed_weights_copied")
        s_vc = sem("bias_columns_ready")
        s_wh = sem("weight_high_ready")
        s_wl = sem("weight_low_ready")
        s_qf = sem("q_filled")
        s_qa = sem("q_copied_by_act")
        s_qd = sem("q_copied_by_dve")
        s_ht = sem("router_hidden_done")
        s_hs = sem("router_silu_done")
        s_lg = sem("router_logits_done")
        s_lc = sem("router_logits_copied")
        s_dv = sem("dve_step_done")
        s_ex = sem("router_exp_done")
        s_df = sem("router_difference_ready")
        s_xa = sem("xa_done")
        s_wxa = sem("xa_weighted")
        s_wxt = sem("xa_transposed")
        s_wxc = sem("xa_transposed_copied")
        s_kf = sem("kv_filled")
        s_kc = sem("kv_copied")
        s_S = sem("scores_ready")
        s_m = sem("max_ready")
        s_e = sem("exp_ready")
        s_ri = sem("rinv_ready")
        s_p = sem("probs_ready")
        s_T = sem("probs_transposed")
        s_Tc = sem("probs_transposed_copied")
        s_O = sem("heads_ready")
        s_Oc = sem("heads_copied")
        s_x1 = sem("x1_ready")
        s_pd = sem("l1_padding_ready")
        s_pe = sem("expert_padding_ready")
        s_sg = sem("shared_up_weights_loaded")
        s_sd = sem("shared_down_weights_loaded")
        s_ew = [sem(f"expert_weights_loaded{i}") for i in range(2)]
        s_va2 = sem("var2_ready")
        s_sd2 = sem("std2_ready")
        s_xn2 = sem("xn2_ready")
        s_xr = sem("xn2_high_ready")
        s_xrl = sem("xn2_low_ready")
        s_t2 = sem("xn2_transposed")
        s_c2 = sem("xn2_transpose_copied")
        s_h2 = sem("xn2_transpose_high_ready")
        s_l2 = sem("xn2_transpose_low_ready")
        s_qk = sem("qkv_done")
        s_qc = sem("qkv_copied")
        s_gh = sem("shared_weight_high_ready")
        s_gl = sem("shared_weight_low_ready")
        s_sf = sem("shared_filled")
        s_ss = sem("shared_silu_done")
        s_sm = sem("shared_product_done")
        s_d1 = sem("gate_logit_differences_ready")
        s_e1 = sem("gate_exp_done")
        s_sel = sem("selection_ready")
        s_po = sem("positions_done")
        s_dm = sem("dispatch_mask_ready")
        s_di = sem("dispatched_tile")
        s_xe = sem("slots_copied")
        s_up = sem("expert_up_done")
        s_es = sem("expert_silu_done")
        s_eh = sem("expert_hidden_ready")
        s_et = sem("expert_hidden_transposed")
        s_ec = sem("expert_hidden_copied")
        s_dn = sem("expert_down_done")
        s_ye = sem("expert_output_copied")
        s_sh = sem("shared_down_done")
        s_x2 = sem("shared_added")
        s_am = sem("attn1_scores_less_max")
        s_ae = sem("attn1_exp_done")
        s_ap = sem("attn1_probs_ready")
        s_pv = sem("attn1_step_done")
        s_ao = sem("attn1_tile_ready")
        s_at = sem("attn1_transposed")
        s_ac = sem("attn1_transposed_copied")
        s_woh = sem("wo_high_ready")
        s_wol = sem("wo_low_ready")
        s_oh = sem("heads_high_ready")
        s_ol = sem("heads_low_ready")
        s_yh = sem("l0_out_half_done")
        s_ix = sem("slot_indices_ready")
        s_er = sem("expert_rows_stored")
        s_g = [sem(f"rows_gathered{j}") for j in range(NT)]
        s_fo = sem("attn1_projected")
        s_pa = sem("attn1_added")
        s_o = sem("out_ready")
        s_out = sem("out_stored")

        block = ctx.enter_context(nc.Block())

        x_t = a["L0_attn_x"].rearrange("b (q p) d -> p b q d", p=P)
        out_t = out.rearrange("b (q p) d -> p (b q) d", p=P)
        wq_t = a["L0_attn_Wq"].rearrange("(c p) n -> p c n", p=P)
        wk_t = a["L0_attn_Wk"].rearrange("(c p) n -> p c n", p=P)
        wv_t = a["L0_attn_Wv"].rearrange("(c p) n -> p c n", p=P)
        two = lambda w: w.rearrange("(o p) i -> p o i", p=P)
        row = lambda v, k: v.rearrange("(h d) -> h d", h=k)

        def unit(u):
            p, hh, b = u // 8, u // 4 % 2, u % 4
            return p, hh, b, 2 * p + hh

        @block.sync
        def _(sp):
            for b in range(B):
                sp.dma_start(X[:, 2 * b:2 * b + 2, :], x_t[:, b]).then_inc(s_x[b], 16)
            sp.dma_start(WQv[:, 0], wq_t[:, :, 0:512]).then_inc(s_wq[0], 16)
            for i, n in enumerate(("bq", "bk", "bv")):
                sp.dma_start(VB[16 * i:16 * i + 16, :], row(a["L0_attn_" + n], H)).then_inc(s_vb, 16)
            sp.dma_start(stR1, a["L0_ffn_rw1"]).then_inc(s_r, 16)
            sp.dma_start(stR2, a["L0_ffn_rw2"][0:E0, :]).then_inc(s_r, 16)
            sp.wait_ge(s_pad, 3)
            sp.dma_start(rb1c[0:HID, :], a["L0_ffn_rb1"].rearrange("(p a) -> p a", a=1)).then_inc(s_r, 16)
            sp.dma_start(rg[:, 0], a["L0_ffn_rb2"][0:E0].partition_broadcast(P)).then_inc(s_r, 16)
            sp.dma_start(rg[:, 1], a["L0_ffn_gates"].partition_broadcast(P)).then_inc(s_r, 16)
            sp.dma_start(WQv[:, 1], wq_t[:, :, 512:1024]).then_inc(s_wq[1], 16)
            sp.dma_start(stW, two(a["L0_ffn_W"])).then_inc(s_sw, 16)
            sp.dma_start(stA, a["L0_ffn_A"].rearrange("(o e) r i -> (e r) o i", o=2)).then_inc(s_sw, 16)
            for o in range(2):
                sp.dma_start(stB[:, o], a["L0_ffn_B"][:, P * o:P * o + P, :].rearrange("e p r -> p e r")).then_inc(s_sw, 16)
            sp.dma_start(stQKV, two(a["L1_attn_weight_qkv"])).then_inc(s_sw, 16)
            sp.dma_start(stP, two(a["L1_attn_weight_proj"])).then_inc(s_sw, 16)
            sp.dma_start(bo2[:, 0], a["L0_attn_bo"].partition_broadcast(P)).then_inc(s_bo, 16)
            sp.dma_start(bo2[:, 1], a["L0_ffn_bias"].partition_broadcast(P)).then_inc(s_bo, 16)
            for g in (2, 3):
                sp.dma_start(WQv[:, g], wq_t[:, :, 512 * g:512 * g + 512]).then_inc(s_wq[g], 16)

            for c in range(C):
                sp.dma_start(QW[:, c, QKV:QKV + E1], a["L1_ffn_Wr"][P * c:P * c + P, :]).then_inc(s_bo, 16)
                sp.dma_start(QW[:, c, QKV + E1:QKV + E1 + 1], a["L1_ffn_Wse"][P * c:P * c + P, :]).then_inc(s_bo, 16)

            def load_kv(p):
                sp.dma_start(KVR[:, 0], wk_t[:, :, 256 * p:256 * p + 256]).then_inc(s_kv, 16)
                sp.dma_start(KVR[:, 1], wv_t[:, :, 256 * p:256 * p + 256]).then_inc(s_kv, 16)

            load_kv(0)
            sp.wait_ge(s_wl, 4)
            sp.dma_start(WOv, a["L0_attn_Wo"].rearrange("(h d) n -> d h n", d=P)).then_inc(s_wo, 16)
            for p in range(1, PAIRS):
                sp.wait_ge(s_wl, 4 + p)
                load_kv(p)
            if stop_after_l0:
                sp.wait_ge(s_x1, NT)
                sp.dma_start(out_t, X[:]).then_inc(s_out, 16)
                sp.wait_ge(s_out, 16)
                return
            sp.wait_ge(s_pd, 2)
            for i, n in enumerate(("Wsg", "Wsu")):
                sp.dma_start(SGR[:, i, :, 0:FS], a["L1_ffn_" + n].rearrange("(c p) n -> p c n", p=P)).then_inc(s_sg, 16)
            sp.dma_start(SD[:, 0:FC - 1], a["L1_ffn_Wsd"][0:P * (FC - 1), :].rearrange("(m p) n -> p m n", p=P)).then_inc(s_sd, 16)
            sp.dma_start(SD[0:FS - P * (FC - 1), FC - 1], a["L1_ffn_Wsd"][P * (FC - 1):FS, :]).then_inc(s_sd, 16)
            sp.wait_ge(s_pe, 3)

            def store_rows(g):
                sp.wait_ge(s_ye, g + 1)
                sp.dma_start(rows[P * g:P * g + P], YE[:, g]).then_inc(s_er, 16)

            for g in range(GR):
                e, i = slice(EPG * g, EPG * g + EPG), g % 2
                if g >= 2:
                    sp.wait_ge(s_dn, g - 1)
                for k, n in enumerate(("Wg", "Wu")):
                    sp.dma_start(WGU[i][:, :, :, F1 * k:F1 * k + F1],
                                 a["L1_ffn_" + n][e].rearrange("e (c p) n -> p e c n", p=P)).then_inc(s_ew[i], 16)
                sp.dma_start(WD[i][:, :, 0], a["L1_ffn_Wd"][e, 0:P].rearrange("e p n -> p e n")).then_inc(s_ew[i], 16)
                sp.dma_start(WD[i][0:F1 - P, :, 1], a["L1_ffn_Wd"][e, P:F1].rearrange("e p n -> p e n")).then_inc(s_ew[i], 16)
                if g >= 2:
                    store_rows(g - 2)
            store_rows(GR - 2)
            store_rows(GR - 1)
            for j in range(NT):
                sp.wait_ge(s_o, j + 1)
                sp.dma_start(out_t[:, j], X[:, j]).then_inc(s_out, 16)
            sp.wait_ge(s_out, 16 * NT)

        @block.gpsimd
        def _(pool):
            steps = [0]

            def step(ins):
                ins.then_inc(s_pool, 1)
                steps[0] += 1
                pool.wait_ge(s_pool, steps[0])

            step(pool.memset(ident[:], 0.0))
            pool.affine_select(out=ident[:], in_=ident[:], compare_op=ALU.not_equal, fill=1.0, base=0,
                               pattern=[[-1, P]], channel_multiplier=1).then_inc(s_const, 1)
            pool.memset(R1T[:], 0.0).then_inc(s_pad, 1)
            pool.memset(R2T[:], 0.0).then_inc(s_pad, 1)
            pool.memset(rb1c[:], 0.0).then_inc(s_pad, 1)
            pool.wait_ge(s_const, 1)
            pool.tensor_copy(identb[:], ident[:]).then_inc(s_const, 1)
            step(pool.memset(maskb[:], 0.0))
            pool.affine_select(out=maskb[:], in_=maskb[:], compare_op=ALU.is_ge, fill=MASKED, base=0,
                               pattern=[[-1, P]], channel_multiplier=1).then_inc(s_const, 1)
            pool.iota(iota[:], [[1, 32]], base=0, channel_multiplier=0,
                      allow_small_or_imprecise_dtypes=True).then_inc(s_const, 1)
            pool.memset(onesb[:], 1.0).then_inc(s_const, 1)
            pool.wait_ge(s_const, 5)
            pool.affine_select(out=trib[:], in_=onesb[:], compare_op=ALU.is_ge, fill=0.0, base=0,
                               pattern=[[1, P]], channel_multiplier=-1).then_inc(s_const, 1)
            pool.wait_ge(s_bo, 96)
            step(pool.tensor_tensor(bo2[:, 0], bo2[:, 0], bo2[:, 1], ALU.add))
            for j in range(NT):
                pool.wait_ge(s_xn, j + 1)
                pool.tensor_tensor(X[:, j], X[:, j], bo2[:, 0], ALU.add).then_inc(s_xb, 1)
            if stop_after_l0:
                return
            pool.wait_ge(s_yh, 2 * NT)
            pool.memset(SGR[:, :, :, FS:FP], 0.0).then_inc(s_pd, 1)
            pool.memset(SD[:, FC - 1], 0.0).then_inc(s_pd, 1)
            for i in range(2):
                pool.memset(WD[i][:, :, 1], 0.0).then_inc(s_pe, 1)
            pool.memset(HTE, 0.0).then_inc(s_pe, 1)
            chain = 0
            for f in range(2):
                pool.wait_ge(s_ap, 1)
                for i in range(4):
                    j = 2 * i + f
                    for k in range(i + 1):
                        v = QS[:, 2 * k + f, 0:QKV].rearrange("p (g n) -> p g n", g=G1)[:, :, None, GW - D1:GW].to_broadcast([P, G1, 4, D1])
                        p = SC[:, f, i, :, k].rearrange("p (g r) -> p g r", g=G1)[:, :, :, None].to_broadcast([P, G1, 4, D1])
                        dst = AO[:, j] if k == 0 else pvt[:]
                        pool.tensor_tensor(dst.rearrange("p (g r d) -> p g r d", g=G1, r=4), p, v, ALU.mult).then_inc(s_pv, 1)
                        chain += 1
                        pool.wait_ge(s_pv, chain)
                        if k:
                            pool.tensor_tensor(AO[:, j], AO[:, j], pvt[:], ALU.add).then_inc(s_pv, 1)
                            chain += 1
                            pool.wait_ge(s_pv, chain)
            pool.wait_ge(s_ix, 1)
            pool.wait_ge(s_dn, GR)
            pool.wait_ge(s_er, 16 * GR)
            for j in range(NT):
                for k in range(K1):
                    pool.indirect_dma_start(G[:, j, k], None, rows, bass.IndirectOffsetOnAxis(ap=idx[:, j, k:k + 1], axis=0)).then_inc(s_g[j], 16)

        @block.scalar
        def _(act):
            for b in range(B):
                act.wait_ge(s_var, b + 1)
                nc.scalar.activation(rstd[:, 2 * b:2 * b + 2], mv[:, 2 * b:2 * b + 2, 1], ACT.Sqrt).then_inc(s_std, 1)

            def w_high(n, raw):
                if n >= 2:
                    act.wait_ge(s_qf, 8 * (n - 1)) if n < 6 else act.wait_ge(s_kf, 8 * (n - 5))
                nc.scalar.activation(WA[:, n % 2, 0], raw, ACT.Copy).then_inc(s_wh, 1)

            for f in range(4):
                half, c = f // 2, f % 2
                act.wait_ge(s_xt, f + 1)
                nc.scalar.activation(XT[:, c, 512 * half:512 * half + 512], pb[f][:], ACT.Copy).then_inc(s_xtc, 1)
                nc.scalar.activation(XTh[:, c, 512 * half:512 * half + 512], pb[f][:], ACT.Copy).then_inc(s_xth, 1)
            act.wait_ge(s_wq[0], 16)
            w_high(0, WQv[:, 0])
            act.wait_ge(s_t, 2)
            act.wait_ge(s_pad, 3)
            nc.scalar.activation(R1T[:, :, 0:HID], pb[5][:, 0:2 * HID].rearrange("p (c n) -> p c n", c=C), ACT.Copy).then_inc(s_tc, 1)
            nc.scalar.activation(R2T[0:HID, :], pb[5][0:HID, 256:256 + E0], ACT.Copy).then_inc(s_tc, 1)
            act.wait_ge(s_r, 80)
            for half in range(2):
                act.wait_ge(s_ht, half + 1)
                nc.scalar.activation(HT[:, 512 * half:512 * half + 512], pb[6 + half][:], ACT.Silu, bias=rb1c[:]).then_inc(s_hs, 1)
            act.wait_ge(s_wq[1], 16)
            w_high(1, WQv[:, 1])
            act.wait_ge(s_vc, 2)

            def q_copy(n):
                blk, half = n // 2, n % 2
                act.wait_ge(s_qf, n + 1)
                nc.scalar.activation(QOb[:, :, 2 * half:2 * half + 2, :, blk].rearrange("p h b t -> p b h t"),
                                     pb[n % 4][:].rearrange("p (b h t) -> p b h t", b=2, h=H),
                                     ACT.Identity, bias=bqs[:, blk:blk + 1], scale=SCALE).then_inc(s_qa, 1)

            def weight_copy(n, dst, src):
                act.wait_ge(s_t, n)
                nc.scalar.activation(dst, src, ACT.Copy).then_inc(s_tc, 1)

            for g in range(4):
                if g >= 1 and g + 1 < 4:
                    act.wait_ge(s_wq[g + 1], 16)
                    w_high(g + 1, WQv[:, g + 1])
                for n in range(8 * g, 8 * g + 8, 2):
                    q_copy(n)
                if g == 0:
                    act.wait_ge(s_df, 1)
                    nc.scalar.activation(p01[:, 1], p01[:, 0], ACT.Exp).then_inc(s_ex, 1)
                    for i, dst in enumerate((WT, AT, B2)):
                        weight_copy(3 + i, dst.rearrange("p c n -> p (c n)"), pb[5 + i][:])
                if g == 1:
                    weight_copy(6, QW[:, 0, 0:QKV], pb[5][:, 0:QKV])
                    weight_copy(7, QW[:, 1, 0:QKV], pb[6][:, 0:QKV])
                    weight_copy(8, projT[:].rearrange("p c n -> p (c n)"), pb[7][:])
            for f in range(4):
                act.wait_ge(s_wxt, f + 1)
                nc.scalar.activation(WXT[:, f // 2, 512 * (f % 2):512 * (f % 2) + 512], pb[f][:], ACT.Copy).then_inc(s_wxc, 1)
            for p in (0, 1, 2):
                act.wait_ge(s_kv, 32 * (p + 1))
                w_high(4 + p, KVR.rearrange("p a c n -> p (a c n)"))

            def exps(u):
                i = u % 2
                act.wait_ge(s_m, u + 1)
                if u >= 2:
                    act.wait_ge(s_T, u - 1)
                nc.scalar.activation(Pb[:, i, 0:128], pb[i][:, 0:128], ACT.Exp, bias=nmax[:, i, 0:1],
                                     accum_out=psumr[:, i, 0:1])
                nc.scalar.activation(Pb[:, i, 128:384], pb[i][:, 128:384], ACT.Exp, bias=nmax[:, i, 1:2],
                                     accum_out=psumr[:, i, 1:2]).then_inc(s_e, 1)

            def t_copy(u):
                act.wait_ge(s_T, u + 1)
                if u >= 2:
                    act.wait_ge(s_O, u - 1)
                nc.scalar.activation(PTb[:, u % 2], pb[2 + u % 2][:, 0:384], ACT.Copy).then_inc(s_Tc, 1)

            def o_copy(u):
                _, _, b, h = unit(u)
                act.wait_ge(s_O, u + 1)
                nc.scalar.activation(QO[:, h, b], pb[4 + u % 2][:, 0:256], ACT.Identity,
                                     bias=VC[:, 32 + h:33 + h]).then_inc(s_Oc, 1)

            def wo_high(n):
                if n == 0:
                    act.wait_ge(s_wo, 16)
                if n == 4:
                    act.wait_ge(s_kf, 8 * PAIRS)
                nc.scalar.activation(WOP[n // 4][:, 0, 2 * (n % 4):2 * (n % 4) + 2], WOv[:, 2 * n:2 * n + 2], ACT.Copy).then_inc(s_woh, 1)

            exps(0)
            exps(1)
            t_copy(0)
            for u in range(UNITS):
                if u >= 1:
                    o_copy(u - 1)
                if u + 2 < UNITS:
                    exps(u + 2)
                if u + 1 < UNITS:
                    t_copy(u + 1)
                if u in WO_AT:
                    wo_high(WO_AT.index(u))
                if u % 8 == 5 and u // 8 + 3 < PAIRS:
                    act.wait_ge(s_kv, 32 * (u // 8 + 4))
                    w_high(4 + u // 8 + 3, KVR.rearrange("p a c n -> p (a c n)"))
            o_copy(UNITS - 1)
            if stop_after_l0:
                return
            def o_high(n):
                j = n // 2
                if n >= 4:
                    act.wait_ge(s_yh, n - 3)
                nc.scalar.activation(OS[:, n % 4, 0], QO[:, 8 * (n % 2):8 * (n % 2) + 8, j // 2, P * (j % 2):P * (j % 2) + P],
                                     ACT.Copy).then_inc(s_oh, 1)

            def t2_copy(j):
                js = slice(P * j, P * j + P)
                act.wait_ge(s_t2, j + 1)
                src = pb[4 + j % 2][:, 0:D].rearrange("p (c n) -> p c n", c=C)
                nc.scalar.activation(XT[:, :, js], src, ACT.Copy).then_inc(s_c2, 1)
                nc.scalar.activation(XTh[:, :, js], src, ACT.Copy).then_inc(s_h2, 1)

            def q_out(j):
                act.wait_ge(s_qk, j + 1)
                nc.scalar.activation(QS[:, j, 0:QKV + E1 + 1], pb[6 + j % 2][:, 0:QKV + E1 + 1], ACT.Copy).then_inc(s_qc, 1)

            act.wait_ge(s_O, UNITS)
            act.wait_ge(s_Oc, UNITS)
            for n in range(4):
                o_high(n)
            for j in range(NT):
                if 2 * j + 4 < 2 * NT:
                    o_high(2 * j + 4)
                    o_high(2 * j + 5)
                if j >= 1:
                    t2_copy(j - 1)
                if j >= 2:
                    q_out(j - 2)
                act.wait_ge(s_va2, j + 1)
                nc.scalar.activation(rstd[:, j:j + 1], mv[:, j, 1:2], ACT.Sqrt).then_inc(s_sd2, 1)
            t2_copy(NT - 1)
            q_out(NT - 2)
            q_out(NT - 1)
            act.wait_ge(s_yh, 2 * NT)
            act.wait_ge(s_xn2, NT)
            for i in range(2):
                nc.scalar.activation(XRh[:, 4 * i:4 * i + 4], XN2[:, 4 * i:4 * i + 4], ACT.Copy).then_inc(s_xr, 1)

            def g_high(m):
                if m >= 2:
                    act.wait_ge(s_sf, 2 * (m - 1))
                nc.scalar.activation(SG[:, m % 2, 0], SGR[:, :, :, P * m:P * m + P], ACT.Copy).then_inc(s_gh, 1)

            act.wait_ge(s_sg, 32)
            g_high(0)
            g_high(1)

            def silu(q):
                m, half = q // 2, q % 2
                act.wait_ge(s_sf, q + 1)
                nc.scalar.activation(ACTT[:, m, 512 * half:512 * half + 512], pb[2 * half][:], ACT.Silu).then_inc(s_ss, 1)

            act.wait_ge(s_d1, 1)
            nc.scalar.activation(w4[:], w4[:], ACT.Exp).then_inc(s_e1, 1)
            nc.scalar.activation(sig[:], QS[:, :, QKV + E1], ACT.Exp, scale=-1.0).then_inc(s_e1, 1)
            for q in range(4):
                silu(q)
                if q % 2:
                    g_high(q // 2 + 2)
            for k in range(4):
                c, half = k // 2, k % 2
                act.wait_ge(s_di, NT)
                nc.scalar.activation(XE[:, c, 512 * half:512 * half + 512], pb[k][:], ACT.Copy).then_inc(s_xe, 1)

            def e_copy(g):
                act.wait_ge(s_et, g + 1)
                if g >= 2:
                    act.wait_ge(s_dn, g - 1)
                nc.scalar.activation(HTE[:, g % 2, 0], pb[6][:, 0:P], ACT.Copy)
                nc.scalar.activation(HTE[0:F1 - P, g % 2, 1], pb[6][0:F1 - P, P:2 * P], ACT.Copy).then_inc(s_ec, 1)

            act.wait_ge(s_pe, 3)
            for g in range(GR):
                if g >= 1:
                    e_copy(g - 1)
                silu(4 + g)
                if g in (1, 3):
                    g_high(4 + g // 2)
                act.wait_ge(s_up, g + 1)
                if g >= 2:
                    act.wait_ge(s_et, g - 1)
                nc.scalar.activation(HE[:, g % 2], pb[4 + g % 2][:, 0:F1], ACT.Silu).then_inc(s_es, 1)
                if g == 4:
                    act.wait_ge(s_am, 1)
                    nc.scalar.activation(SCf, SCf, ACT.Exp, scale=SCALE1).then_inc(s_ae, 1)
            e_copy(GR - 1)
            for f in range(4):
                act.wait_ge(s_at, f + 1)
                nc.scalar.activation(AOT[:, f // 2, 512 * (f % 2):512 * (f % 2) + 512], pb[4 + f][:], ACT.Copy).then_inc(s_ac, 1)

        @block.tensor
        def _(pe):
            def mm3(dst, wh, wl, xh, xl, start, stop):
                pe.matmul(dst, wh, xl, start=start, stop=False)
                pe.matmul(dst, wl, xh, start=False, stop=False)
                return pe.matmul(dst, wh, xh, start=False, stop=stop)

            pe.wait_ge(s_const, 1)
            for f in range(4):
                half, c = f // 2, f % 2
                for i in range(4):
                    j = 4 * half + i
                    if c == 0:
                        pe.wait_ge(s_xn, j + 1)
                    ins = pe.transpose(pb[f][:, P * i:P * i + P], XN[:, j, P * c:P * c + P], ident[:])
                ins.then_inc(s_xt, 1)
            pe.wait_ge(s_vb, 48)
            pe.transpose(pb[4][:, 0:48], VB, ident[0:48, 0:48]).then_inc(s_t, 1)
            pe.wait_ge(s_r, 80)
            for c in range(C):
                pe.transpose(pb[5][:, HID * c:HID * c + HID], stR1[:, P * c:P * c + P], ident[0:HID, 0:HID])
            pe.transpose(pb[5][0:HID, 256:256 + E0], stR2, ident[0:E0, 0:E0]).then_inc(s_t, 1)
            pe.wait_ge(s_tc, 2)
            pe.wait_ge(s_xtc, 4)
            for half in range(2):
                for c in range(C):
                    ins = pe.matmul(pb[6 + half][:], R1T[:, c], XT[:, c, 512 * half:512 * half + 512],
                                    start=(c == 0), stop=(c == C - 1))
                ins.then_inc(s_ht, 1)
            pe.wait_ge(s_hs, 2)
            pe.wait_ge(s_vc, 2)
            for j in range(NT):
                ins = pe.matmul(pb[4][:, E0 * j:E0 * j + E0], HT[:, P * j:P * j + P], R2T[:], start=True, stop=True)
            ins.then_inc(s_lg, 1)
            pe.wait_ge(s_xtl, 4)

            def square(bank, st):
                for c in range(C):
                    for o in range(2):
                        ins = pe.transpose(pb[bank][:, 256 * c + P * o:256 * c + P * o + P], st[:, o, P * c:P * c + P], ident[:])
                ins.then_inc(s_t, 1)

            for g in range(4):
                pe.wait_ge(s_wh, g + 1)
                pe.wait_ge(s_wl, g + 1)
                wh = WA[:, g % 2, 0].rearrange("p (c n) -> p c n", c=C)
                wl = WA[:, g % 2, 1].rearrange("p (c n) -> p c n", c=C)
                for n in range(8 * g, 8 * g + 8):
                    blk, half = n // 2 % 4, n % 2
                    if n >= 4:
                        pe.wait_ge(s_qa if n % 2 == 0 else s_qd, n // 2 - 1)
                    for c in range(C):
                        xs = slice(512 * half, 512 * half + 512)
                        ins = mm3(pb[n % 4][:], wh[:, c, P * blk:P * blk + P], wl[:, c, P * blk:P * blk + P],
                                  XTh[:, c, xs], XTl[:, c, xs], c == 0, c == C - 1)
                    ins.then_inc(s_qf, 1)
                if g == 0:
                    pe.wait_ge(s_sw, 96)
                    square(5, stW)
                    square(6, stA)
                    square(7, stBf)
                if g == 1:
                    pe.wait_ge(s_tc, 5)
                    for c in range(C):
                        for o in range(3):
                            ins = pe.transpose(pb[5 + c][:, P * o:P * o + P], stQKV[:, o, P * c:P * c + P], ident[:])
                        ins.then_inc(s_t, 1)
                    square(7, stP)
                if g == 2:
                    pe.wait_ge(s_tc, 8)
                    pe.wait_ge(s_lc, 1)
                    for j in range(NT):
                        for c in range(C):
                            ins = pe.matmul(pb[4 + j // 2][:, 256 * (j % 2):256 * (j % 2) + 256], XT[:, c, P * j:P * j + P],
                                            AT[:, c], start=(c == 0), stop=(c == C - 1))
                        ins.then_inc(s_xa, 1)
            pe.wait_ge(s_qa, 16)
            pe.wait_ge(s_qd, 16)
            for f in range(4):
                c, half = f // 2, f % 2
                for i in range(4):
                    j = 4 * half + i
                    if c == 0:
                        pe.wait_ge(s_wxa, j + 1)
                    ins = pe.transpose(pb[f][:, P * i:P * i + P], WXA[:, j, P * c:P * c + P], ident[:])
                ins.then_inc(s_wxt, 1)

            def fill(n):
                p, f = n // 8, n % 8
                if f == 0:
                    pe.wait_ge(s_wh, 5 + p)
                    pe.wait_ge(s_wl, 5 + p)
                if n >= 2:
                    pe.wait_ge(s_kc, n - 1)
                bank = pb[6 + n % 2]
                wh = WA[:, p % 2, 0].rearrange("p (a c n) -> p a c n", a=2, c=C)
                wl = WA[:, p % 2, 1].rearrange("p (a c n) -> p a c n", a=2, c=C)
                if f < 4:
                    hh, xs = f // 2, slice(512 * (f % 2), 512 * (f % 2) + 512)
                    for c in range(C):
                        ins = mm3(bank[:], wh[:, 0, c, P * hh:P * hh + P], wl[:, 0, c, P * hh:P * hh + P],
                                  XTh[:, c, xs], XTl[:, c, xs], c == 0, c == C - 1)
                else:
                    for i in range(2):
                        j = 2 * (f - 4) + i
                        for c in range(C):
                            ins = mm3(bank[:, 256 * i:256 * i + 256], XTh[:, c, P * j:P * j + P], XTl[:, c, P * j:P * j + P],
                                      wh[:, 1, c], wl[:, 1, c], c == 0, c == C - 1)
                ins.then_inc(s_kf, 1)

            def scores(u):
                p, hh, b, h = unit(u)
                if u % 8 == 0:
                    pe.wait_ge(s_kc, 8 * p + 8)
                if u >= 2:
                    pe.wait_ge(s_e, u - 1)
                s, k = pb[u % 2], KT[:, p % 2, hh]
                pe.matmul(s[:, 0:128], QO[:, h, b, 0:128], k[:, T * b:T * b + 128], start=True, stop=False)
                pe.matmul(s[:, 0:128], identb[:], maskb[:], start=False, stop=True)
                pe.matmul(s[:, 128:384], QO[:, h, b, 128:256], k[:, T * b:T * b + 256], start=True, stop=False)
                pe.matmul(s[:, 256:384], identb[:], maskb[:], start=False, stop=True).then_inc(s_S, 1)

            def turn(u):
                pe.wait_ge(s_p, u + 1)
                if u >= 2:
                    pe.wait_ge(s_Tc, u - 1)
                for i in range(3):
                    ins = pe.transpose(pb[2 + u % 2][:, P * i:P * i + P], Pb[:, u % 2, P * i:P * i + P], ident[:])
                ins.then_inc(s_T, 1)

            def heads(u):
                p, hh, b, h = unit(u)
                pe.wait_ge(s_Tc, u + 1)
                if u >= 2:
                    pe.wait_ge(s_Oc, u - 1)
                o = pb[4 + u % 2][:, 0:256]
                pe.matmul(o, V[:, p % 2, 2 * b, P * hh:P * hh + P], PTb[:, u % 2, 0:256], start=True, stop=False)
                pe.matmul(o[:, 128:256], V[:, p % 2, 2 * b + 1, P * hh:P * hh + P], PTb[:, u % 2, 256:384],
                          start=False, stop=True).then_inc(s_O, 1)

            for n in range(AHEAD):
                if n == 0:
                    pe.wait_ge(s_wxa, NT)
                fill(n)
            pe.wait_ge(s_wxc, 4)
            pe.wait_ge(s_const, 3)
            scores(0)
            scores(1)
            turn(0)
            for u in range(UNITS):
                if u + 2 < UNITS:
                    scores(u + 2)
                if u + 1 < UNITS:
                    turn(u + 1)
                heads(u)
                if u + AHEAD < UNITS:
                    fill(u + AHEAD)

            def turn2(j):
                pe.wait_ge(s_xn2, j + 1)
                if j >= 2:
                    pe.wait_ge(s_h2, j - 1)
                for c in range(C):
                    ins = pe.transpose(pb[4 + j % 2][:, P * c:P * c + P], XN2[:, j, P * c:P * c + P], ident[:])
                ins.then_inc(s_t2, 1)

            def qkv(j):
                pe.wait_ge(s_c2, j + 1)
                if j >= 2:
                    pe.wait_ge(s_qc, j - 1)
                for c in range(C):
                    ins = pe.matmul(pb[6 + j % 2][:, 0:QKV + E1 + 1], XT[:, c, P * j:P * j + P], QW[:, c],
                                    start=(c == 0), stop=(c == C - 1))
                ins.then_inc(s_qk, 1)

            def out_small(j):
                dst, t = pb[j % 4][:, 0:D], slice(P * j, P * j + P)
                if j >= 4:
                    pe.wait_ge(s_x1, j - 3)
                pe.matmul(dst, XT[:, 0, t], WT[:, 0], start=True, stop=False)
                pe.matmul(dst, XT[:, 1, t], WT[:, 1], start=False, stop=False)
                pe.matmul(dst, WXT[:, 0, t], B2[:, 0], start=False, stop=False)
                pe.matmul(dst, WXT[:, 1, t], B2[:, 1], start=False, stop=False)

            def out_heads(j):
                for k in range(2):
                    n = 2 * j + k
                    pe.wait_ge(s_oh, n + 1)
                    pe.wait_ge(s_ol, n + 1)
                    for h in range(H // 2):
                        last = k == 1 and h == H // 2 - 1
                        ins = mm3(pb[j % 4][:, 0:D], OS[:, n % 4, 0, h], OS[:, n % 4, 1, h],
                                  WOP[k][:, 0, h], WOP[k][:, 1, h], False, last)
                    ins.then_inc(s_yh, 1)

            pe.wait_ge(s_Oc, UNITS)
            pe.wait_ge(s_wol, 8)
            out_small(0)
            out_small(1)
            for j in range(NT):
                out_heads(j)
                if j + 2 < NT:
                    out_small(j + 2)
                if stop_after_l0:
                    continue
                if j >= 1:
                    turn2(j - 1)
                if j >= 2:
                    qkv(j - 2)
            if stop_after_l0:
                return
            turn2(NT - 1)
            qkv(NT - 2)
            qkv(NT - 1)
            pe.wait_ge(s_l2, NT)

            def shared_up(q):
                m, half = q // 2, q % 2
                pe.wait_ge(s_gh, m + 1)
                pe.wait_ge(s_gl, m + 1)
                if q >= 2:
                    pe.wait_ge(s_sm, q - 1)
                xs = slice(512 * half, 512 * half + 512)
                for k in range(2):
                    for c in range(C):
                        ins = mm3(pb[2 * half + k][:], SG[:, m % 2, 0, k, c], SG[:, m % 2, 1, k, c],
                                  XTh[:, c, xs], XTl[:, c, xs], c == 0, c == C - 1)
                ins.then_inc(s_sf, 1)

            pe.wait_ge(s_h2, NT)
            pe.wait_ge(s_x1, NT)
            for q in range(4):
                shared_up(q)
            pe.wait_ge(s_sel, 1)
            pe.wait_ge(s_qc, NT)
            for j in range(NT):
                for i in range(j + 1):
                    ins = pe.matmul(pb[4][:, E1 * j:E1 * j + E1], (trib if i == j else onesb)[:], selb[:, i],
                                    start=(i == 0), stop=(i == j))
            ins.then_inc(s_po, 1)
            pe.wait_ge(s_sm, 4)
            for j in range(NT):
                pe.wait_ge(s_dm, j + 1)
                pe.wait_ge(s_xr, 2)
                pe.wait_ge(s_xrl, 2)
                for k in range(4):
                    c, half = k // 2, k % 2
                    for n, xr in enumerate((XRh, XRl)):
                        ins = pe.matmul(pb[k][:], xr[:, j, P * c:P * c + P], DM[:, j % 2, 512 * half:512 * half + 512],
                                        start=(j == 0 and n == 0), stop=(j == NT - 1 and n == 1))
                ins.then_inc(s_di, 1)

            def expert_up(g):
                pe.wait_ge(s_ew[g % 2], 64 * (g // 2 + 1))
                if g >= 2:
                    pe.wait_ge(s_eh, g - 1)
                for c in range(C):
                    for e in range(EPG):
                        s = slice(CAP * (EPG * g + e), CAP * (EPG * g + e) + CAP)
                        ins = pe.matmul(pb[4 + g % 2][CAP * e:CAP * e + CAP, 0:2 * F1], XE[:, c, s], WGU[g % 2][:, e, c],
                                        start=(c == 0), stop=(c == C - 1), skip_group_check=True)
                ins.then_inc(s_up, 1)

            def expert_turn(g):
                pe.wait_ge(s_eh, g + 1)
                if g >= 1:
                    pe.wait_ge(s_ec, g)
                pe.transpose(pb[6][:, 0:P], HE[:, g % 2, 0:P], ident[:])
                pe.transpose(pb[6][0:F1 - P, P:2 * P], HE[:, g % 2, P:F1], ident[:]).then_inc(s_et, 1)

            def expert_down(g):
                pe.wait_ge(s_ec, g + 1)
                if g >= 1:
                    pe.wait_ge(s_ye, g)
                for k in range(2):
                    for e in range(EPG):
                        ins = pe.matmul(pb[7][CAP * e:CAP * e + CAP, 0:D], HTE[:, g % 2, k, CAP * e:CAP * e + CAP],
                                        WD[g % 2][:, e, k], start=(k == 0), stop=(k == 1), skip_group_check=True)
                ins.then_inc(s_dn, 1)

            pe.wait_ge(s_xe, 4)
            for g in range(GR):
                if g >= 1:
                    expert_turn(g - 1)
                shared_up(4 + g)
                if g >= 1:
                    expert_down(g - 1)
                expert_up(g)
            expert_turn(GR - 1)
            pe.wait_ge(s_sd, 32)
            pe.wait_ge(s_sm, 12)
            for j in range(NT):
                if j >= 4:
                    pe.wait_ge(s_x2, j - 3)
                for m in range(FC):
                    ins = pe.matmul(pb[j % 4][:, 0:D], ACTT[:, m, P * j:P * j + P], SD[:, m], start=(m == 0), stop=(m == FC - 1))
                ins.then_inc(s_sh, 1)
                if j == 0:
                    expert_down(GR - 1)
            pe.wait_ge(s_ye, GR)
            pe.wait_ge(s_pv, 32)
            for f in range(4):
                c, half = f // 2, f % 2
                for i in range(4):
                    ins = pe.transpose(pb[4 + f][:, P * i:P * i + P], AO[:, 4 * half + i, P * c:P * c + P], ident[:])
                ins.then_inc(s_at, 1)
            pe.wait_ge(s_ac, 4)
            for j in range(NT):
                if j >= 4:
                    pe.wait_ge(s_pa, j - 3)
                for c in range(C):
                    ins = pe.matmul(pb[4 + j % 4][:, 0:D], AOT[:, c, P * j:P * j + P], projT[:, c], start=(c == 0), stop=(c == C - 1))
                ins.then_inc(s_fo, 1)

        @block.vector
        def _(dve):
            steps = [0]

            def step(ins):
                ins.then_inc(s_dv, 1)
                steps[0] += 1
                dve.wait_ge(s_dv, steps[0])

            for b in range(B):
                dve.wait_ge(s_x[b], 16)
                for j in (2 * b, 2 * b + 1):
                    nc.vector.bn_stats(stats[:, j], X[:, j]).then_inc(s_st, 1)
                dve.wait_ge(s_st, 2 * b + 2)
                nc.vector.bn_aggr(mv[:, 2 * b], stats[:, 2 * b])
                step(nc.vector.bn_aggr(mv[:, 2 * b + 1], stats[:, 2 * b + 1]))
                nc.vector.tensor_scalar(mv[:, 2 * b:2 * b + 2, 1], mv[:, 2 * b:2 * b + 2, 1], EPS, None,
                                        ALU.add).then_inc(s_var, 1)
                dve.wait_ge(s_std, b + 1)
                step(nc.vector.reciprocal(rstd[:, 2 * b:2 * b + 2], rstd[:, 2 * b:2 * b + 2]))
                for j in (2 * b, 2 * b + 1):
                    nc.vector.tensor_scalar(XN[:, j], X[:, j], mv[:, j, 0:1], rstd[:, j:j + 1],
                                            ALU.subtract, ALU.mult).then_inc(s_xn, 1)

            def w_low(n, raw):
                if n >= 2:
                    dve.wait_ge(s_qf, 8 * (n - 1)) if n < 6 else dve.wait_ge(s_kf, 8 * (n - 5))
                dve.wait_ge(s_wh, n + 1)
                nc.vector.tensor_tensor(WA[:, n % 2, 1], raw, WA[:, n % 2, 0].bitcast(F32), ALU.subtract).then_inc(s_wl, 1)

            kvraw = KVR.rearrange("p a c n -> p (a c n)")
            wqraw = lambda g: WQ[:, 1024 * g:1024 * g + 1024]
            for f in range(4):
                half, c = f // 2, f % 2
                xs = slice(512 * half, 512 * half + 512)
                dve.wait_ge(s_xtc, f + 1)
                dve.wait_ge(s_xth, f + 1)
                nc.vector.tensor_tensor(XTl[:, c, xs], XT[:, c, xs], XTh[:, c, xs].bitcast(F32), ALU.subtract).then_inc(s_xtl, 1)
            w_low(0, wqraw(0))
            dve.wait_ge(s_t, 1)
            nc.vector.tensor_copy(VC[:], pb[4][:, 0:48]).then_inc(s_vc, 1)
            dve.wait_ge(s_vc, 1)
            nc.vector.tensor_scalar(bqs[:], VC[:, 0:H], SCALE, None, ALU.mult).then_inc(s_vc, 1)
            w_low(1, wqraw(1))
            dve.wait_ge(s_r, 80)
            step(nc.vector.tensor_tensor(rg[:, 0], rg[:, 0], rg[:, 1], ALU.add))
            dve.wait_ge(s_lg, 1)
            nc.vector.tensor_tensor(lg[:], pb[4][:, 0:NT * E0].rearrange("p (j e) -> p j e", j=NT),
                                    rg[:, 0:1].to_broadcast([P, NT, E0]), ALU.add).then_inc(s_lc, 1)
            dve.wait_ge(s_lc, 1)
            for j in range(NT):
                ins = nc.vector.max(top[:, j], lg[:, j])
            step(ins)
            for j in range(NT):
                ins = nc.vector.max_index(topi[:, j], top[:, j], lg[:, j])
            step(ins)
            step(nc.vector.tensor_copy(topf[:], topi[:]))
            nc.vector.tensor_tensor(p01[:, 0], top[:, :, 1], top[:, :, 0], ALU.subtract).then_inc(s_df, 1)

            def q_copy(n):
                blk, half = n // 2, n % 2
                dve.wait_ge(s_qf, n + 1)
                nc.vector.tensor_scalar(QOb[:, :, 2 * half:2 * half + 2, :, blk].rearrange("p h b t -> p b h t"),
                                        pb[n % 4][:].rearrange("p (b h t) -> p b h t", b=2, h=H),
                                        SCALE, bqs[:, blk:blk + 1], ALU.mult, ALU.add).then_inc(s_qd, 1)

            def chosen(k):
                return (iota[:, None, 0:E0].to_broadcast([P, NT, E0]), topf[:, :, k:k + 1].to_broadcast([P, NT, E0]))

            for g in range(4):
                if g >= 1 and g + 1 < 4:
                    w_low(g + 1, wqraw(g + 1))
                for n in range(8 * g + 1, 8 * g + 8, 2):
                    q_copy(n)
                if g == 0:
                    dve.wait_ge(s_ex, 1)
                    step(nc.vector.tensor_scalar(p01[:, 0], p01[:, 1], 1.0, None, ALU.add))
                    step(nc.vector.reciprocal(p01[:, 0], p01[:, 0]))
                    step(nc.vector.tensor_tensor(p01[:, 1], p01[:, 1], p01[:, 0], ALU.mult))
                    dve.wait_ge(s_const, 4)
                    for k in range(2):
                        i, t = chosen(k)
                        dst = coef if k == 0 else tmpk
                        step(nc.vector.tensor_tensor(dst[:], i, t, ALU.is_equal))
                        step(nc.vector.tensor_tensor(dst[:], dst[:], p01[:, k, :, None].to_broadcast([P, NT, E0]), ALU.mult))
                    step(nc.vector.tensor_tensor(coef[:], coef[:], tmpk[:], ALU.add))
                if g == 2:
                    for j in range(NT):
                        dve.wait_ge(s_xa, 2 * (j // 2) + 2)
                        nc.vector.tensor_tensor(
                            WXA[:, j].rearrange("p (e r) -> p e r", e=E0),
                            pb[4 + j // 2][:, 256 * (j % 2):256 * (j % 2) + 256].rearrange("p (e r) -> p e r", e=E0),
                            coef[:, j, :, None].to_broadcast([P, E0, RANK]), ALU.mult).then_inc(s_wxa, 1)

            def fill_copy(n):
                p, f = n // 8, n % 8
                dve.wait_ge(s_kf, n + 1)
                if f == 0 and p >= 2:
                    dve.wait_ge(s_S, 8 * (p - 1))
                if f == 4 and p >= 2:
                    dve.wait_ge(s_O, 8 * (p - 1))
                if f == 0 and p == 0:
                    dve.wait_ge(s_xb, NT)
                if f < 4:
                    hh, ts = f // 2, slice(512 * (f % 2), 512 * (f % 2) + 512)
                    nc.vector.tensor_scalar(KT[:, p % 2, hh, ts], pb[6 + n % 2][:], VC[:, 16 + 2 * p + hh:17 + 2 * p + hh],
                                            None, ALU.add).then_inc(s_kc, 1)
                else:
                    nc.vector.tensor_copy(V[:, p % 2, 2 * (f - 4):2 * (f - 4) + 2].rearrange("p j n -> p (j n)"),
                                          pb[6 + n % 2][:]).then_inc(s_kc, 1)

            def max_of(u):
                i = u % 2
                dve.wait_ge(s_S, u + 1)
                nc.vector.tensor_reduce(nmax[:, i, 0:1], pb[i][:, 0:128], AX, ALU.max, negate=True)
                nc.vector.tensor_reduce(nmax[:, i, 1:2], pb[i][:, 128:384], AX, ALU.max, negate=True).then_inc(s_m, 1)

            def normalise(u):
                i = u % 2
                dve.wait_ge(s_e, u + 1)
                nc.vector.reciprocal(rinv[:, i], psumr[:, i]).then_inc(s_ri, 1)
                dve.wait_ge(s_ri, u + 1)
                nc.vector.tensor_scalar(Pb[:, i, 0:128], Pb[:, i, 0:128], rinv[:, i, 0:1], None, ALU.mult)
                nc.vector.tensor_scalar(Pb[:, i, 128:384], Pb[:, i, 128:384], rinv[:, i, 1:2], None, ALU.mult).then_inc(s_p, 1)

            w_low(4, kvraw)
            dve.wait_ge(s_kv, 64)
            w_low(5, kvraw)
            for n in range(AHEAD):
                fill_copy(n)
                if n == 7:
                    w_low(6, kvraw)
            max_of(0)
            max_of(1)
            normalise(0)
            normalise(1)
            def wo_low(n):
                dve.wait_ge(s_woh, n + 1)
                k, hs = n // 4, slice(2 * (n % 4), 2 * (n % 4) + 2)
                nc.vector.tensor_tensor(WOP[k][:, 1, hs], WOv[:, 2 * n:2 * n + 2], WOP[k][:, 0, hs].bitcast(F32), ALU.subtract).then_inc(s_wol, 1)

            for u in range(UNITS):
                if u + 2 < UNITS:
                    max_of(u + 2)
                if u + 2 < UNITS:
                    normalise(u + 2)
                if u in WO_AT:
                    wo_low(WO_AT.index(u))
                if u + AHEAD < UNITS:
                    fill_copy(u + AHEAD)
                if u % 8 == 5 and u // 8 + 3 < PAIRS:
                    w_low(4 + u // 8 + 3, kvraw)
            def o_low(n):
                j = n // 2
                dve.wait_ge(s_oh, n + 1)
                nc.vector.tensor_tensor(OS[:, n % 4, 1], QO[:, 8 * (n % 2):8 * (n % 2) + 8, j // 2, P * (j % 2):P * (j % 2) + P],
                                        OS[:, n % 4, 0].bitcast(F32), ALU.subtract).then_inc(s_ol, 1)

            def xt_low(j):
                js = slice(P * j, P * j + P)
                dve.wait_ge(s_h2, j + 1)
                nc.vector.tensor_tensor(XTl[:, :, js], XT[:, :, js], XTh[:, :, js].bitcast(F32), ALU.subtract).then_inc(s_l2, 1)

            for n in range(4):
                o_low(n)
            for j in range(NT):
                if 2 * j + 4 < 2 * NT:
                    o_low(2 * j + 4)
                    o_low(2 * j + 5)
                if j >= 1 and not stop_after_l0:
                    xt_low(j - 1)
                dve.wait_ge(s_yh, 2 * j + 2)
                dve.wait_ge(s_xb, j + 1)
                nc.vector.tensor_tensor(X[:, j], pb[j % 4][:, 0:D], X[:, j], ALU.add).then_inc(s_x1, 1)
                if stop_after_l0:
                    continue
                dve.wait_ge(s_x1, j + 1)
                step(nc.vector.bn_stats(stats[:, j], X[:, j]))
                step(nc.vector.bn_aggr(mv[:, j], stats[:, j]))
                nc.vector.tensor_scalar(mv[:, j, 1:2], mv[:, j, 1:2], EPS, None, ALU.add).then_inc(s_va2, 1)
                dve.wait_ge(s_sd2, j + 1)
                step(nc.vector.reciprocal(rstd[:, j:j + 1], rstd[:, j:j + 1]))
                nc.vector.tensor_scalar(XN2[:, j], X[:, j], mv[:, j, 0:1], rstd[:, j:j + 1], ALU.subtract, ALU.mult).then_inc(s_xn2, 1)
            if stop_after_l0:
                return
            def g_low(m):
                dve.wait_ge(s_gh, m + 1)
                nc.vector.tensor_tensor(SG[:, m % 2, 1].rearrange("p a c n -> p (a c) n"),
                                        SGR[:, :, :, P * m:P * m + P].rearrange("p a c n -> p (a c) n"),
                                        SG[:, m % 2, 0].bitcast(F32).rearrange("p a c n -> p (a c) n"), ALU.subtract).then_inc(s_gl, 1)

            xt_low(NT - 1)
            g_low(0)
            g_low(1)
            dve.wait_ge(s_qc, NT)
            for j in range(NT):
                ins = nc.vector.max(top1[:, j], QS[:, j, QKV:QKV + E1])
            step(ins)
            for j in range(NT):
                ins = nc.vector.max_index(topi1[:, j], top1[:, j], QS[:, j, QKV:QKV + E1])
            step(ins)
            nc.vector.tensor_copy(topf1[:], topi1[:])
            nc.vector.tensor_tensor(w4[:], top1[:, :, 0:K1], top1[:, :, 0:1].to_broadcast([P, NT, K1]), ALU.subtract).then_inc(s_d1, 1)

            def shared_product(q):
                m, half = q // 2, q % 2
                dst = ACTT[:, m, 512 * half:512 * half + 512]
                dve.wait_ge(s_ss, q + 1)
                nc.vector.tensor_tensor(dst, dst, pb[2 * half + 1][:], ALU.mult).then_inc(s_sm, 1)

            dve.wait_ge(s_e1, 2)
            step(nc.vector.tensor_reduce(ws[:], w4[:], AX, ALU.add))
            step(nc.vector.reciprocal(ws[:], ws[:]))
            step(nc.vector.tensor_tensor(w4[:], w4[:], ws[:, :, None].to_broadcast([P, NT, K1]), ALU.mult))
            step(nc.vector.tensor_scalar(sig[:], sig[:], 1.0, None, ALU.add))
            step(nc.vector.reciprocal(sig[:], sig[:]))
            full = [P, NT, E1]
            for k in range(K1):
                one = sel if k == 0 else tmp1
                step(nc.vector.tensor_tensor(one[:], iota[:, None, :].to_broadcast(full),
                                             topf1[:, :, k:k + 1].to_broadcast(full), ALU.is_equal))
                if k:
                    step(nc.vector.tensor_tensor(sel[:], sel[:], one[:], ALU.add))
            nc.vector.tensor_copy(selb[:], sel[:]).then_inc(s_sel, 1)
            for i in range(2):
                dve.wait_ge(s_xr, i + 1)
                nc.vector.tensor_tensor(XRl[:, 4 * i:4 * i + 4], XN2[:, 4 * i:4 * i + 4], XRh[:, 4 * i:4 * i + 4].bitcast(F32),
                                        ALU.subtract).then_inc(s_xrl, 1)
            for q in range(4):
                shared_product(q)
                if q % 2:
                    g_low(q // 2 + 2)
            dve.wait_ge(s_po, 1)
            step(nc.vector.tensor_tensor(posm[:], pb[4][:, 0:NT * E1].rearrange("p (j e) -> p j e", j=NT), sel[:], ALU.mult))
            step(nc.vector.tensor_scalar(posm[:], posm[:], -1.0, None, ALU.add))

            def slots_of(j, dst):
                return nc.vector.tensor_tensor(dst.rearrange("p (e c) -> p e c", e=E1),
                                               posm[:, j, :, None].to_broadcast([P, E1, CAP]),
                                               iota[:, None, :].to_broadcast([P, E1, CAP]), ALU.is_equal)

            slots_of(0, DM[:, 0]).then_inc(s_dm, 1)
            slots_of(1, DM[:, 1]).then_inc(s_dm, 1)
            for j in range(2, NT):
                dve.wait_ge(s_di, j - 1)
                slots_of(j, DM[:, j % 2]).then_inc(s_dm, 1)
            step(nc.vector.memset(region(30720, 512), MASKED))

            def attn_scores(f, k):
                kk = QS[:, 2 * k + f, 0:QKV].rearrange("p (g n) -> p g n", g=G1)[:, :, None, GW - 2 * D1:GW - D1].to_broadcast([P, G1, 4, D1])
                for i in range(k, 4):
                    q = QS[:, 2 * i + f, 0:QKV].rearrange("p (g n) -> p g n", g=G1)[:, :, 0:4 * D1].rearrange("p g (r d) -> p g r d", r=4)
                    ins = nc.vector.tensor_tensor(PR[:, i].rearrange("p (g r d) -> p g r d", g=G1, r=4), q, kk, ALU.mult)
                step(ins)
                step(nc.vector.tensor_reduce(SC[:, f, k:4, :, k], PR[:, k:4].rearrange("p i (h d) -> p i h d", h=H1), AX, ALU.add))

            def slot_indices():
                full = [P, NT, E1]
                for k in range(K1):
                    step(nc.vector.tensor_tensor(tmp1[:], iota[:, None, :].to_broadcast(full), topf1[:, :, k:k + 1].to_broadcast(full), ALU.is_equal))
                    step(nc.vector.tensor_tensor(tmp1[:], tmp1[:], posm[:], ALU.mult))
                    step(nc.vector.tensor_reduce(pk[:, :, k], tmp1[:], AX, ALU.add))
                step(nc.vector.tensor_scalar(ok[:], pk[:], float(CAP), None, ALU.is_lt))
                step(nc.vector.tensor_tensor(w4[:], w4[:], ok[:], ALU.mult))
                step(nc.vector.tensor_scalar(pk[:], pk[:], float(CAP - 1), None, ALU.min))
                step(nc.vector.scalar_tensor_tensor(out=pk[:], in0=topf1[:, :, 0:K1], scalar=float(CAP), in1=pk[:],
                                                    op0=ALU.mult, op1=ALU.add))
                nc.vector.tensor_copy(idx[:], pk[:]).then_inc(s_ix, 1)

            for g in range(GR):
                shared_product(4 + g)
                if g in (1, 3):
                    g_low(4 + g // 2)
                if g >= 1:
                    dve.wait_ge(s_dn, g)
                    nc.vector.tensor_copy(YE[:, g - 1], pb[7][:, 0:D]).then_inc(s_ye, 1)
                dve.wait_ge(s_es, g + 1)
                nc.vector.tensor_tensor(HE[:, g % 2], HE[:, g % 2], pb[4 + g % 2][:, F1:2 * F1], ALU.mult).then_inc(s_eh, 1)
                if g < 4:
                    attn_scores(0, g)
                    attn_scores(1, g)
                if g == 4:
                    step(nc.vector.tensor_reduce(mx1[:], SCf, AX, ALU.max))
                    nc.vector.tensor_tensor(SCf, SCf, mx1[:, :, None].to_broadcast([P, 128, 4]), ALU.subtract).then_inc(s_am, 1)
                if g == 5:
                    dve.wait_ge(s_ae, 1)
                    step(nc.vector.tensor_reduce(mx1[:], SCf, AX, ALU.add))
                    step(nc.vector.reciprocal(mx1[:], mx1[:]))
                    nc.vector.tensor_tensor(SCf, SCf, mx1[:, :, None].to_broadcast([P, 128, 4]), ALU.mult).then_inc(s_ap, 1)
                if g == 6:
                    slot_indices()
            dve.wait_ge(s_dn, GR)
            nc.vector.tensor_copy(YE[:, GR - 1], pb[7][:, 0:D]).then_inc(s_ye, 1)
            for j in range(NT):
                dve.wait_ge(s_sh, j + 1)
                nc.vector.scalar_tensor_tensor(out=X[:, j], in0=pb[j % 4][:, 0:D], scalar=sig[:, j:j + 1], in1=X[:, j],
                                               op0=ALU.mult, op1=ALU.add).then_inc(s_x2, 1)
            dve.wait_ge(s_x2, NT)
            for j in range(NT):
                dve.wait_ge(s_fo, j + 1)
                nc.vector.tensor_tensor(X[:, j], pb[4 + j % 4][:, 0:D], X[:, j], ALU.add).then_inc(s_pa, 1)
            dve.wait_ge(s_pa, NT)
            for j in range(NT):
                dve.wait_ge(s_g[j], 16 * K1)
                for k in range(K1):
                    ins = nc.vector.scalar_tensor_tensor(out=X[:, j], in0=G[:, j, k], scalar=w4[:, j, k:k + 1], in1=X[:, j],
                                                         op0=ALU.mult, op1=ALU.add)
                    if k < K1 - 1:
                        step(ins)
                ins.then_inc(s_o, 1)


_INS = ['L0_attn_x', 'L0_attn_Wq', 'L0_attn_bq', 'L0_attn_Wk', 'L0_attn_bk', 'L0_attn_Wv', 'L0_attn_bv', 'L0_attn_Wo',
        'L0_attn_bo', 'L0_ffn_W', 'L0_ffn_bias', 'L0_ffn_rw1', 'L0_ffn_rb1', 'L0_ffn_rw2', 'L0_ffn_rb2', 'L0_ffn_A',
        'L0_ffn_B', 'L0_ffn_gates', 'L1_attn_weight_qkv', 'L1_attn_weight_proj', 'L1_ffn_Wr', 'L1_ffn_Wg', 'L1_ffn_Wu',
        'L1_ffn_Wd', 'L1_ffn_Wsg', 'L1_ffn_Wsu', 'L1_ffn_Wsd', 'L1_ffn_Wse']


def kernel(**inputs):
    import numpy as np
    from concourse import bacc
    from concourse.bass_utils import run_bass_kernel_spmd

    nc = bacc.Bacc("TRN2", target_bir_lowering=False, num_devices=1, dynamic_dma_scratch_size=2048)
    arrays, aps = {}, {}
    for name in _INS:
        v = np.ascontiguousarray(inputs[name])
        arrays[f"in_{name}"] = v
        aps[name] = nc.dram_tensor(f"in_{name}", v.shape, mybir.dt.from_np(v.dtype), kind="ExternalInput").ap()
    out = nc.dram_tensor("out", (B, T, D), F32, kind="ExternalOutput").ap()
    program(nc, aps, out)
    r = run_bass_kernel_spmd(nc, [arrays], core_ids=[0])
    return r.results[0]["out"]
```

```python
from contextlib import ExitStack

import concourse.bass as bass
from concourse import mybir

F32 = mybir.dt.float32
FR = mybir.dt.float32r
BF16 = mybir.dt.bfloat16
U32 = mybir.dt.uint32
ALU = mybir.AluOpType
ACT = mybir.ActivationFunctionType
AX = mybir.AxisListType.X

P = 128
B, T, D = 4, 256, 256
N = B * T
NT = N // P
C = D // P
H, DH = 16, 128
SCALE = float(DH) ** -0.5
PAIRS = H // 2
UNITS = H * B
WO_AT = [16, 19, 22, 26, 53, 55, 57, 59]
O_AT = {56: 0, 58: 2, 62: 1}
EXPERT_STEPS = [("shared", (4, 0)), ("up", 0), ("shared", (4, 1)), ("turn", 0), ("up", 1), ("down", 0)]
for group in range(1, 7):
    EXPERT_STEPS += [("shared", ((9 + group) // 2, (9 + group) % 2)), ("turn", group), ("up", group + 1), ("down", group)]
EXPERT_STEPS += [("turn", 7), ("shared", (8, 0)), ("down", 7), ("shared", (8, 1))]
EXPERT_STEPS += [("shared", (q, k)) for q in (9, 10, 11) for k in range(2)]
PROJ_AFTER = 6
TOPK_FIRST = 6
AHEAD = 11
E0, RANK, HID = 16, 16, 64
H1, D1, G1 = 16, 16, 4
SCALE1 = float(D1) ** -0.5
GW = (H1 // G1 + 2) * D1
QKV = G1 * GW
E1, K1, CAP = 32, 4, 32
F1, FS = 176, 704
FC = 6
FP = FC * P
SLOTS = E1 * CAP
GR = SLOTS // P
EPG = E1 // GR
EPS = 1e-5
MASKED = -1.0e30


def program(nc, a, out):
    ctx = ExitStack()
    with ctx:
        def sb(name, shape, dt=F32):
            return ctx.enter_context(nc.sbuf_tensor(name, shape, dt))

        def sem(name):
            return ctx.enter_context(nc.semaphore(name))

        pb = [ctx.enter_context(nc.psum_tensor(f"bank{i}", [P, 512], F32)) for i in range(8)]

        ident = sb("ident", [P, P])
        identb = sb("identb", [P, P], BF16)
        maskb = sb("maskb", [P, P], BF16)
        trib = sb("trib", [P, P], BF16)
        onesb = sb("onesb", [P, P], BF16)
        iota = sb("iota", [P, 32])

        X = sb("X", [P, NT, D])
        XT = sb("XT", [P, C, N])
        XTh = sb("XTh", [P, C, N], FR)
        XTl = sb("XTl", [P, C, N], FR)
        stats = sb("stats", [P, NT, 6])
        mv = sb("mv", [P, NT, 2])
        rstd = sb("rstd", [P, NT])

        at_wa = nc.sbuf_base
        WA = sb("WA", [P, 2, 2, 1024], FR)
        WAF = nc.alloc_sbuf_tensor_at("WAF", [P, 4096], F32, offset=at_wa)

        at0 = nc.sbuf_base
        arena = sb("arena", [P, 35840])

        def region(at, words):
            return arena[:, at:at + words]

        QO = region(0, 16384).rearrange("p (h b t) -> p h b t", h=H, b=B)
        QOb = region(0, 16384).rearrange("p (h b t k) -> p h b t k", h=H, b=B, k=16)
        WQ = region(16384, 4096)
        WQv = WQ.rearrange("p (g c n) -> p g c n", g=4, c=C)
        WOv = WQ.rearrange("p (h n) -> p h n", h=H)
        KVR = region(31744, 1024).rearrange("p (a c n) -> p a c n", a=2, c=C)
        KTf = region(20480, 4096)
        KT = KTf.rearrange("p (a h n) -> p a h n", a=2, h=2)
        XN = KTf[:, 0:2048].rearrange("p (j d) -> p j d", j=NT)
        WXA = KTf[:, 2048:4096].rearrange("p (j d) -> p j d", j=NT)
        Vf = region(24576, 4096)
        V = Vf.rearrange("p (a j n) -> p a j n", a=2, j=NT)
        stW = Vf[:, 0:512].rearrange("p (o i) -> p o i", o=2)
        stA = Vf[:, 512:1024].rearrange("p (o i) -> p o i", o=2)
        stB = Vf[:, 1024:1536].rearrange("p (o e r) -> p o e r", o=2, e=E0)
        stBf = Vf[:, 1024:1536].rearrange("p (o i) -> p o i", o=2)
        stQKV = Vf[:, 1536:2304].rearrange("p (o i) -> p o i", o=3)
        stP = Vf[:, 2304:2816].rearrange("p (o i) -> p o i", o=2)
        stR1 = Vf[0:HID, 2816:3072]
        stR2 = Vf[0:E0, 3072:3136]
        VB = Vf[0:48, 3136:3264]
        bo2 = Vf[:, 3264:3776].rearrange("p (o i) -> p o i", o=2)
        Pb = region(28672, 768).rearrange("p (i n) -> p i n", i=2)
        PTb = region(29440, 768).rearrange("p (i n) -> p i n", i=2)
        nmax = sb("nmax", [P, 2, 2])
        psumr = sb("psumr", [P, 2, 2])
        rinv = sb("rinv", [P, 2, 2])
        WT, AT, B2 = (region(30208 + 512 * i, 512).rearrange("p (c n) -> p c n", c=C) for i in range(3))
        QW = sb("QW", [P, C, QKV + E1 + 1])
        projT = sb("projT", [P, C, D])
        R1T = sb("R1T", [P, C, P])
        R2T = sb("R2T", [P, E0])
        rb1c = sb("rb1c", [P, 1])
        VC = sb("VC", [P, 48])
        bqs = sb("bqs", [P, H])
        rg = sb("rg", [P, 2, E0])
        HT = region(32768, N)
        lg = sb("lg", [P, NT, E0])
        top = sb("top", [P, NT, 8])
        topi = sb("topi", [P, NT, 8], U32)
        topf = sb("topf", [P, NT, 8])
        tmpk = sb("tmpk", [P, NT, E0])
        coef = sb("coef", [P, NT, E0])
        p01 = sb("p01", [P, 3, NT])
        WXT = region(33792, 2048).rearrange("p (c n) -> p c n", c=C)

        at1 = nc.sbuf_base
        FRX = sb("FRX", [P, 4096], FR)
        FRF = nc.alloc_sbuf_tensor_at("FRF", [P, 4096], F32, offset=at1)
        WOP = [w.rearrange("p (s h n) -> p s h n", s=2, h=H // 2)
               for w in (FRX[:], WA[:].rearrange("p a s n -> p (a s n)"))]
        OS = nc.alloc_sbuf_tensor_at("OS", [P, 4, 2, H // 2, P], FR, offset=at0 + 4 * 20480)

        up_parts = [(region(0, 2816),), (region(4864, 2816),), (XT[:].rearrange("p c n -> p (c n)")[:, 0:1408], FRF[:, 1536:2944]),
                    (region(24576, 2816),)]
        WGU = [[w.rearrange("p (e c n) -> p e c n", e=EPG // len(ws_), c=C) for w in ws_] for ws_ in up_parts]
        WD = [w.rearrange("p (e c n) -> p e c n", e=EPG, c=2)
              for w in (region(2816, 2048), region(7680, 2048), region(33792, 2048), WAF[:, 2048:4096])]
        PLACES = len(WD)

        def up_weights(g, e):
            parts = WGU[g % PLACES]
            return parts[e * len(parts) // EPG][:, e % (EPG // len(parts))]

        SGR = region(9728, 3072).rearrange("p (a c n) -> p a c n", a=2, c=C)
        ACTT = [region(12800 + N * m, N) for m in range(3)] + [WAF[:, 0:N], WAF[:, N:2 * N], region(27648, N)]
        G = region(0, 8192).rearrange("p (j k n) -> p j k n", j=NT, k=K1)
        HTE = region(15872, 512).rearrange("p (i k n) -> p i k n", i=2, k=2)
        QS = region(16384, 3360).rearrange("p (j n) -> p j n", j=NT)
        HE = region(19744, 352).rearrange("p (i n) -> p i n", i=2)
        PR = [region(27648, 1024).rearrange("p (i n) -> p i n", i=4),
              FRF[:, 2944:3968].rearrange("p (i n) -> p i n", i=4)]
        SD = FRF[:, 0:1536].rearrange("p (m n) -> p m n", m=FC)
        AOT = XT
        XE = region(28672, 2048).rearrange("p (c n) -> p c n", c=C)
        SC = region(30720, 512).rearrange("p (f i h j) -> p f i h j", f=2, i=4, h=H1)
        SCf = region(30720, 512).rearrange("p (x j) -> p x j", j=4)
        XN2 = region(31744, 2048).rearrange("p (j n) -> p j n", j=NT)
        AO = XN2
        YE = region(22528, 2048).rearrange("p (g n) -> p g n", g=GR)
        XRh, XRl = (WA[:, i].rearrange("p a n -> p (a n)").rearrange("p (j n) -> p j n", j=NT) for i in range(2))
        SG, DM = (OS[:, i].rearrange("p s h n -> p (s h n)") for i in range(2))
        SG = SG.rearrange("p (i s a c n) -> p i s a c n", i=2, s=2, a=2, c=C)
        DM = DM.rearrange("p (i n) -> p i n", i=2)
        selb = sb("selb", [P, NT, E1], BF16)
        sel = sb("sel", [P, NT, E1])
        tmp1 = sb("tmp1", [P, NT, E1])
        posm = sb("posm", [P, NT, E1])
        top1 = sb("top1", [P, NT, 8])
        topi1 = sb("topi1", [P, NT, 8], U32)
        topf1 = sb("topf1", [P, NT, 8])
        w4 = sb("w4", [P, NT, K1])
        pk = sb("pk", [P, NT, K1])
        ok = sb("ok", [P, NT, K1])
        idx = sb("idx", [P, NT, K1], U32)
        rows = nc.dram_tensor("expert_rows", (SLOTS, D), F32, kind="Internal").ap()
        ws = sb("ws", [P, NT])
        sig = sb("sig", [P, NT])
        mx1 = sb("mx1", [P, 128])
        pvt = sb("pvt", [P, 256])

        s_x = [sem(f"x_loaded{b}") for b in range(B)]
        s_vb = sem("bias_vectors_loaded")
        s_r = sem("router_weights_loaded")
        s_wq = [sem(f"wq_loaded{g}") for g in range(4)]
        s_sw = sem("small_weights_loaded")
        s_bo = sem("output_biases_loaded")
        s_kv = sem("kv_weights_loaded")
        s_wo = sem("wo_loaded")
        s_pool = sem("pool_step_done")
        s_const = sem("constants_ready")
        s_pad = sem("padding_ready")
        s_st = sem("ln_stats_done")
        s_var = sem("var_ready")
        s_std = sem("std_ready")
        s_xn = sem("xn_ready")
        s_xb = sem("x_biased")
        s_xt = sem("xn_transposed")
        s_xtc = sem("xt_copied")
        s_xth = sem("xt_high_ready")
        s_xtl = sem("xt_low_ready")
        s_t = sem("weights_transposed")
        s_tc = sem("transposed_weights_copied")
        s_vc = sem("bias_columns_ready")
        s_wh = sem("weight_high_ready")
        s_wl = sem("weight_low_ready")
        s_qf = sem("q_filled")
        s_qa = sem("q_copied_by_act")
        s_qd = sem("q_copied_by_dve")
        s_ht = sem("router_hidden_done")
        s_hs = sem("router_silu_done")
        s_lg = sem("router_logits_done")
        s_lc = sem("router_logits_copied")
        s_dv = sem("dve_step_done")
        s_ex = sem("router_exp_done")
        s_df = sem("router_difference_ready")
        s_xa = sem("xa_done")
        s_wxa = sem("xa_weighted")
        s_wxt = sem("xa_transposed")
        s_wxc = sem("xa_transposed_copied")
        s_kf = sem("kv_filled")
        s_kc = sem("kv_copied")
        s_S = sem("scores_ready")
        s_m = sem("max_ready")
        s_e = sem("exp_ready")
        s_ri = sem("rinv_ready")
        s_p = sem("probs_ready")
        s_T = sem("probs_transposed")
        s_Tc = sem("probs_transposed_copied")
        s_O = sem("heads_ready")
        s_Oc = sem("heads_copied")
        s_x1 = sem("x1_ready")
        s_pd = sem("shared_up_padding_ready")
        s_ps = sem("shared_down_padding_ready")
        s_pe = sem("expert_padding_ready")
        s_sg = sem("shared_up_weights_loaded")
        s_sd = sem("shared_down_weights_loaded")
        s_ew = [sem(f"expert_up_weights_loaded{i}") for i in range(4)]
        s_ed = [sem(f"expert_down_weights_loaded{i}") for i in range(4)]
        s_va2 = sem("var2_ready")
        s_sd2 = sem("std2_ready")
        s_xn2 = sem("xn2_ready")
        s_xr = sem("xn2_high_ready")
        s_xrl = sem("xn2_low_ready")
        s_t2 = sem("xn2_transposed")
        s_c2 = sem("xn2_transpose_copied")
        s_h2 = sem("xn2_transpose_high_ready")
        s_l2 = sem("xn2_transpose_low_ready")
        s_qk = sem("qkv_done")
        s_qc = sem("qkv_copied")
        s_gh = sem("shared_weight_high_ready")
        s_gl = sem("shared_weight_low_ready")
        s_sf = sem("shared_filled")
        s_ss = sem("shared_silu_done")
        s_sm = sem("shared_product_done")
        s_d1 = sem("gate_logit_differences_ready")
        s_e1 = sem("gate_exp_done")
        s_sel = sem("selection_ready")
        s_po = sem("positions_done")
        s_dm = sem("dispatch_mask_ready")
        s_di = sem("dispatched_tile")
        s_xe = sem("slots_copied")
        s_up = sem("expert_up_done")
        s_es = sem("expert_silu_done")
        s_eh = sem("expert_hidden_ready")
        s_et = sem("expert_hidden_transposed")
        s_ec = sem("expert_hidden_copied")
        s_dn = sem("expert_down_done")
        s_ye = sem("expert_output_copied")
        s_sh = sem("shared_down_done")
        s_x2 = sem("shared_added")
        s_pp = sem("attn1_products_ready")
        s_sr = sem("attn1_scores_summed")
        s_xd = sem("slots_copied_by_dve")
        s_am = sem("attn1_scores_less_max")
        s_ae = sem("attn1_exp_done")
        s_ap = sem("attn1_probs_ready")
        s_pv = sem("attn1_step_done")
        s_at = sem("attn1_transposed")
        s_ac = sem("attn1_transposed_copied")
        s_woh = sem("wo_high_ready")
        s_wol = sem("wo_low_ready")
        s_oh = sem("heads_high_ready")
        s_ol = sem("heads_low_ready")
        s_yh = sem("l0_out_half_done")
        s_ix = sem("slot_indices_ready")
        s_er = sem("expert_rows_stored")
        s_g = [sem(f"rows_gathered{j}") for j in range(NT)]
        s_fo = sem("attn1_projected")
        s_pa = sem("attn1_added")
        s_o = sem("out_ready")
        s_out = sem("out_stored")

        block = ctx.enter_context(nc.Block())

        x_t = a["L0_attn_x"].rearrange("b (q p) d -> p b q d", p=P)
        out_t = out.rearrange("b (q p) d -> p (b q) d", p=P)
        wq_t = a["L0_attn_Wq"].rearrange("(c p) n -> p c n", p=P)
        wk_t = a["L0_attn_Wk"].rearrange("(c p) n -> p c n", p=P)
        wv_t = a["L0_attn_Wv"].rearrange("(c p) n -> p c n", p=P)
        two = lambda w: w.rearrange("(o p) i -> p o i", p=P)
        row = lambda v, k: v.rearrange("(h d) -> h d", h=k)

        def unit(u):
            p, hh, b = u // 8, u // 4 % 2, u % 4
            return p, hh, b, 2 * p + hh

        def place(n):
            return {0: 1, 2: 2, 1: 3}.get(n, n + 1)

        def y_bank(j):
            return 6 + j if j < 2 else j % 4

        shared = [(0, 0), (1, 0), (0, 1), (1, 1)] + [(m, half) for m in range(2, FC) for half in range(2)]

        @block.sync
        def _(sp):
            for b in range(B):
                sp.dma_start(X[:, 2 * b:2 * b + 2, :], x_t[:, b]).then_inc(s_x[b], 16)
                if b == 1:
                    sp.dma_start(WQv[:, 0], wq_t[:, :, 0:512]).then_inc(s_wq[0], 16)
            for i, n in enumerate(("bq", "bk", "bv")):
                sp.dma_start(VB[16 * i:16 * i + 16, :], row(a["L0_attn_" + n], H)).then_inc(s_vb, 16)
            sp.dma_start(stR1, a["L0_ffn_rw1"]).then_inc(s_r, 16)
            sp.dma_start(stR2, a["L0_ffn_rw2"][0:E0, :]).then_inc(s_r, 16)
            sp.wait_ge(s_pad, 3)
            sp.dma_start(rb1c[0:HID, :], a["L0_ffn_rb1"].rearrange("(p a) -> p a", a=1)).then_inc(s_r, 16)
            sp.dma_start(rg[:, 0], a["L0_ffn_rb2"][0:E0].partition_broadcast(P)).then_inc(s_r, 16)
            sp.dma_start(rg[:, 1], a["L0_ffn_gates"].partition_broadcast(P)).then_inc(s_r, 16)
            sp.dma_start(WQv[:, 1], wq_t[:, :, 512:1024]).then_inc(s_wq[1], 16)
            sp.dma_start(stW, two(a["L0_ffn_W"])).then_inc(s_sw, 16)
            sp.dma_start(stA, a["L0_ffn_A"].rearrange("(o e) r i -> (e r) o i", o=2)).then_inc(s_sw, 16)
            for o in range(2):
                sp.dma_start(stB[:, o], a["L0_ffn_B"][:, P * o:P * o + P, :].rearrange("e p r -> p e r")).then_inc(s_sw, 16)
            sp.dma_start(stQKV, two(a["L1_attn_weight_qkv"])).then_inc(s_sw, 16)
            sp.dma_start(stP, two(a["L1_attn_weight_proj"])).then_inc(s_sw, 16)
            sp.dma_start(bo2[:, 0], a["L0_attn_bo"].partition_broadcast(P)).then_inc(s_bo, 16)
            sp.dma_start(bo2[:, 1], a["L0_ffn_bias"].partition_broadcast(P)).then_inc(s_bo, 16)
            for g in (2, 3):
                sp.dma_start(WQv[:, g], wq_t[:, :, 512 * g:512 * g + 512]).then_inc(s_wq[g], 16)

            for c in range(C):
                sp.dma_start(QW[:, c, QKV:QKV + E1], a["L1_ffn_Wr"][P * c:P * c + P, :]).then_inc(s_bo, 16)
                sp.dma_start(QW[:, c, QKV + E1:QKV + E1 + 1], a["L1_ffn_Wse"][P * c:P * c + P, :]).then_inc(s_bo, 16)

            def load_kv(p):
                sp.dma_start(KVR[:, 0], wk_t[:, :, 256 * p:256 * p + 256]).then_inc(s_kv, 16)
                sp.dma_start(KVR[:, 1], wv_t[:, :, 256 * p:256 * p + 256]).then_inc(s_kv, 16)

            load_kv(0)
            sp.wait_ge(s_wl, 4)
            sp.dma_start(WOv, a["L0_attn_Wo"].rearrange("(h d) n -> d h n", d=P)).then_inc(s_wo, 16)
            for p in range(1, PAIRS):
                sp.wait_ge(s_wl, 4 + p)
                load_kv(p)
            sp.wait_ge(s_pd, 1)
            for i, n in enumerate(("Wsg", "Wsu")):
                sp.dma_start(SGR[:, i, :, 0:FS], a["L1_ffn_" + n].rearrange("(c p) n -> p c n", p=P)).then_inc(s_sg, 16)
            sp.wait_ge(s_pe, 3)

            def store_rows(g):
                sp.wait_ge(s_ye, g + 1)
                sp.dma_start(rows[P * g:P * g + P], YE[:, g]).then_inc(s_er, 16)

            for g in range(GR):
                e, i = slice(EPG * g, EPG * g + EPG), g % PLACES
                if g == 2:
                    sp.wait_ge(s_l2, NT)
                    sp.wait_ge(s_qk, NT)
                    sp.wait_ge(s_pe, 4)
                if g >= PLACES:
                    sp.wait_ge(s_up, g - PLACES + 1)
                for k, n in enumerate(("Wg", "Wu")):
                    w = a["L1_ffn_" + n][e].rearrange("e (c p) n -> p e c n", p=P)
                    m = EPG // len(WGU[i])
                    for h, part in enumerate(WGU[i]):
                        sp.dma_start(part[:, :, :, F1 * k:F1 * k + F1], w[:, m * h:m * h + m]).then_inc(s_ew[i], 16)
                if g == 3:
                    sp.wait_ge(s_pe, 5)
                if g >= PLACES:
                    sp.wait_ge(s_dn, g - PLACES + 1)
                sp.dma_start(WD[i][:, :, 0], a["L1_ffn_Wd"][e, 0:P].rearrange("e p n -> p e n")).then_inc(s_ed[i], 16)
                sp.dma_start(WD[i][0:F1 - P, :, 1], a["L1_ffn_Wd"][e, P:F1].rearrange("e p n -> p e n")).then_inc(s_ed[i], 16)
                if g == 1:
                    sp.wait_ge(s_ps, 1)
                    sp.dma_start(SD[:, 0:FC - 1], a["L1_ffn_Wsd"][0:P * (FC - 1), :].rearrange("(m p) n -> p m n", p=P)).then_inc(s_sd, 16)
                    sp.dma_start(SD[0:FS - P * (FC - 1), FC - 1], a["L1_ffn_Wsd"][P * (FC - 1):FS, :]).then_inc(s_sd, 16)
                if g >= 4:
                    store_rows(g - 4)
            store_rows(GR - 4)
            store_rows(GR - 3)
            store_rows(GR - 2)
            store_rows(GR - 1)
            for j in range(NT):
                sp.wait_ge(s_o, j + 1)
                sp.wait_ge(s_pa, j + 1)
                sp.dma_start(out_t[:, j], X[:, j]).then_inc(s_out, 16)
            sp.wait_ge(s_out, 16 * NT)

        @block.gpsimd
        def _(pool):
            steps = [0]

            def step(ins):
                ins.then_inc(s_pool, 1)
                steps[0] += 1
                pool.wait_ge(s_pool, steps[0])

            step(pool.memset(ident[:], 0.0))
            pool.affine_select(out=ident[:], in_=ident[:], compare_op=ALU.not_equal, fill=1.0, base=0,
                               pattern=[[-1, P]], channel_multiplier=1).then_inc(s_const, 1)
            pool.memset(R1T[:], 0.0).then_inc(s_pad, 1)
            pool.memset(R2T[:], 0.0).then_inc(s_pad, 1)
            pool.memset(rb1c[:], 0.0).then_inc(s_pad, 1)
            pool.wait_ge(s_const, 1)
            pool.tensor_copy(identb[:], ident[:]).then_inc(s_const, 1)
            step(pool.memset(maskb[:], 0.0))
            pool.affine_select(out=maskb[:], in_=maskb[:], compare_op=ALU.is_ge, fill=MASKED, base=0,
                               pattern=[[-1, P]], channel_multiplier=1).then_inc(s_const, 1)
            pool.iota(iota[:], [[1, 32]], base=0, channel_multiplier=0,
                      allow_small_or_imprecise_dtypes=True).then_inc(s_const, 1)
            pool.memset(onesb[:], 1.0).then_inc(s_const, 1)
            pool.wait_ge(s_const, 5)
            pool.affine_select(out=trib[:], in_=onesb[:], compare_op=ALU.is_ge, fill=0.0, base=0,
                               pattern=[[1, P]], channel_multiplier=-1).then_inc(s_const, 1)
            pool.wait_ge(s_wh, 1)
            pool.tensor_tensor(WA[:, 0, 1], WQ[:, 0:1024], WA[:, 0, 0].bitcast(F32), ALU.subtract).then_inc(s_wl, 1)
            pool.wait_ge(s_bo, 96)
            step(pool.tensor_tensor(bo2[:, 0], bo2[:, 0], bo2[:, 1], ALU.add))
            for j in range(NT):
                pool.wait_ge(s_xn, j + 1)
                pool.tensor_tensor(X[:, j], X[:, j], bo2[:, 0], ALU.add).then_inc(s_xb, 1)
            pool.wait_ge(s_ol, 2 * NT)
            pool.memset(region(30720, 512), MASKED).then_inc(s_pad, 1)
            pool.memset(SGR[:, :, :, FS:FP], 0.0).then_inc(s_pd, 1)
            for i in range(2):
                pool.memset(WD[i][:, :, 1], 0.0).then_inc(s_pe, 1)
            pool.memset(HTE, 0.0).then_inc(s_pe, 1)
            pool.wait_ge(s_yh, 2 * NT)
            pool.memset(SD[:, FC - 1], 0.0).then_inc(s_ps, 1)
            pool.memset(WD[2][:, :, 1], 0.0).then_inc(s_pe, 1)
            for f in range(2):
                for k in range(4):
                    m = 4 * f + k
                    if k == 0:
                        pool.wait_ge(s_qc, NT - 1 + f)
                    if m >= 2:
                        pool.wait_ge(s_sr, m - 1)
                    kk = QS[:, 2 * k + f, 0:QKV].rearrange("p (g n) -> p g n", g=G1)[:, :, None, GW - 2 * D1:GW - D1].to_broadcast([P, G1, 4, D1])
                    for i in range(k, 4):
                        q = QS[:, 2 * i + f, 0:QKV].rearrange("p (g n) -> p g n", g=G1)[:, :, 0:4 * D1].rearrange("p g (r d) -> p g r d", r=4)
                        pool.tensor_tensor(PR[m % 2][:, i].rearrange("p (g r d) -> p g r d", g=G1, r=4), q, kk, ALU.mult).then_inc(s_pp, 1)
            pool.wait_ge(s_di, NT)
            pool.memset(WD[3][:, :, 1], 0.0).then_inc(s_pe, 1)
            chain = 0
            for f in range(2):
                pool.wait_ge(s_ap, 1)
                for i in range(4):
                    j = 2 * i + f
                    for k in range(i + 1):
                        v = QS[:, 2 * k + f, 0:QKV].rearrange("p (g n) -> p g n", g=G1)[:, :, None, GW - D1:GW].to_broadcast([P, G1, 4, D1])
                        p = SC[:, f, i, :, k].rearrange("p (g r) -> p g r", g=G1)[:, :, :, None].to_broadcast([P, G1, 4, D1])
                        dst = AO[:, j] if k == 0 else pvt[:]
                        pool.tensor_tensor(dst.rearrange("p (g r d) -> p g r d", g=G1, r=4), p, v, ALU.mult).then_inc(s_pv, 1)
                        chain += 1
                        pool.wait_ge(s_pv, chain)
                        if k:
                            pool.tensor_tensor(AO[:, j], AO[:, j], pvt[:], ALU.add).then_inc(s_pv, 1)
                            chain += 1
                            pool.wait_ge(s_pv, chain)
            pool.wait_ge(s_ix, 1)
            pool.wait_ge(s_dn, GR)
            pool.wait_ge(s_er, 16 * GR)
            for j in range(NT):
                for k in range(K1):
                    pool.indirect_dma_start(G[:, j, k], None, rows, bass.IndirectOffsetOnAxis(ap=idx[:, j, k:k + 1], axis=0)).then_inc(s_g[j], 16)

        @block.scalar
        def _(act):
            def w_high(n, raw):
                if n >= 2:
                    act.wait_ge(s_qf, 8 * (n - 1)) if n < 6 else act.wait_ge(s_kf, 8 * (n - 5))
                nc.scalar.activation(WA[:, n % 2, 0], raw, ACT.Copy).then_inc(s_wh, 1)

            def deviations(half):
                act.wait_ge(s_var, half + 1)
                nc.scalar.activation(rstd[:, 4 * half:4 * half + 4], mv[:, 4 * half:4 * half + 4, 1], ACT.Sqrt).then_inc(s_std, 1)

            deviations(0)
            act.wait_ge(s_wq[0], 16)
            w_high(0, WQv[:, 0])
            for f in range(4):
                half, c = f // 2, f % 2
                if f == 2:
                    deviations(1)
                act.wait_ge(s_xt, f + 1)
                nc.scalar.activation(XTh[:, c, 512 * half:512 * half + 512], pb[4 + f][:], ACT.Copy).then_inc(s_xth, 1)
                nc.scalar.activation(XT[:, c, 512 * half:512 * half + 512], pb[4 + f][:], ACT.Copy).then_inc(s_xtc, 1)
            act.wait_ge(s_vc, 2)

            def q_copy(n):
                blk, half = 4 * (n // 8) + n % 4, n // 4 % 2
                act.wait_ge(s_qf, n + 1)
                nc.scalar.activation(QOb[:, :, 2 * half:2 * half + 2, :, blk].rearrange("p h b t -> p b h t"),
                                     pb[n % 4][:].rearrange("p (b h t) -> p b h t", b=2, h=H),
                                     ACT.Identity, bias=bqs[:, blk:blk + 1], scale=SCALE).then_inc(s_qa, 1)

            def weight_copy(n, dst, src):
                act.wait_ge(s_t, n)
                nc.scalar.activation(dst, src, ACT.Copy).then_inc(s_tc, 1)

            for g in range(4):
                if g < 3:
                    act.wait_ge(s_wq[g + 1], 16)
                    w_high(g + 1, WQv[:, g + 1])
                else:
                    act.wait_ge(s_kv, 32)
                    w_high(4, KVR.rearrange("p a c n -> p (a c n)"))
                for n in range(8 * g, 8 * g + 8, 2):
                    q_copy(n)
                    if n == 2:
                        act.wait_ge(s_t, 2)
                        act.wait_ge(s_pad, 3)
                        nc.scalar.activation(R1T[:, :, 0:HID], pb[5][:, 0:2 * HID].rearrange("p (c n) -> p c n", c=C), ACT.Copy).then_inc(s_tc, 1)
                        nc.scalar.activation(R2T[0:HID, :], pb[5][0:HID, 256:256 + E0], ACT.Copy).then_inc(s_tc, 1)
                if g == 0:
                    act.wait_ge(s_r, 80)
                    for half in range(2):
                        act.wait_ge(s_ht, half + 1)
                        nc.scalar.activation(HT[:, 512 * half:512 * half + 512], pb[6 + half][:], ACT.Silu, bias=rb1c[:]).then_inc(s_hs, 1)
                if g == 1:
                    for i, dst in enumerate((WT, AT, B2)):
                        weight_copy(3 + i, dst.rearrange("p c n -> p (c n)"), pb[5 + i][:])
                if g == 2:
                    act.wait_ge(s_df, 1)
                    nc.scalar.activation(p01[:, 1], p01[:, 0], ACT.Exp).then_inc(s_ex, 1)
                    weight_copy(6, QW[:, 0, 0:QKV], pb[5][:, 0:QKV])
                    weight_copy(7, QW[:, 1, 0:QKV], pb[6][:, 0:QKV])
                    weight_copy(8, projT[:].rearrange("p c n -> p (c n)"), pb[7][:])
            act.wait_ge(s_kv, 64)
            w_high(5, KVR.rearrange("p a c n -> p (a c n)"))
            for f in range(4):
                act.wait_ge(s_wxt, f + 1)
                nc.scalar.activation(WXT[:, f // 2, 512 * (f % 2):512 * (f % 2) + 512], pb[4 + f % 2][:], ACT.Copy).then_inc(s_wxc, 1)
            act.wait_ge(s_kv, 96)
            w_high(6, KVR.rearrange("p a c n -> p (a c n)"))

            def exps(u):
                i = u % 2
                act.wait_ge(s_m, u + 1)
                if u >= 2:
                    act.wait_ge(s_T, u - 1)
                nc.scalar.activation(Pb[:, i, 0:128], pb[i][:, 0:128], ACT.Exp, bias=nmax[:, i, 0:1],
                                     accum_out=psumr[:, i, 0:1])
                nc.scalar.activation(Pb[:, i, 128:384], pb[i][:, 128:384], ACT.Exp, bias=nmax[:, i, 1:2],
                                     accum_out=psumr[:, i, 1:2]).then_inc(s_e, 1)

            def t_copy(u):
                act.wait_ge(s_T, u + 1)
                if u >= 2:
                    act.wait_ge(s_O, u - 1)
                nc.scalar.activation(PTb[:, u % 2], pb[2 + u % 2][:, 0:384], ACT.Copy).then_inc(s_Tc, 1)

            def o_copy(u):
                _, _, b, h = unit(u)
                act.wait_ge(s_O, u + 1)
                nc.scalar.activation(QO[:, h, b], pb[4 + u % 2][:, 0:256], ACT.Identity,
                                     bias=VC[:, 32 + h:33 + h]).then_inc(s_Oc, 1)

            def wo_high(n):
                if n == 0:
                    act.wait_ge(s_wo, 16)
                if n == 4:
                    act.wait_ge(s_kf, 8 * PAIRS)
                nc.scalar.activation(WOP[n // 4][:, 0, 2 * (n % 4):2 * (n % 4) + 2], WOv[:, 2 * n:2 * n + 2], ACT.Copy).then_inc(s_woh, 1)

            def o_high(n):
                j = n // 2
                if n < 4:
                    act.wait_ge(s_S if n < 2 else s_O, UNITS - 8 * (1 - n % 2))
                    act.wait_ge(s_Oc, UNITS // 2 if n % 2 == 0 else UNITS - 3 + j)
                else:
                    act.wait_ge(s_yh, place(n - 4))
                nc.scalar.activation(OS[:, n % 4, 0], QO[:, 8 * (n % 2):8 * (n % 2) + 8, j // 2, P * (j % 2):P * (j % 2) + P],
                                     ACT.Copy).then_inc(s_oh, 1)

            exps(0)
            exps(1)
            t_copy(0)
            for u in range(UNITS):
                if u >= 1:
                    o_copy(u - 1)
                if u + 2 < UNITS:
                    exps(u + 2)
                if u + 1 < UNITS:
                    t_copy(u + 1)
                if u in WO_AT:
                    wo_high(WO_AT.index(u))
                if u in O_AT:
                    o_high(O_AT[u])
                if u % 8 == 5 and u // 8 + 3 < PAIRS:
                    act.wait_ge(s_kv, 32 * (u // 8 + 4))
                    w_high(4 + u // 8 + 3, KVR.rearrange("p a c n -> p (a c n)"))
            o_copy(UNITS - 1)
            def t2_copy(j):
                js = slice(P * j, P * j + P)
                act.wait_ge(s_t2, j + 1)
                src = pb[4 + j % 2][:, 0:D].rearrange("p (c n) -> p c n", c=C)
                nc.scalar.activation(XT[:, :, js], src, ACT.Copy).then_inc(s_c2, 1)
                nc.scalar.activation(XTh[:, :, js], src, ACT.Copy).then_inc(s_h2, 1)

            def q_out(j):
                act.wait_ge(s_qk, j + 1)
                nc.scalar.activation(QS[:, j, 0:QKV + E1 + 1], pb[6 + j % 2][:, 0:QKV + E1 + 1], ACT.Copy).then_inc(s_qc, 1)

            def g_high(m):
                if m >= 2:
                    act.wait_ge(s_sf, 2 * shared.index((m - 2, 1)) + 2)
                nc.scalar.activation(SG[:, m % 2, 0], SGR[:, :, :, P * m:P * m + P], ACT.Copy).then_inc(s_gh, 1)

            o_high(3)
            for j in range(NT):
                if 2 * j + 4 < 2 * NT:
                    o_high(2 * j + 4)
                if j >= 1:
                    t2_copy(j - 1)
                    if j == NT - 1:
                        act.wait_ge(s_sg, 32)
                        act.wait_ge(s_yh, place(12))
                        g_high(0)
                    q_out(j - 1)
                act.wait_ge(s_va2, j + 1)
                nc.scalar.activation(rstd[:, j:j + 1], mv[:, j, 1:2], ACT.Sqrt).then_inc(s_sd2, 1)
                if 2 * j + 5 < 2 * NT:
                    o_high(2 * j + 5)

            def silu(q):
                m, half = shared[q]
                act.wait_ge(s_sf, 2 * q + 1)
                nc.scalar.activation(ACTT[m][:, 512 * half:512 * half + 512], pb[2 * (q % 2)][:], ACT.Silu).then_inc(s_ss, 1)

            g_high(1)
            def xr_high(i):
                act.wait_ge(s_yh, 2 * NT)
                act.wait_ge(s_xn2, 4 * i + 4)
                nc.scalar.activation(XRh[:, 4 * i:4 * i + 4], XN2[:, 4 * i:4 * i + 4], ACT.Copy).then_inc(s_xr, 1)

            silu(0)
            t2_copy(NT - 1)
            xr_high(0)
            q_out(NT - 1)
            silu(1)
            xr_high(1)
            for q in range(2, 4):
                silu(q)
                g_high(q)
            act.wait_ge(s_d1, 1)
            nc.scalar.activation(w4[:], w4[:], ACT.Exp).then_inc(s_e1, 1)
            nc.scalar.activation(sig[:], QS[:, :, QKV + E1], ACT.Exp, scale=-1.0).then_inc(s_e1, 1)
            for half in range(2):
                act.wait_ge(s_di, NT)
                nc.scalar.activation(XE[:, 0, 512 * half:512 * half + 512], pb[4 + half][:], ACT.Copy).then_inc(s_xe, 1)
            act.wait_ge(s_am, 1)
            nc.scalar.activation(SCf, SCf, ACT.Exp, scale=SCALE1).then_inc(s_ae, 1)
            act.wait_ge(s_pe, 3)
            for what, n in EXPERT_STEPS:
                if what == "shared":
                    q, k = n
                    if k == 0:
                        silu(q)
                    elif q in (5, 7):
                        g_high(4 + (q - 5) // 2)
                if what == "up":
                    act.wait_ge(s_up, n + 1)
                    if n >= 2:
                        act.wait_ge(s_et, n - 1)
                    nc.scalar.activation(HE[:, n % 2], pb[4 + n % 2][:, 0:F1], ACT.Silu).then_inc(s_es, 1)
                if what == "turn":
                    act.wait_ge(s_et, n + 1)
                    if n >= 2:
                        act.wait_ge(s_dn, n - 1)
                    nc.scalar.activation(HTE[:, n % 2, 0], pb[6][:, 0:P], ACT.Copy)
                    nc.scalar.activation(HTE[0:F1 - P, n % 2, 1], pb[6][0:F1 - P, P:2 * P], ACT.Copy).then_inc(s_ec, 1)
            for f in range(4):
                act.wait_ge(s_at, f + 1)
                nc.scalar.activation(AOT[:, f // 2, 512 * (f % 2):512 * (f % 2) + 512], pb[4 + f][:], ACT.Copy).then_inc(s_ac, 1)

        @block.tensor
        def _(pe):
            def mm3(dst, wh, wl, xh, xl, start, stop):
                pe.matmul(dst, wh, xl, start=start, stop=False)
                pe.matmul(dst, wl, xh, start=False, stop=False)
                return pe.matmul(dst, wh, xh, start=False, stop=stop)

            pe.wait_ge(s_const, 1)

            def tokens_turn(f):
                half, c = f // 2, f % 2
                for i in range(4):
                    j = 4 * half + i
                    if c == 0:
                        pe.wait_ge(s_xn, j + 1)
                    ins = pe.transpose(pb[4 + f][:, P * i:P * i + P], XN[:, j, P * c:P * c + P], ident[:])
                ins.then_inc(s_xt, 1)

            def router_turn():
                pe.wait_ge(s_r, 80)
                for c in range(C):
                    pe.transpose(pb[5][:, HID * c:HID * c + HID], stR1[:, P * c:P * c + P], ident[0:HID, 0:HID])
                pe.transpose(pb[5][0:HID, 256:256 + E0], stR2, ident[0:E0, 0:E0]).then_inc(s_t, 1)

            def router_hidden():
                pe.wait_ge(s_tc, 2)
                for half in range(2):
                    for c in range(C):
                        ins = pe.matmul(pb[6 + half][:], R1T[:, c], XT[:, c, 512 * half:512 * half + 512],
                                        start=(c == 0), stop=(c == C - 1))
                    ins.then_inc(s_ht, 1)

            def router_logits():
                pe.wait_ge(s_hs, 2)
                pe.wait_ge(s_vc, 2)
                for j in range(NT):
                    ins = pe.matmul(pb[4][:, E0 * j:E0 * j + E0], HT[:, P * j:P * j + P], R2T[:], start=True, stop=True)
                ins.then_inc(s_lg, 1)

            def square(bank, st):
                for c in range(C):
                    for o in range(2):
                        ins = pe.transpose(pb[bank][:, 256 * c + P * o:256 * c + P * o + P], st[:, o, P * c:P * c + P], ident[:])
                ins.then_inc(s_t, 1)

            def queries(n):
                g, half, blk = n // 8, n // 4 % 2, n % 4
                pe.wait_ge(s_wh, g + 1)
                pe.wait_ge(s_wl, g + 1)
                if n >= 4:
                    pe.wait_ge(s_qa if n % 2 == 0 else s_qd, n // 2 - 1)
                wh = WA[:, g % 2, 0].rearrange("p (c n) -> p c n", c=C)
                wl = WA[:, g % 2, 1].rearrange("p (c n) -> p c n", c=C)
                xs = slice(512 * half, 512 * half + 512)
                for c in range(C):
                    pe.wait_ge(s_xtl, 2 * half + c + 1)
                    ins = mm3(pb[n % 4][:], wh[:, c, P * blk:P * blk + P], wl[:, c, P * blk:P * blk + P],
                              XTh[:, c, xs], XTl[:, c, xs], c == 0, c == C - 1)
                ins.then_inc(s_qf, 1)

            tokens_turn(0)
            tokens_turn(1)
            queries(0)
            queries(1)
            tokens_turn(2)
            tokens_turn(3)
            pe.wait_ge(s_vb, 48)
            pe.wait_ge(s_xtc, 1)
            pe.transpose(pb[4][:, 0:48], VB, ident[0:48, 0:48]).then_inc(s_t, 1)
            queries(2)
            queries(3)
            router_turn()
            for n in range(4, 8):
                queries(n)
            router_hidden()
            for n in range(8, 16):
                queries(n)
            router_logits()
            pe.wait_ge(s_sw, 96)
            square(5, stW)
            square(6, stA)
            square(7, stBf)
            for n in range(16, 24):
                queries(n)
            pe.wait_ge(s_tc, 5)
            for c in range(C):
                for o in range(3):
                    ins = pe.transpose(pb[5 + c][:, P * o:P * o + P], stQKV[:, o, P * c:P * c + P], ident[:])
                ins.then_inc(s_t, 1)
            square(7, stP)
            for n in range(24, 32):
                queries(n)

            def experts_in():
                pe.wait_ge(s_qa, 16)
                pe.wait_ge(s_qd, 16)
                for j in range(NT):
                    for c in range(C):
                        ins = pe.matmul(pb[j // 2][:, 256 * (j % 2):256 * (j % 2) + 256], XT[:, c, P * j:P * j + P],
                                        AT[:, c], start=(c == 0), stop=(c == C - 1))
                    ins.then_inc(s_xa, 1)

            def experts_turn(c):
                pe.wait_ge(s_wxa, NT)
                if c == 0:
                    pe.wait_ge(s_lc, 1)
                else:
                    pe.wait_ge(s_wxc, 2)
                for half in range(2):
                    for i in range(4):
                        ins = pe.transpose(pb[4 + half][:, P * i:P * i + P], WXA[:, 4 * half + i, P * c:P * c + P], ident[:])
                    ins.then_inc(s_wxt, 1)

            def fill(n):
                p, f = n // 8, n % 8
                if f == 0:
                    pe.wait_ge(s_wh, 5 + p)
                    pe.wait_ge(s_wl, 5 + p)
                if n >= 2:
                    pe.wait_ge(s_kc, n - 1)
                bank = pb[6 + n % 2]
                wh = WA[:, p % 2, 0].rearrange("p (a c n) -> p a c n", a=2, c=C)
                wl = WA[:, p % 2, 1].rearrange("p (a c n) -> p a c n", a=2, c=C)
                if f < 4:
                    hh, xs = f // 2, slice(512 * (f % 2), 512 * (f % 2) + 512)
                    for c in range(C):
                        ins = mm3(bank[:], wh[:, 0, c, P * hh:P * hh + P], wl[:, 0, c, P * hh:P * hh + P],
                                  XTh[:, c, xs], XTl[:, c, xs], c == 0, c == C - 1)
                else:
                    for i in range(2):
                        j = 2 * (f - 4) + i
                        for c in range(C):
                            ins = mm3(bank[:, 256 * i:256 * i + 256], XTh[:, c, P * j:P * j + P], XTl[:, c, P * j:P * j + P],
                                      wh[:, 1, c], wl[:, 1, c], c == 0, c == C - 1)
                ins.then_inc(s_kf, 1)

            def scores(u):
                p, hh, b, h = unit(u)
                if u % 8 == 0:
                    pe.wait_ge(s_kc, 8 * p + 8)
                if u >= 2:
                    pe.wait_ge(s_e, u - 1)
                s, k = pb[u % 2], KT[:, p % 2, hh]
                pe.matmul(s[:, 0:128], QO[:, h, b, 0:128], k[:, T * b:T * b + 128], start=True, stop=False)
                pe.matmul(s[:, 0:128], identb[:], maskb[:], start=False, stop=True)
                pe.matmul(s[:, 128:384], QO[:, h, b, 128:256], k[:, T * b:T * b + 256], start=True, stop=False)
                pe.matmul(s[:, 256:384], identb[:], maskb[:], start=False, stop=True).then_inc(s_S, 1)

            def turn(u):
                pe.wait_ge(s_p, u + 1)
                if u >= 2:
                    pe.wait_ge(s_Tc, u - 1)
                for i in range(3):
                    ins = pe.transpose(pb[2 + u % 2][:, P * i:P * i + P], Pb[:, u % 2, P * i:P * i + P], ident[:])
                ins.then_inc(s_T, 1)

            def heads(u):
                p, hh, b, h = unit(u)
                pe.wait_ge(s_Tc, u + 1)
                if u >= 2:
                    pe.wait_ge(s_Oc, u - 1)
                o = pb[4 + u % 2][:, 0:256]
                pe.matmul(o, V[:, p % 2, 2 * b, P * hh:P * hh + P], PTb[:, u % 2, 0:256], start=True, stop=False)
                pe.matmul(o[:, 128:256], V[:, p % 2, 2 * b + 1, P * hh:P * hh + P], PTb[:, u % 2, 256:384],
                          start=False, stop=True).then_inc(s_O, 1)

            def turn2(j):
                pe.wait_ge(s_xn2, j + 1)
                if j >= 2:
                    pe.wait_ge(s_h2, j - 1)
                for c in range(C):
                    ins = pe.transpose(pb[4 + j % 2][:, P * c:P * c + P], XN2[:, j, P * c:P * c + P], ident[:])
                ins.then_inc(s_t2, 1)

            def qkv(j):
                pe.wait_ge(s_c2, j + 1)
                pe.wait_ge(s_x1, j + 1) if j < 2 else pe.wait_ge(s_qc, j - 1)
                for c in range(C):
                    ins = pe.matmul(pb[6 + j % 2][:, 0:QKV + E1 + 1], XT[:, c, P * j:P * j + P], QW[:, c],
                                    start=(c == 0), stop=(c == C - 1))
                ins.then_inc(s_qk, 1)

            def out_small(j, part):
                dst, t = pb[y_bank(j)][:, 0:D], slice(P * j, P * j + P)
                if j < 2:
                    pe.wait_ge(s_kc, 8 * PAIRS - 1 + j)
                elif j >= 6:
                    pe.wait_ge(s_x1, j - 3)
                l, r = ((XT, WT), (WXT, B2))[part]
                pe.matmul(dst, l[:, 0, t], r[:, 0], start=(part == 0), stop=False)
                pe.matmul(dst, l[:, 1, t], r[:, 1], start=False, stop=False)

            def out_heads(n, part):
                j, k = n // 2, n % 2
                pe.wait_ge(s_oh, place(n))
                pe.wait_ge(s_ol, place(n))
                pe.wait_ge(s_wol, 4 * k + 4)
                for h in range(4 * part, 4 * part + 4):
                    ins = mm3(pb[y_bank(j)][:, 0:D], OS[:, n % 4, 0, h], OS[:, n % 4, 1, h],
                              WOP[k][:, 0, h], WOP[k][:, 1, h], False, k == 1 and h == H // 2 - 1)
                if part == 1:
                    ins.then_inc(s_yh, 1)

            FIRST_OUT = {54: lambda: out_small(0, 0), 55: lambda: out_small(0, 1),
                         56: lambda: out_small(1, 0), 57: lambda: out_small(1, 1),
                         58: lambda: out_heads(0, 0), 59: lambda: out_heads(0, 1),
                         60: lambda: out_heads(2, 0), 61: lambda: out_heads(2, 1)}

            pe.wait_ge(s_tc, 8)
            for n in range(AHEAD):
                fill(n)
                if n == 1:
                    experts_in()
                if n == 3:
                    experts_turn(0)
                if n == 5:
                    experts_turn(1)
            pe.wait_ge(s_wxa, NT)
            pe.wait_ge(s_wxc, 4)
            pe.wait_ge(s_const, 3)
            scores(0)
            scores(1)
            turn(0)
            for u in range(UNITS):
                if u + 2 < UNITS:
                    scores(u + 2)
                if u + 1 < UNITS:
                    turn(u + 1)
                heads(u)
                if u + AHEAD < UNITS:
                    fill(u + AHEAD)
                elif u in FIRST_OUT:
                    FIRST_OUT[u]()

            pe.wait_ge(s_Tc, UNITS)
            pe.wait_ge(s_e, UNITS)
            out_small(2, 0)
            out_small(2, 1)
            for j in range(NT):
                if j >= 2:
                    out_heads(2 * j, 0)
                    out_heads(2 * j, 1)
                out_heads(2 * j + 1, 0)
                if j >= 1:
                    turn2(j - 1)
                out_heads(2 * j + 1, 1)
                if j >= 1:
                    qkv(j - 1)
                if 3 <= j + 3 < NT:
                    out_small(j + 3, 0)
                    out_small(j + 3, 1)
            def shared_up(q, k):
                m, half = shared[q]
                pe.wait_ge(s_gh, m + 1)
                pe.wait_ge(s_gl, m + 1)
                pe.wait_ge(s_l2, 4 * half + 4)
                pe.wait_ge(s_h2, 4 * half + 4)
                if q >= 2:
                    pe.wait_ge(s_sm if k else s_ss, q - 1)
                xs = slice(512 * half, 512 * half + 512)
                for c in range(C):
                    ins = mm3(pb[2 * (q % 2) + k][:], SG[:, m % 2, 0, k, c], SG[:, m % 2, 1, k, c],
                              XTh[:, c, xs], XTl[:, c, xs], c == 0, c == C - 1)
                ins.then_inc(s_sf, 1)

            pe.wait_ge(s_x1, NT - 2)
            shared_up(0, 0)
            shared_up(0, 1)
            turn2(NT - 1)
            pe.wait_ge(s_x1, NT)
            shared_up(1, 0)
            qkv(NT - 1)
            shared_up(1, 1)
            shared_up(2, 0)
            shared_up(2, 1)
            pe.wait_ge(s_sel, 1)
            pe.wait_ge(s_qc, NT)
            for j in range(NT):
                for i in range(j + 1):
                    ins = pe.matmul(pb[6][:, E1 * j:E1 * j + E1], (trib if i == j else onesb)[:], selb[:, i],
                                    start=(i == 0), stop=(i == j))
            ins.then_inc(s_po, 1)
            shared_up(3, 0)
            shared_up(3, 1)
            for j in range(NT):
                pe.wait_ge(s_dm, j + 1)
                pe.wait_ge(s_xr, j // 4 + 1)
                pe.wait_ge(s_xrl, j // 4 + 1)
                for k in range(4):
                    c, half = k // 2, k % 2
                    for n, xr in enumerate((XRh, XRl)):
                        ins = pe.matmul(pb[4 + k][:], xr[:, j, P * c:P * c + P], DM[:, j % 2, 512 * half:512 * half + 512],
                                        start=(j == 0 and n == 0), stop=(j == NT - 1 and n == 1))
                ins.then_inc(s_di, 1)

            def expert_up(g):
                i = g % PLACES
                pe.wait_ge(s_ew[i], 32 * len(WGU[i]) * (g // PLACES + 1))
                pe.wait_ge(s_xe, g // 4 + 1)
                pe.wait_ge(s_xd, g // 4 + 1)
                if g == 1:
                    pe.wait_ge(s_xe, 2)
                if g >= 2:
                    pe.wait_ge(s_eh, g - 1)
                for c in range(C):
                    for e in range(EPG):
                        s = slice(CAP * (EPG * g + e), CAP * (EPG * g + e) + CAP)
                        ins = pe.matmul(pb[4 + g % 2][CAP * e:CAP * e + CAP, 0:2 * F1], XE[:, c, s], up_weights(g, e)[:, c],
                                        start=(c == 0), stop=(c == C - 1), skip_group_check=True)
                ins.then_inc(s_up, 1)

            def expert_turn(g):
                pe.wait_ge(s_eh, g + 1)
                if g >= 1:
                    pe.wait_ge(s_ec, g)
                pe.transpose(pb[6][:, 0:P], HE[:, g % 2, 0:P], ident[:])
                pe.transpose(pb[6][0:F1 - P, P:2 * P], HE[:, g % 2, P:F1], ident[:]).then_inc(s_et, 1)

            def expert_down(g):
                pe.wait_ge(s_ec, g + 1)
                pe.wait_ge(s_ed[g % PLACES], 32 * (g // PLACES + 1))
                if g == 0:
                    pe.wait_ge(s_xd, 2)
                if g >= 1:
                    pe.wait_ge(s_ye, g)
                for k in range(2):
                    for e in range(EPG):
                        ins = pe.matmul(pb[7][CAP * e:CAP * e + CAP, 0:D], HTE[:, g % 2, k, CAP * e:CAP * e + CAP],
                                        WD[g % PLACES][:, e, k], start=(k == 0), stop=(k == 1), skip_group_check=True)
                ins.then_inc(s_dn, 1)

            def shared_down(j):
                if j >= 4:
                    pe.wait_ge(s_x2, j - 3)
                for m in range(FC):
                    ins = pe.matmul(pb[j % 4][:, 0:D], ACTT[m][:, P * j:P * j + P], SD[:, m], start=(m == 0), stop=(m == FC - 1))
                ins.then_inc(s_sh, 1)

            for what, n in EXPERT_STEPS:
                if what == "shared":
                    shared_up(*n)
                if what == "up":
                    expert_up(n)
                if what == "turn":
                    expert_turn(n)
                if what == "down":
                    expert_down(n)
            pe.wait_ge(s_sd, 32)
            pe.wait_ge(s_sm, len(shared))
            for j in range(4):
                shared_down(j)
            pe.wait_ge(s_ye, GR)
            pe.wait_ge(s_pv, 32)
            for f in range(4):
                c, half = f // 2, f % 2
                for i in range(4):
                    ins = pe.transpose(pb[4 + f][:, P * i:P * i + P], AO[:, 4 * half + i, P * c:P * c + P], ident[:])
                ins.then_inc(s_at, 1)
            for j in range(4, NT):
                shared_down(j)
            pe.wait_ge(s_ac, 4)
            for j in range(NT):
                if j >= 4:
                    pe.wait_ge(s_pa, j - 3)
                for c in range(C):
                    ins = pe.matmul(pb[4 + j % 4][:, 0:D], AOT[:, c, P * j:P * j + P], projT[:, c], start=(c == 0), stop=(c == C - 1))
                ins.then_inc(s_fo, 1)

        @block.vector
        def _(dve):
            steps = [0]

            def step(ins):
                ins.then_inc(s_dv, 1)
                steps[0] += 1
                dve.wait_ge(s_dv, steps[0])

            def stats_of(half):
                js = range(4 * half, 4 * half + 4)
                for j in js:
                    dve.wait_ge(s_x[j // 2], 16)
                    nc.vector.bn_stats(stats[:, j], X[:, j]).then_inc(s_st, 1)
                dve.wait_ge(s_st, 4 * half + 4)
                for j in js:
                    ins = nc.vector.bn_aggr(mv[:, j], stats[:, j])
                step(ins)
                nc.vector.tensor_scalar(mv[:, 4 * half:4 * half + 4, 1], mv[:, 4 * half:4 * half + 4, 1], EPS, None,
                                        ALU.add).then_inc(s_var, 1)

            def norm(half):
                dve.wait_ge(s_std, half + 1)
                step(nc.vector.reciprocal(rstd[:, 4 * half:4 * half + 4], rstd[:, 4 * half:4 * half + 4]))
                for j in range(4 * half, 4 * half + 4):
                    nc.vector.tensor_scalar(XN[:, j], X[:, j], mv[:, j, 0:1], rstd[:, j:j + 1],
                                            ALU.subtract, ALU.mult).then_inc(s_xn, 1)

            def w_low(n, raw):
                if n >= 2:
                    dve.wait_ge(s_qf, 8 * (n - 1)) if n < 6 else dve.wait_ge(s_kf, 8 * (n - 5))
                dve.wait_ge(s_wh, n + 1)
                nc.vector.tensor_tensor(WA[:, n % 2, 1], raw, WA[:, n % 2, 0].bitcast(F32), ALU.subtract).then_inc(s_wl, 1)

            kvraw = KVR.rearrange("p a c n -> p (a c n)")
            wqraw = lambda g: WQ[:, 1024 * g:1024 * g + 1024]

            def tokens_low(f):
                half, c = f // 2, f % 2
                xs = slice(512 * half, 512 * half + 512)
                dve.wait_ge(s_xtc, f + 1)
                dve.wait_ge(s_xth, f + 1)
                nc.vector.tensor_tensor(XTl[:, c, xs], XT[:, c, xs], XTh[:, c, xs].bitcast(F32), ALU.subtract).then_inc(s_xtl, 1)

            stats_of(0)
            norm(0)
            stats_of(1)
            tokens_low(0)
            tokens_low(1)
            norm(1)
            dve.wait_ge(s_t, 1)
            nc.vector.tensor_copy(VC[:], pb[4][:, 0:48]).then_inc(s_vc, 1)
            dve.wait_ge(s_vc, 1)
            nc.vector.tensor_scalar(bqs[:], VC[:, 0:H], SCALE, None, ALU.mult).then_inc(s_vc, 1)
            tokens_low(2)
            tokens_low(3)
            dve.wait_ge(s_wl, 1)
            w_low(1, wqraw(1))

            def router():
                dve.wait_ge(s_r, 80)
                step(nc.vector.tensor_tensor(rg[:, 0], rg[:, 0], rg[:, 1], ALU.add))
                dve.wait_ge(s_lg, 1)
                nc.vector.tensor_tensor(lg[:], pb[4][:, 0:NT * E0].rearrange("p (j e) -> p j e", j=NT),
                                        rg[:, 0:1].to_broadcast([P, NT, E0]), ALU.add).then_inc(s_lc, 1)
                dve.wait_ge(s_lc, 1)
                for j in range(NT):
                    ins = nc.vector.max(top[:, j], lg[:, j])
                step(ins)
                for j in range(NT):
                    ins = nc.vector.max_index(topi[:, j], top[:, j], lg[:, j])
                step(ins)
                step(nc.vector.tensor_copy(topf[:], topi[:]))
                nc.vector.tensor_tensor(p01[:, 0], top[:, :, 1], top[:, :, 0], ALU.subtract).then_inc(s_df, 1)

            def q_copy(n):
                blk, half = 4 * (n // 8) + n % 4, n // 4 % 2
                dve.wait_ge(s_qf, n + 1)
                nc.vector.tensor_scalar(QOb[:, :, 2 * half:2 * half + 2, :, blk].rearrange("p h b t -> p b h t"),
                                        pb[n % 4][:].rearrange("p (b h t) -> p b h t", b=2, h=H),
                                        SCALE, bqs[:, blk:blk + 1], ALU.mult, ALU.add).then_inc(s_qd, 1)

            def chosen(k):
                return (iota[:, None, 0:E0].to_broadcast([P, NT, E0]), topf[:, :, k:k + 1].to_broadcast([P, NT, E0]))

            for g in range(4):
                if g == 3:
                    w_low(4, kvraw)
                elif g >= 1:
                    w_low(g + 1, wqraw(g + 1))
                for n in range(8 * g + 1, 8 * g + 8, 2):
                    q_copy(n)
                if g == 1:
                    router()
                if g == 2:
                    dve.wait_ge(s_ex, 1)
                    step(nc.vector.tensor_scalar(p01[:, 0], p01[:, 1], 1.0, None, ALU.add))
                    step(nc.vector.reciprocal(p01[:, 0], p01[:, 0]))
                    step(nc.vector.tensor_tensor(p01[:, 1], p01[:, 1], p01[:, 0], ALU.mult))
                    dve.wait_ge(s_const, 4)
                    for k in range(2):
                        i, t = chosen(k)
                        dst = coef if k == 0 else tmpk
                        step(nc.vector.tensor_tensor(dst[:], i, t, ALU.is_equal))
                        step(nc.vector.tensor_tensor(dst[:], dst[:], p01[:, k, :, None].to_broadcast([P, NT, E0]), ALU.mult))
                    step(nc.vector.tensor_tensor(coef[:], coef[:], tmpk[:], ALU.add))

            def weigh(j):
                dve.wait_ge(s_xa, 2 * (j // 2) + 2)
                nc.vector.tensor_tensor(
                    WXA[:, j].rearrange("p (e r) -> p e r", e=E0),
                    pb[j // 2][:, 256 * (j % 2):256 * (j % 2) + 256].rearrange("p (e r) -> p e r", e=E0),
                    coef[:, j, :, None].to_broadcast([P, E0, RANK]), ALU.mult).then_inc(s_wxa, 1)

            def fill_copy(n):
                p, f = n // 8, n % 8
                dve.wait_ge(s_kf, n + 1)
                if f == 0 and p >= 2:
                    dve.wait_ge(s_S, 8 * (p - 1))
                if f == 4 and p >= 2:
                    dve.wait_ge(s_O, 8 * (p - 1))
                if f == 0 and p == 1:
                    dve.wait_ge(s_wxt, 4)
                if f == 0 and p == 0:
                    dve.wait_ge(s_xb, NT)
                if f < 4:
                    hh, ts = f // 2, slice(512 * (f % 2), 512 * (f % 2) + 512)
                    nc.vector.tensor_scalar(KT[:, p % 2, hh, ts], pb[6 + n % 2][:], VC[:, 16 + 2 * p + hh:17 + 2 * p + hh],
                                            None, ALU.add).then_inc(s_kc, 1)
                else:
                    nc.vector.tensor_copy(V[:, p % 2, 2 * (f - 4):2 * (f - 4) + 2].rearrange("p j n -> p (j n)"),
                                          pb[6 + n % 2][:]).then_inc(s_kc, 1)

            def max_of(u):
                i = u % 2
                dve.wait_ge(s_S, u + 1)
                nc.vector.tensor_reduce(nmax[:, i, 0:1], pb[i][:, 0:128], AX, ALU.max, negate=True)
                nc.vector.tensor_reduce(nmax[:, i, 1:2], pb[i][:, 128:384], AX, ALU.max, negate=True).then_inc(s_m, 1)

            def normalise(u):
                i = u % 2
                dve.wait_ge(s_e, u + 1)
                nc.vector.reciprocal(rinv[:, i], psumr[:, i]).then_inc(s_ri, 1)
                dve.wait_ge(s_ri, u + 1)
                nc.vector.tensor_scalar(Pb[:, i, 0:128], Pb[:, i, 0:128], rinv[:, i, 0:1], None, ALU.mult)
                nc.vector.tensor_scalar(Pb[:, i, 128:384], Pb[:, i, 128:384], rinv[:, i, 1:2], None, ALU.mult).then_inc(s_p, 1)

            w_low(5, kvraw)
            for n in range(AHEAD):
                fill_copy(n)
                if n in (1, 2):
                    for j in range(4 * (n - 1), 4 * n):
                        weigh(j)
                if n == 7:
                    w_low(6, kvraw)
            max_of(0)
            max_of(1)
            normalise(0)
            normalise(1)
            def wo_low(n):
                dve.wait_ge(s_woh, n + 1)
                k, hs = n // 4, slice(2 * (n % 4), 2 * (n % 4) + 2)
                nc.vector.tensor_tensor(WOP[k][:, 1, hs], WOv[:, 2 * n:2 * n + 2], WOP[k][:, 0, hs].bitcast(F32), ALU.subtract).then_inc(s_wol, 1)

            def o_low(n):
                j = n // 2
                dve.wait_ge(s_oh, place(n))
                nc.vector.tensor_tensor(OS[:, n % 4, 1], QO[:, 8 * (n % 2):8 * (n % 2) + 8, j // 2, P * (j % 2):P * (j % 2) + P],
                                        OS[:, n % 4, 0].bitcast(F32), ALU.subtract).then_inc(s_ol, 1)

            for u in range(UNITS):
                if u + 2 < UNITS:
                    max_of(u + 2)
                    normalise(u + 2)
                if u in WO_AT:
                    wo_low(WO_AT.index(u))
                if u in O_AT:
                    o_low(O_AT[u])
                if u + AHEAD < UNITS:
                    fill_copy(u + AHEAD)
                if u % 8 == 5 and u // 8 + 3 < PAIRS:
                    w_low(4 + u // 8 + 3, kvraw)

            def xt_low(j):
                js = slice(P * j, P * j + P)
                dve.wait_ge(s_h2, j + 1)
                nc.vector.tensor_tensor(XTl[:, :, js], XT[:, :, js], XTh[:, :, js].bitcast(F32), ALU.subtract).then_inc(s_l2, 1)

            def top_k(j0, j1, s_done):
                full = [P, j1 - j0, E1]
                for j in range(j0, j1):
                    ins = nc.vector.max(top1[:, j], QS[:, j, QKV:QKV + E1])
                step(ins)
                for j in range(j0, j1):
                    ins = nc.vector.max_index(topi1[:, j], top1[:, j], QS[:, j, QKV:QKV + E1])
                step(ins)
                step(nc.vector.tensor_copy(topf1[:, j0:j1], topi1[:, j0:j1]))
                for k in range(K1):
                    one = (sel if k == 0 else tmp1)[:, j0:j1]
                    step(nc.vector.tensor_tensor(one, iota[:, None, :].to_broadcast(full),
                                                 topf1[:, j0:j1, k:k + 1].to_broadcast(full), ALU.is_equal))
                    if k:
                        step(nc.vector.tensor_tensor(sel[:, j0:j1], sel[:, j0:j1], one, ALU.add))
                ins = nc.vector.tensor_copy(selb[:, j0:j1], sel[:, j0:j1])
                ins.then_inc(s_sel, 1) if s_done else step(ins)

            def g_low(m):
                dve.wait_ge(s_gh, m + 1)
                nc.vector.tensor_tensor(SG[:, m % 2, 1].rearrange("p a c n -> p (a c) n"),
                                        SGR[:, :, :, P * m:P * m + P].rearrange("p a c n -> p (a c) n"),
                                        SG[:, m % 2, 0].bitcast(F32).rearrange("p a c n -> p (a c) n"), ALU.subtract).then_inc(s_gl, 1)

            def sum_products(m):
                f, k = m // 4, m % 4
                dve.wait_ge(s_pp, 10 * f + (4, 7, 9, 10)[k])
                nc.vector.tensor_reduce(SC[:, f, k:4, :, k], PR[m % 2][:, k:4].rearrange("p i (h d) -> p i h d", h=H1),
                                        AX, ALU.add).then_inc(s_sr, 1)

            o_low(3)
            for j in range(NT):
                if 2 * j + 4 < 2 * NT:
                    o_low(2 * j + 4)
                if j >= 1:
                    xt_low(j - 1)
                if j == NT - 1:
                    g_low(0)
                dve.wait_ge(s_yh, place(2 * j + 1))
                dve.wait_ge(s_xb, j + 1)
                nc.vector.tensor_tensor(X[:, j], pb[y_bank(j)][:, 0:D], X[:, j], ALU.add).then_inc(s_x1, 1)
                dve.wait_ge(s_x1, j + 1)
                step(nc.vector.bn_stats(stats[:, j], X[:, j]))
                step(nc.vector.bn_aggr(mv[:, j], stats[:, j]))
                nc.vector.tensor_scalar(mv[:, j, 1:2], mv[:, j, 1:2], EPS, None, ALU.add).then_inc(s_va2, 1)
                dve.wait_ge(s_sd2, j + 1)
                step(nc.vector.reciprocal(rstd[:, j:j + 1], rstd[:, j:j + 1]))
                nc.vector.tensor_scalar(XN2[:, j], X[:, j], mv[:, j, 0:1], rstd[:, j:j + 1], ALU.subtract, ALU.mult).then_inc(s_xn2, 1)
                if 2 * j + 5 < 2 * NT:
                    o_low(2 * j + 5)
                if j == TOPK_FIRST:
                    dve.wait_ge(s_qc, TOPK_FIRST)
                    top_k(0, TOPK_FIRST, False)
            g_low(1)
            dve.wait_ge(s_pad, 4)
            sum_products(0)
            xt_low(NT - 1)

            def shared_product(q):
                m, half = shared[q]
                dst = ACTT[m][:, 512 * half:512 * half + 512]
                dve.wait_ge(s_ss, q + 1)
                dve.wait_ge(s_sf, 2 * q + 2)
                nc.vector.tensor_tensor(dst, dst, pb[2 * (q % 2) + 1][:], ALU.mult).then_inc(s_sm, 1)

            def slots_of(j):
                if j >= 2:
                    dve.wait_ge(s_di, j - 1)
                nc.vector.tensor_tensor(DM[:, j % 2].rearrange("p (e c) -> p e c", e=E1),
                                        posm[:, j, :, None].to_broadcast([P, E1, CAP]),
                                        iota[:, None, :].to_broadcast([P, E1, CAP]), ALU.is_equal).then_inc(s_dm, 1)

            def xr_low(i):
                dve.wait_ge(s_xr, i + 1)
                nc.vector.tensor_tensor(XRl[:, 4 * i:4 * i + 4], XN2[:, 4 * i:4 * i + 4], XRh[:, 4 * i:4 * i + 4].bitcast(F32),
                                        ALU.subtract).then_inc(s_xrl, 1)

            shared_product(0)
            sum_products(1)
            dve.wait_ge(s_qc, NT)
            top_k(TOPK_FIRST, NT, True)
            shared_product(1)
            xr_low(0)
            dve.wait_ge(s_po, 1)
            step(nc.vector.tensor_tensor(posm[:], pb[6][:, 0:NT * E1].rearrange("p (j e) -> p j e", j=NT), sel[:], ALU.mult))
            step(nc.vector.tensor_scalar(posm[:], posm[:], -1.0, None, ALU.add))
            slots_of(0)
            shared_product(2)
            slots_of(1)
            shared_product(3)
            nc.vector.tensor_tensor(w4[:], top1[:, :, 0:K1], top1[:, :, 0:1].to_broadcast([P, NT, K1]), ALU.subtract).then_inc(s_d1, 1)
            for j in range(2, NT):
                slots_of(j)
                if j == 2:
                    xr_low(1)
                if j in (5, 6):
                    g_low(j - 3)
                if j >= 3:
                    sum_products(j - 1)
            sum_products(7)
            dve.wait_ge(s_sr, 8)
            step(nc.vector.tensor_reduce(mx1[:], SCf, AX, ALU.max))
            nc.vector.tensor_tensor(SCf, SCf, mx1[:, :, None].to_broadcast([P, 128, 4]), ALU.subtract).then_inc(s_am, 1)
            for half in range(2):
                dve.wait_ge(s_di, NT)
                nc.vector.tensor_copy(XE[:, 1, 512 * half:512 * half + 512], pb[6 + half][:]).then_inc(s_xd, 1)
            dve.wait_ge(s_ae, 1)
            step(nc.vector.tensor_reduce(mx1[:], SCf, AX, ALU.add))
            step(nc.vector.reciprocal(mx1[:], mx1[:]))
            nc.vector.tensor_tensor(SCf, SCf, mx1[:, :, None].to_broadcast([P, 128, 4]), ALU.mult).then_inc(s_ap, 1)

            def gate_weights():
                dve.wait_ge(s_e1, 2)
                step(nc.vector.tensor_reduce(ws[:], w4[:], AX, ALU.add))
                step(nc.vector.reciprocal(ws[:], ws[:]))
                step(nc.vector.tensor_tensor(w4[:], w4[:], ws[:, :, None].to_broadcast([P, NT, K1]), ALU.mult))
                step(nc.vector.tensor_scalar(sig[:], sig[:], 1.0, None, ALU.add))
                step(nc.vector.reciprocal(sig[:], sig[:]))

            def place_with(k):
                full = [P, NT, E1]
                step(nc.vector.tensor_tensor(tmp1[:], iota[:, None, :].to_broadcast(full), topf1[:, :, k:k + 1].to_broadcast(full), ALU.is_equal))
                step(nc.vector.tensor_tensor(tmp1[:], tmp1[:], posm[:], ALU.mult))
                step(nc.vector.tensor_reduce(pk[:, :, k], tmp1[:], AX, ALU.add))

            def slot_indices():
                step(nc.vector.tensor_scalar(ok[:], pk[:], float(CAP), None, ALU.is_lt))
                step(nc.vector.tensor_tensor(w4[:], w4[:], ok[:], ALU.mult))
                step(nc.vector.tensor_scalar(pk[:], pk[:], float(CAP - 1), None, ALU.min))
                step(nc.vector.scalar_tensor_tensor(out=pk[:], in0=topf1[:, :, 0:K1], scalar=float(CAP), in1=pk[:],
                                                    op0=ALU.mult, op1=ALU.add))
                nc.vector.tensor_copy(idx[:], pk[:]).then_inc(s_ix, 1)

            for what, n in EXPERT_STEPS:
                if what == "shared":
                    q, k = n
                    if k == 1:
                        shared_product(q)
                        if q in (5, 7):
                            g_low(4 + (q - 5) // 2)
                if what == "up":
                    dve.wait_ge(s_es, n + 1)
                    nc.vector.tensor_tensor(HE[:, n % 2], HE[:, n % 2], pb[4 + n % 2][:, F1:2 * F1], ALU.mult).then_inc(s_eh, 1)
                if what == "down":
                    dve.wait_ge(s_dn, n + 1)
                    nc.vector.tensor_copy(YE[:, n], pb[7][:, 0:D]).then_inc(s_ye, 1)
                    if n == 0:
                        gate_weights()
                    elif n < 5:
                        place_with(n - 1)
                    elif n == 5:
                        slot_indices()

            def add_shared(j):
                dve.wait_ge(s_sh, j + 1)
                nc.vector.scalar_tensor_tensor(out=X[:, j], in0=pb[j % 4][:, 0:D], scalar=sig[:, j:j + 1], in1=X[:, j],
                                               op0=ALU.mult, op1=ALU.add).then_inc(s_x2, 1)

            def add_experts(j, rows_sem):
                dve.wait_ge(s_x2, j + 1)
                if j > PROJ_AFTER:
                    dve.wait_ge(s_pa, j + 1)
                dve.wait_ge(rows_sem, 16 * K1)
                for k in range(K1):
                    ins = nc.vector.scalar_tensor_tensor(out=X[:, j], in0=G[:, j, k], scalar=w4[:, j, k:k + 1], in1=X[:, j],
                                                         op0=ALU.mult, op1=ALU.add)
                    if k < K1 - 1:
                        step(ins)
                ins.then_inc(s_o, 1)

            def add_attention(j):
                dve.wait_ge(s_x2, j + 1)
                dve.wait_ge(s_fo, j + 1)
                if j <= PROJ_AFTER:
                    dve.wait_ge(s_o, j + 1)
                nc.vector.tensor_tensor(X[:, j], pb[4 + j % 4][:, 0:D], X[:, j], ALU.add).then_inc(s_pa, 1)

            EXPERTS_AFTER = (1, 2, 3, 5, 6, 7)
            for j in range(NT):
                add_shared(j)
                if j in EXPERTS_AFTER:
                    add_experts(EXPERTS_AFTER.index(j), s_g[EXPERTS_AFTER.index(j)])
            for j in range(NT):
                add_attention(j)
                if j == 3:
                    add_experts(6, s_g[6])
            add_experts(7, s_g[7])


_INS = ['L0_attn_x', 'L0_attn_Wq', 'L0_attn_bq', 'L0_attn_Wk', 'L0_attn_bk', 'L0_attn_Wv', 'L0_attn_bv', 'L0_attn_Wo',
        'L0_attn_bo', 'L0_ffn_W', 'L0_ffn_bias', 'L0_ffn_rw1', 'L0_ffn_rb1', 'L0_ffn_rw2', 'L0_ffn_rb2', 'L0_ffn_A',
        'L0_ffn_B', 'L0_ffn_gates', 'L1_attn_weight_qkv', 'L1_attn_weight_proj', 'L1_ffn_Wr', 'L1_ffn_Wg', 'L1_ffn_Wu',
        'L1_ffn_Wd', 'L1_ffn_Wsg', 'L1_ffn_Wsu', 'L1_ffn_Wsd', 'L1_ffn_Wse']


def kernel(**inputs):
    import numpy as np
    from concourse import bacc
    from concourse.bass_utils import run_bass_kernel_spmd

    nc = bacc.Bacc("TRN2", target_bir_lowering=False, num_devices=1, dynamic_dma_scratch_size=2048)
    arrays, aps = {}, {}
    for name in _INS:
        v = np.ascontiguousarray(inputs[name])
        arrays[f"in_{name}"] = v
        aps[name] = nc.dram_tensor(f"in_{name}", v.shape, mybir.dt.from_np(v.dtype), kind="ExternalInput").ap()
    out = nc.dram_tensor("out", (B, T, D), F32, kind="ExternalOutput").ap()
    program(nc, aps, out)
    r = run_bass_kernel_spmd(nc, [arrays], core_ids=[0])
    return r.results[0]["out"]
```
